# Optimizing a Trainium2 kernel written in Bass

```python
import numpy as np
import jax
import jax.numpy as jnp

def _softmax(x, axis=-1):
    return jax.nn.softmax(x, axis=axis)

def _gelu(x):
    return jax.nn.gelu(x, approximate=True)

def _silu(x):
    return jax.nn.silu(x)

def _sigmoid(x):
    return jax.nn.sigmoid(x)

def _layernorm(x, axis=-1, eps=1e-05):
    m = jnp.mean(x, axis=axis, keepdims=True)
    v = jnp.var(x, axis=axis, keepdims=True)
    return (x - m) / jnp.sqrt(v + eps)

def _scatter_add(tgt, idx, src, axis=0):
    return tgt.at[idx].add(src)

def _segment_sum(src, seg, n):
    return jax.ops.segment_sum(src, seg, n)
kernel_name = 'mk_sandwich_d1_jaxref_r8_d73b58'

def setup_inputs(seed: int=0):
    np.random.seed(seed)
    _w = jnp.asarray

    def _L0_attn_setup():
        import jax, jax.numpy as jnp
        import numpy as np
        from jax import lax
        EPS = 1e-05

        def layer_norm(x, w, b):
            mu = x.mean(-1, keepdims=True)
            var = ((x - mu) ** 2).mean(-1, keepdims=True)
            return (x - mu) * lax.rsqrt(var + EPS) * w + b

        def causal_dw_conv(x, w, b):
            B, L, D = x.shape
            K = w.shape[1]
            xt = jnp.pad(x.transpose(0, 2, 1), ((0, 0), (0, 0), (K - 1, 0)))
            y = lax.conv_general_dilated(xt, w[:, None, :], (1,), 'VALID', dimension_numbers=('NCH', 'OIH', 'NCH'), feature_group_count=D)
            return (y + b[:, None]).transpose(0, 2, 1)

        def mamba_block(x, ln_w, ln_b, W_in, b_in, conv_w, conv_b, W_xproj, W_dt, b_dt, A_log, Dp, W_out, b_out):
            res = x
            x = layer_norm(x, ln_w, ln_b)
            xz = x @ W_in + b_in
            Di = xz.shape[-1] // 2
            xp, z = (xz[..., :Di], xz[..., Di:])
            xp = jax.nn.silu(causal_dw_conv(xp, conv_w, conv_b))
            dbl = xp @ W_xproj
            N = A_log.shape[-1]
            R = dbl.shape[-1] - 2 * N
            dt, Bm, Cm = (dbl[..., :R], dbl[..., R:R + N], dbl[..., R + N:])
            delta = jax.nn.softplus(dt @ W_dt + b_dt)
            A = -jnp.exp(A_log)
            dA = jnp.exp(delta[..., None] * A)
            dBx = delta[..., None] * Bm[:, :, None, :] * xp[..., None]

            def step(h, inp):
                dAt, dBxt, ct = inp
                h = dAt * h + dBxt
                return (h, jnp.einsum('bdn,bn->bd', h, ct))
            h0 = jnp.zeros((x.shape[0], Di, N), x.dtype)
            _, ys = lax.scan(step, h0, (dA.transpose(1, 0, 2, 3), dBx.transpose(1, 0, 2, 3), Cm.transpose(1, 0, 2)))
            y = ys.transpose(1, 0, 2) + xp * Dp
            y = y * jax.nn.silu(z)
            return res + y @ W_out + b_out
        B, L, Dm = (2, 128, 128)
        Di, N, R, K = (256, 16, 64, 4)
        key = jax.random.key(seed)
        ks = jax.random.split(key, 12)
        s_in = 1.0 / np.sqrt(Dm)
        s_di = 1.0 / np.sqrt(Di)
        A = jnp.broadcast_to(jnp.arange(1, N + 1, dtype=jnp.float32), (Di, N))
        return {'x': jax.random.normal(ks[0], (B, L, Dm), jnp.float32), 'ln_w': jnp.ones((2, Dm), jnp.float32), 'ln_b': jnp.zeros((2, Dm), jnp.float32), 'W_in': jax.random.normal(ks[1], (2, Dm, 2 * Di), jnp.float32) * s_in, 'b_in': jnp.zeros((2, 2 * Di), jnp.float32), 'conv_w': jax.random.normal(ks[2], (2, Di, K), jnp.float32) * 0.5, 'conv_b': jnp.zeros((2, Di), jnp.float32), 'W_xproj': jax.random.normal(ks[3], (2, Di, R + 2 * N), jnp.float32) * s_di, 'W_dt': jax.random.normal(ks[4], (2, R, Di), jnp.float32) * 0.02, 'b_dt': jnp.full((2, Di), -4.6, jnp.float32) + 0.1 * jax.random.normal(ks[5], (2, Di), jnp.float32), 'A_log': jnp.log(jnp.stack([A, A])), 'D': jnp.ones((2, Di), jnp.float32), 'W_out': jax.random.normal(ks[6], (2, Di, Dm), jnp.float32) * s_di, 'b_out': jnp.zeros((2, Dm), jnp.float32), 'Wg': jax.random.normal(ks[7], (2 * Dm, Dm), jnp.float32) / np.sqrt(2 * Dm), 'bg': jnp.zeros((Dm,), jnp.float32), 'Wv': jax.random.normal(ks[8], (2 * Dm, Dm), jnp.float32) / np.sqrt(2 * Dm), 'bv': jnp.zeros((Dm,), jnp.float32)}
    _L0_attn_in = _L0_attn_setup()

    def _L0_ffn_setup():
        import jax, jax.numpy as jnp
        import numpy as np
        D_MODEL = 128
        D_FF = 512
        N_EXPERTS = 8
        TOP_K = 2
        LN_EPS = 1e-06

        def _moe(x, router_w, w1, b1, w2, b2, gamma, beta):
            B, S, D = x.shape
            x_flat = x.reshape(-1, D)
            N = x_flat.shape[0]
            logits = x_flat @ router_w
            gate_vals, gate_idx = jax.lax.top_k(logits, TOP_K)
            gate_w = jax.nn.softmax(gate_vals, axis=-1)
            gates = jnp.zeros_like(logits).at[jnp.arange(N)[:, None], gate_idx].set(gate_w)
            h = jax.nn.gelu(jnp.einsum('nd,edf->enf', x_flat, w1) + b1[:, None, :], approximate=False)
            out = jnp.einsum('enf,efd->end', h, w2) + b2[:, None, :]
            res = x_flat[None, :, :] + out
            mu = jnp.mean(res, axis=-1, keepdims=True)
            var = jnp.mean(jnp.square(res - mu), axis=-1, keepdims=True)
            normed = (res - mu) * jax.lax.rsqrt(var + LN_EPS)
            expert_out = normed * gamma[:, None, :] + beta[:, None, :]
            y = jnp.einsum('end,ne->nd', expert_out, gates)
            return y.reshape(B, S, D)
        key = jax.random.key(seed)
        ks = jax.random.split(key, 8)
        x = jax.random.normal(ks[0], (2, 256, D_MODEL), dtype=jnp.float32)
        router_w = jax.random.normal(ks[1], (D_MODEL, N_EXPERTS), dtype=jnp.float32) * 0.02
        w1 = jax.random.normal(ks[2], (N_EXPERTS, D_MODEL, D_FF), dtype=jnp.float32) * 0.02
        b1 = jnp.zeros((N_EXPERTS, D_FF), dtype=jnp.float32)
        w2 = jax.random.normal(ks[3], (N_EXPERTS, D_FF, D_MODEL), dtype=jnp.float32) * 0.02
        b2 = jnp.zeros((N_EXPERTS, D_MODEL), dtype=jnp.float32)
        gamma = jnp.ones((N_EXPERTS, D_MODEL), dtype=jnp.float32)
        beta = jnp.zeros((N_EXPERTS, D_MODEL), dtype=jnp.float32)
        return {'x': x, 'router_w': router_w, 'w1': w1, 'b1': b1, 'w2': w2, 'b2': b2, 'gamma': gamma, 'beta': beta}
    _L0_ffn_in = _L0_ffn_setup()
    _d = {'L0_attn_x': _L0_attn_in['x'], 'L0_attn_ln_w': _L0_attn_in['ln_w'], 'L0_attn_ln_b': _L0_attn_in['ln_b'], 'L0_attn_W_in': _L0_attn_in['W_in'], 'L0_attn_b_in': _L0_attn_in['b_in'], 'L0_attn_conv_w': _L0_attn_in['conv_w'], 'L0_attn_conv_b': _L0_attn_in['conv_b'], 'L0_attn_W_xproj': _L0_attn_in['W_xproj'], 'L0_attn_W_dt': _L0_attn_in['W_dt'], 'L0_attn_b_dt': _L0_attn_in['b_dt'], 'L0_attn_A_log': _L0_attn_in['A_log'], 'L0_attn_D': _L0_attn_in['D'], 'L0_attn_W_out': _L0_attn_in['W_out'], 'L0_attn_b_out': _L0_attn_in['b_out'], 'L0_attn_Wg': _L0_attn_in['Wg'], 'L0_attn_bg': _L0_attn_in['bg'], 'L0_attn_Wv': _L0_attn_in['Wv'], 'L0_attn_bv': _L0_attn_in['bv'], 'L0_ffn_router_w': _L0_ffn_in['router_w'], 'L0_ffn_w1': _L0_ffn_in['w1'], 'L0_ffn_b1': _L0_ffn_in['b1'], 'L0_ffn_w2': _L0_ffn_in['w2'], 'L0_ffn_b2': _L0_ffn_in['b2'], 'L0_ffn_gamma': _L0_ffn_in['gamma'], 'L0_ffn_beta': _L0_ffn_in['beta']}
    _x0 = _d['L0_attn_x']
    _d['L0_attn_x'] = jax.random.normal(jax.random.fold_in(jax.random.key(seed), 1), (8, 1024, 128), dtype=_x0.dtype)
    del _x0
    return _d

def reference(L0_attn_x, L0_attn_ln_w, L0_attn_ln_b, L0_attn_W_in, L0_attn_b_in, L0_attn_conv_w, L0_attn_conv_b, L0_attn_W_xproj, L0_attn_W_dt, L0_attn_b_dt, L0_attn_A_log, L0_attn_D, L0_attn_W_out, L0_attn_b_out, L0_attn_Wg, L0_attn_bg, L0_attn_Wv, L0_attn_bv, L0_ffn_router_w, L0_ffn_w1, L0_ffn_b1, L0_ffn_w2, L0_ffn_b2, L0_ffn_gamma, L0_ffn_beta):

    def _L0_attn_ref(x, ln_w, ln_b, W_in, b_in, conv_w, conv_b, W_xproj, W_dt, b_dt, A_log, D, W_out, b_out, Wg, bg, Wv, bv):
        import jax, jax.numpy as jnp
        import numpy as np
        from jax import lax
        EPS = 1e-05

        def layer_norm(x, w, b):
            mu = x.mean(-1, keepdims=True)
            var = ((x - mu) ** 2).mean(-1, keepdims=True)
            return (x - mu) * lax.rsqrt(var + EPS) * w + b

        def causal_dw_conv(x, w, b):
            B, L, D = x.shape
            K = w.shape[1]
            xt = jnp.pad(x.transpose(0, 2, 1), ((0, 0), (0, 0), (K - 1, 0)))
            y = lax.conv_general_dilated(xt, w[:, None, :], (1,), 'VALID', dimension_numbers=('NCH', 'OIH', 'NCH'), feature_group_count=D)
            return (y + b[:, None]).transpose(0, 2, 1)

        def mamba_block(x, ln_w, ln_b, W_in, b_in, conv_w, conv_b, W_xproj, W_dt, b_dt, A_log, Dp, W_out, b_out):
            res = x
            x = layer_norm(x, ln_w, ln_b)
            xz = x @ W_in + b_in
            Di = xz.shape[-1] // 2
            xp, z = (xz[..., :Di], xz[..., Di:])
            xp = jax.nn.silu(causal_dw_conv(xp, conv_w, conv_b))
            dbl = xp @ W_xproj
            N = A_log.shape[-1]
            R = dbl.shape[-1] - 2 * N
            dt, Bm, Cm = (dbl[..., :R], dbl[..., R:R + N], dbl[..., R + N:])
            delta = jax.nn.softplus(dt @ W_dt + b_dt)
            A = -jnp.exp(A_log)
            dA = jnp.exp(delta[..., None] * A)
            dBx = delta[..., None] * Bm[:, :, None, :] * xp[..., None]

            def step(h, inp):
                dAt, dBxt, ct = inp
                h = dAt * h + dBxt
                return (h, jnp.einsum('bdn,bn->bd', h, ct))
            h0 = jnp.zeros((x.shape[0], Di, N), x.dtype)
            _, ys = lax.scan(step, h0, (dA.transpose(1, 0, 2, 3), dBx.transpose(1, 0, 2, 3), Cm.transpose(1, 0, 2)))
            y = ys.transpose(1, 0, 2) + xp * Dp
            y = y * jax.nn.silu(z)
            return res + y @ W_out + b_out
        fwd = mamba_block(x, ln_w[0], ln_b[0], W_in[0], b_in[0], conv_w[0], conv_b[0], W_xproj[0], W_dt[0], b_dt[0], A_log[0], D[0], W_out[0], b_out[0])
        bwd = mamba_block(x[:, ::-1], ln_w[1], ln_b[1], W_in[1], b_in[1], conv_w[1], conv_b[1], W_xproj[1], W_dt[1], b_dt[1], A_log[1], D[1], W_out[1], b_out[1])
        bwd = bwd[:, ::-1]
        comb = jnp.concatenate([fwd, bwd], -1)
        gate = jax.nn.sigmoid(comb @ Wg + bg)
        value = comb @ Wv + bv
        return (gate * value + (1.0 - gate) * fwd + (1.0 - gate) * bwd) / 2.0

    def _L0_ffn_ref(x, router_w, w1, b1, w2, b2, gamma, beta):
        import jax, jax.numpy as jnp
        import numpy as np
        D_MODEL = 128
        D_FF = 512
        N_EXPERTS = 8
        TOP_K = 2
        LN_EPS = 1e-06

        def _moe(x, router_w, w1, b1, w2, b2, gamma, beta):
            B, S, D = x.shape
            x_flat = x.reshape(-1, D)
            N = x_flat.shape[0]
            logits = x_flat @ router_w
            gate_vals, gate_idx = jax.lax.top_k(logits, TOP_K)
            gate_w = jax.nn.softmax(gate_vals, axis=-1)
            gates = jnp.zeros_like(logits).at[jnp.arange(N)[:, None], gate_idx].set(gate_w)
            h = jax.nn.gelu(jnp.einsum('nd,edf->enf', x_flat, w1) + b1[:, None, :], approximate=False)
            out = jnp.einsum('enf,efd->end', h, w2) + b2[:, None, :]
            res = x_flat[None, :, :] + out
            mu = jnp.mean(res, axis=-1, keepdims=True)
            var = jnp.mean(jnp.square(res - mu), axis=-1, keepdims=True)
            normed = (res - mu) * jax.lax.rsqrt(var + LN_EPS)
            expert_out = normed * gamma[:, None, :] + beta[:, None, :]
            y = jnp.einsum('end,ne->nd', expert_out, gates)
            return y.reshape(B, S, D)
        return _moe(x, router_w, w1, b1, w2, b2, gamma, beta)
    x = L0_attn_x
    x = x + _layernorm(_L0_attn_ref(_layernorm(x, axis=-1), L0_attn_ln_w, L0_attn_ln_b, L0_attn_W_in, L0_attn_b_in, L0_attn_conv_w, L0_attn_conv_b, L0_attn_W_xproj, L0_attn_W_dt, L0_attn_b_dt, L0_attn_A_log, L0_attn_D, L0_attn_W_out, L0_attn_b_out, L0_attn_Wg, L0_attn_bg, L0_attn_Wv, L0_attn_bv), axis=-1)
    x = x + _layernorm(_L0_ffn_ref(_layernorm(x, axis=-1), L0_ffn_router_w, L0_ffn_w1, L0_ffn_b1, L0_ffn_w2, L0_ffn_b2, L0_ffn_gamma, L0_ffn_beta), axis=-1)
    return x

_drawn_inputs = setup_inputs


def setup_inputs(seed=0):
    import zlib

    import numpy as np

    out = dict(_drawn_inputs(seed))
    spreads = {'L0_attn_ln_w': (1.0, 0.2),
     'L0_attn_ln_b': (0.0, 0.1),
     'L0_attn_b_in': (0.0, 0.1),
     'L0_attn_conv_b': (0.0, 0.357),
     'L0_attn_D': (1.0, 0.2),
     'L0_attn_b_out': (0.0, 0.1),
     'L0_attn_bg': (0.0, 0.389),
     'L0_attn_bv': (0.0, 0.347),
     'L0_ffn_b1': (0.0, 0.8),
     'L0_ffn_b2': (0.0, 0.328),
     'L0_ffn_gamma': (1.0, 0.2),
     'L0_ffn_beta': (0.0, 0.342)}
    factors = {'L0_attn_W_dt': 8.0,
     'L0_attn_b_dt': 64.0,
     'L0_attn_A_log': 3.312,
     'L0_ffn_w1': 4.309,
     'L0_ffn_w2': 3.921,
     'L0_attn_W_xproj': 8.0}
    for name, (base, spread) in spreads.items():
        noise = np.random.default_rng([zlib.crc32(name.encode()), seed]).standard_normal(out[name].shape)
        drawn = base * np.exp(spread * noise) if base else spread * noise
        out[name] = jnp.asarray(drawn.astype(out[name].dtype))
    for name, factor in factors.items():
        out[name] = (out[name] * factor).astype(out[name].dtype)
    return out
```

```python
from contextlib import ExitStack

import concourse.bass as bass
from concourse import mybir

F32 = mybir.dt.float32
F32R = mybir.dt.float32r
U32 = mybir.dt.uint32
ALU = mybir.AluOpType
ACT = mybir.ActivationFunctionType

P = 128
ROWS, STEPS, DM = 8, 1024, 128
DI, NS, RANK, TAPS = 256, 16, 64, 4
NH = DI // P
CH = 512
NCH = STEPS // CH
UNITS = 2 * NCH
CPG = P // NS
GPH = P // CPG
GROUPS = NH * GPH
SLOTS = UNITS * GROUPS
TILES = STEPS // P
PAD = TAPS - 1
HRING, XRING = 8, 4
LAG = 3
EPS_IN, EPS_OUT = 1e-5, 1e-6
NE, FF = 8, 512
FT = FF // P
TC = 512
NTC = ROWS * STEPS // TC
TT = TC // P


class Signal:

    def __init__(self, ctx, nc, name, per):
        self.sem, self.per = ctx.enter_context(nc.semaphore(name)), per

    def at(self, row, count):
        value = row * self.per + count
        return max(value, 0) if isinstance(value, int) else value


def unit_of(u):
    return (0, u) if u < NCH else (1, 2 * NCH - 1 - u)


def group_of(g):
    half, j = divmod(g, GPH)
    tile, r = j % 4, j // 4
    jj = 4 * tile + r
    return half, jj, jj % 8, 2 * half + jj // 8, tile, r


def directed(ap, direction):
    return ap if direction == 0 else ap[:, ::-1]


def build(nc, x, ln_w, ln_b, W_in, b_in, conv_w, conv_b, W_xproj, W_dt, b_dt, A_log, Dp, W_out,
          b_out, Wg, bg, Wv, bv, router_w, w1, b1, w2, b2, gamma, beta, out):
    ctx = ExitStack()
    with ctx:
        x3_dram = nc.dram_tensor("x3_scratch", (ROWS * STEPS, DM), F32, kind="Internal").ap()
        ident = ctx.enter_context(nc.sbuf_tensor("ident", [P, P], F32))
        cols = ctx.enter_context(nc.sbuf_tensor("cols", [P, 124], F32))
        mhalf = ctx.enter_context(nc.sbuf_tensor("mhalf", [P, 8], F32))
        with ExitStack() as phase:
            mamba(nc, phase, ident, cols, mhalf, x, ln_w, ln_b, W_in, b_in, conv_w, conv_b, W_xproj,
                  W_dt, b_dt, A_log, Dp, W_out, b_out, Wg, bg, Wv, bv, b1, x3_dram)
        with ExitStack() as phase:
            experts(nc, phase, ident, cols, mhalf, router_w, w1, w2, b2, gamma, beta, x3_dram, out)


STACK_DMAS = 4 * 16
LOADS = 21 * 16
PREP_DVE = 39

C_LNW, C_LNB, C_BIN, C_CONVB, C_BDT, C_D, C_BOUT, C_BG, C_BV, C_B1, C_A = \
    0, 2, 4, 12, 16, 20, 24, 26, 27, 28, 60


def mamba(nc, ctx, ident, cols, mhalf, x, ln_w, ln_b, W_in, b_in, conv_w, conv_b, W_xproj, W_dt,
          b_dt, A_log, Dp, W_out, b_out, Wg, bg, Wv, bv, b1, x3_dram):
    def sb(name, shape, dt=F32):
        return ctx.enter_context(nc.sbuf_tensor(name, shape, dt))

    def pb(name, shape):
        return ctx.enter_context(nc.psum_tensor(name, shape, F32))

    def sig(name, per):
        return Signal(ctx, nc, name, per)

    rows = sb("rows", [P, P])
    sel = sb("sel", [P, 8, P], F32R)
    red = sb("red", [P, 4, 32])
    negA = sb("negA", [P, 2 * GROUPS])
    taps = sb("taps", [P, 2, NH, TAPS])
    Wk = sb("Wk", [P, 2, TAPS, DI])
    Wz = sb("Wz", [P, 2, DI])
    bz = sb("bz", [P, 2 * 4])
    cbias = sb("cbias", [P, 4])
    edge = sb("edge", [P, 2, 3, NH])
    psum4 = sb("psum4", [P, 4, 4])
    Wdtx = sb("Wdtx", [P, 2, NH, RANK])
    Wbc = sb("Wbc", [P, 2, NH, 2, P])
    Wdt = sb("Wdt", [RANK, 2, DI])
    Wo = sb("Wo", [P, 2, NH, DM])
    Wgs = sb("Wgs", [P, 2, DM])
    Wvs = sb("Wvs", [P, 2, DM])
    halfD = sb("halfD", [P, 4])
    halfbg = sb("halfbg", [P, 1])
    ones = sb("ones", [P, 2])
    xt = sb("xt", [P, TILES, DM])
    x1n = sb("x1n", [P, STEPS])
    x1T = sb("x1T", [P, STEPS])
    x2T = sb("x2T", [P, STEPS + 2 * PAD])
    stA = sb("stA", [P, TILES, 6])
    mvA = sb("mvA", [P, TILES, 2])
    rsA = sb("rsA", [P, 4, TILES])
    th = sb("th", [P, NH, CH])
    xp2 = sb("xp2", [P, 2, NH, CH])
    sz2 = sb("sz2", [P, 2, NH, CH])
    Brep = sb("Brep", [P, 2, CH])
    Crep = sb("Crep", [P, 2, CH])
    dtT = sb("dtT", [RANK, CH])
    ex = sb("ex", [P, NH, CH])
    lg = sb("lg", [P, NH, CH])
    w1p = sb("w1p", [P, NH, CH])
    u2 = sb("u2", [P, NH, CH])
    dhi = sb("dhi", [P, NH, CH], F32R)
    dlo = sb("dlo", [P, NH, CH], F32R)
    uhi = sb("uhi", [P, NH, CH], F32R)
    ulo = sb("ulo", [P, NH, CH], F32R)
    stackD = sb("stackD", [P, 4, CH], F32R)
    stackU = sb("stackU", [P, 4, CH], F32R)
    yg = sb("yg", [P, NH, CH])
    fbT = sb("fbT", [P, 2, STEPS])
    dbx = sb("dbx", [P, XRING, CH])
    hs = sb("hs", [P, HRING, CH])
    carry = sb("carry", [P, 2 * GROUPS])
    sfb = sb("sfb", [P, CH])
    tg = sb("tg", [P, CH])
    a4 = sb("a4", [P, STEPS])
    x3 = sb("x3", [P, TILES, DM])
    stG = sb("stG", [P, TILES, 6])
    mvG = sb("mvG", [P, TILES, 2])
    rsG = sb("rsG", [P, 2, TILES])

    D = pb("D", [P, 2, CH])
    U = pb("U", [P, 2, CH])
    Y = pb("Y", [P, CH])
    PW = pb("PW", [P, NH, CH])
    M = pb("M", [P, CH])

    win_raw = hs[:, 0:2, :]
    taps_b = hs[:, 2:6, :].rearrange("p a b -> p (a b)").rearrange("p (d c k) -> p d c k", d=2, k=TAPS)
    wx_raw = hs[:, 6, 0:384].rearrange("p (d h n) -> p d h n", d=2, h=NH)
    sel_f = ex[:, :, :].rearrange("p h t -> p (h t)").rearrange("p (k m) -> p k m", k=8)

    loaded = sig("loaded", 0)
    made = {n: sig(n, 0) for n in ("ident_made", "masks_made", "cols_made", "bias_mm", "prep_dve",
                                   "rows_T", "zeros_made", "a_made", "half_made")}
    sp_ticks, pool_ticks, dve_ticks = (sig(n, 0) for n in ("sp_ticks", "pool_ticks", "dve_ticks"))
    x_loaded = sig("x_loaded", 16)
    xres_loaded = sig("xres_loaded", 16)
    x3_stored = sig("x3_stored", 16)
    dstack_loaded = [sig(f"dstack{h}_loaded", UNITS * STACK_DMAS) for h in range(NH)]
    ustack_loaded = [sig(f"ustack{h}_loaded", UNITS * STACK_DMAS) for h in range(NH)]
    statsA = sig("statsA", 2 * TILES)
    rstdA = sig("rstdA", 6)
    x1_ready = sig("x1_ready", TILES)
    x2_ready = sig("x2_ready", TILES)
    x1_turned = sig("x1_turned", 1)
    x2_turned = sig("x2_turned", 1)
    x1n_ready = sig("x1n_ready", 1)
    x2T_ready = sig("x2T_ready", 1)
    x1T_ready = sig("x1T_ready", 1)
    xp_mm = sig("xp_mm", UNITS * NH)
    conv_ready = sig("conv_ready", UNITS * NH)
    edge_done = sig("edge_done", 2)
    thx_ready = sig("thx_ready", UNITS)
    xp_ready = sig("xp_ready", UNITS)
    z_mm = sig("z_mm", UNITS)
    z_ready = sig("z_ready", UNITS * NH)
    thz_ready = sig("thz_ready", UNITS)
    sz_ready = sig("sz_ready", UNITS)
    dt_mm = sig("dt_mm", UNITS)
    dt_ready = sig("dt_ready", UNITS)
    b_mm = sig("b_mm", UNITS)
    b_ready = sig("b_ready", UNITS)
    c_mm = sig("c_mm", UNITS)
    c_ready = sig("c_ready", UNITS)
    dp_mm = sig("dp_mm", UNITS)
    abs_ready = sig("abs_ready", UNITS * NH)
    relu_ready = sig("relu_ready", UNITS * NH)
    exp_ready = sig("exp_ready", UNITS)
    ln_ready = sig("ln_ready", UNITS)
    onep_ready = sig("onep_ready", UNITS)
    back_ready = sig("back_ready", UNITS)
    resid_ready = sig("resid_ready", UNITS)
    sp_sum = sig("sp_sum", UNITS)
    delta_ready = sig("delta_ready", UNITS)
    delta_copied = sig("delta_copied", UNITS)
    dhi_ready = sig("dhi_ready", UNITS)
    dlo_ready = sig("dlo_ready", UNITS)
    u_ready = sig("u_ready", UNITS)
    uhi_ready = sig("uhi_ready", UNITS)
    ulo_ready = sig("ulo_ready", UNITS)
    drep_ready = sig("drep_ready", SLOTS)
    urep_ready = sig("urep_ready", SLOTS)
    da_ready = sig("da_ready", SLOTS)
    dbx_ready = sig("dbx_ready", SLOTS)
    h_ready = sig("h_ready", SLOTS)
    carry_saved = sig("carry_saved", 2 * GROUPS)
    hc_ready = sig("hc_ready", SLOTS)
    reduced = sig("reduced", SLOTS // 4)
    yd_ready = sig("yd_ready", UNITS * NH)
    yg_ready = sig("yg_ready", UNITS * NH)
    out_mm = sig("out_mm", UNITS)
    outb_ready = sig("outb_ready", UNITS)
    fb_ready = sig("fb_ready", UNITS)
    gate_mm = sig("gate_mm", NCH)
    value_mm = sig("value_mm", NCH)
    sfb_ready = sig("sfb_ready", NCH)
    tg_ready = sig("tg_ready", NCH)
    diff_ready = sig("diff_ready", NCH)
    gated_ready = sig("gated_ready", NCH)
    a4_ready = sig("a4_ready", NCH)
    a4_turned = sig("a4_turned", 1)
    statsG = sig("statsG", 2 * TILES)
    rstdG = sig("rstdG", 2)
    an_ready = sig("an_ready", TILES)
    x3_ready = sig("x3_ready", 1)

    x_rows = x.rearrange("r (t p) d -> r p t d", p=P)
    x3_rows = x3_dram.rearrange("(r t p) d -> r p t d", r=ROWS, p=P)

    def dram_row(view, b):
        return view[b] if isinstance(b, int) else view[bass.ds(b, 1), :, :, :].rearrange("o p t d -> (o p) t d")

    block = ctx.enter_context(nc.Block())

    @block.sync
    def _(sp):
        def load(dst, src):
            sp.dma_start(dst, src).then_inc(loaded.sem, 16)
            load.n += 16

        load.n = 0
        for at, t in ((C_LNW, ln_w), (C_LNB, ln_b), (C_BIN, b_in), (C_CONVB, conv_b), (C_BDT, b_dt),
                      (C_D, Dp), (C_BOUT, b_out), (C_B1, b1)):
            n = t.shape[0] * t.shape[1] // P
            load(rows[at:at + n, :], t.rearrange("a (b c) -> (a b) c", c=P))
        load(rows[C_BG:C_BG + 1, :], bg.rearrange("(a c) -> a c", a=1))
        load(rows[C_BV:C_BV + 1, :], bv.rearrange("(a c) -> a c", a=1))
        load(rows[C_A:C_A + 2 * GROUPS, :], A_log.rearrange("d (g c) n -> (d g) (c n)", c=CPG))
        load(win_raw, W_in.rearrange("d p c -> p d c"))
        load(taps[:, :, :, :], conv_w.rearrange("d (h p) k -> p d h k", p=P))
        load(hs[:, 2:6, :].rearrange("p a b -> p (a b)"),
             conv_w.rearrange("(o d) c k -> o (d c k)", o=1).to_broadcast([P, 2 * DI * TAPS]))
        for d in range(2):
            load(wx_raw[:, d], W_xproj[d].rearrange("(h p) n -> p h n", p=P))
            load(Wo[:, d], W_out[d].rearrange("(h p) n -> p h n", p=P))
        load(Wdt[:, :, :], W_dt.rearrange("d r c -> r d c"))
        load(Wgs[:, :, :], Wg.rearrange("(h p) n -> p h n", p=P))
        load(Wvs[:, :, :], Wv.rearrange("(h p) n -> p h n", p=P))
        assert load.n == LOADS

        def load_x(b):
            sp.wait_ge(x2_turned.sem, x2_turned.at(b, 0))
            sp.sem_inc(sp_ticks.sem, 1)
            sp.dma_start(xt[:, :, :], dram_row(x_rows, b)).then_inc(x_loaded.sem, 16)

        def stacks(b, u, half):
            sp.wait_ge(drep_ready.sem, drep_ready.at(b, GROUPS * (u - 1) + GPH * (half + 1)))
            sp.sem_inc(sp_ticks.sem, 1)
            sp.wait_ge(urep_ready.sem, urep_ready.at(b, GROUPS * (u - 1) + GPH * (half + 1)))
            sp.sem_inc(sp_ticks.sem, 1)
            for hi, lo, hi_ready, lo_ready, stack, signal in (
                    (dhi, dlo, dhi_ready, dlo_ready, stackD, dstack_loaded[half]),
                    (uhi, ulo, uhi_ready, ulo_ready, stackU, ustack_loaded[half])):
                sp.wait_ge(hi_ready.sem, hi_ready.at(b, u + 1))
                sp.sem_inc(sp_ticks.sem, 1)
                sp.wait_ge(lo_ready.sem, lo_ready.at(b, u + 1))
                sp.sem_inc(sp_ticks.sem, 1)
                for a in range(2):
                    for k, part in enumerate((hi, lo)):
                        sp.dma_start(stack[64 * k:64 * k + 64, 2 * half + a, :].bitcast(F32),
                                     part[64 * a:64 * a + 64, half, :].bitcast(F32)) \
                            .then_inc(signal.sem, 16)

        def row(b, next_row, last_end):
            for u in range(UNITS):
                stacks(b, u, 1)
                if u == 1 and next_row:
                    load_x(b + 1)
                if u == 1 and last_end:
                    sp.wait_ge(x3_ready.sem, x3_ready.at(b, 0))
                    sp.sem_inc(sp_ticks.sem, 1)
                    sp.dma_start(dram_row(x3_rows, b - 1), x3[:, :, :]).then_inc(x3_stored.sem, 16)
                if u == 2:
                    sp.wait_ge(x3_stored.sem, x3_stored.at(b, 0))
                    sp.sem_inc(sp_ticks.sem, 1)
                    sp.dma_start(x3[:, :, :], dram_row(x_rows, b)).then_inc(xres_loaded.sem, 16)
                if u < UNITS - 1:
                    stacks(b, u + 1, 0)
                elif next_row:
                    stacks(b + 1, 0, 0)

        load_x(0)
        stacks(0, 0, 0)
        row(0, True, False)
        with nc.sync.Fori(1, ROWS - 1) as b:
            row(b, True, True)
        row(ROWS - 1, False, True)
        sp.wait_ge(x3_ready.sem, x3_ready.at(ROWS, 0))
        sp.sem_inc(sp_ticks.sem, 1)
        sp.dma_start(dram_row(x3_rows, ROWS - 1), x3[:, :, :]).then_inc(x3_stored.sem, 16)
        sp.wait_ge(x3_stored.sem, x3_stored.at(ROWS, 0))
        sp.sem_inc(sp_ticks.sem, 1)

    @block.gpsimd
    def _(pool):
        nc.gpsimd.memset(ident[:, :], 0.0).then_inc(made["zeros_made"].sem, 1)
        nc.gpsimd.memset(sel_f, 0.0).then_inc(made["zeros_made"].sem, 1)
        nc.gpsimd.memset(red[:, :, :], 1.0).then_inc(made["zeros_made"].sem, 1)
        nc.gpsimd.memset(mhalf[:, :], -0.5).then_inc(made["zeros_made"].sem, 1)
        nc.gpsimd.memset(x2T[:, 0:PAD], 0.0).then_inc(made["zeros_made"].sem, 1)
        nc.gpsimd.memset(x2T[:, PAD + STEPS:], 0.0).then_inc(made["zeros_made"].sem, 1)
        pool.wait_ge(made["zeros_made"].sem, 6)
        nc.gpsimd.affine_select(out=ident[:, :], in_=ident[:, :], compare_op=ALU.not_equal, fill=1.0,
                                base=0, pattern=[[-1, P]], channel_multiplier=1) \
            .then_inc(made["ident_made"].sem, 1)
        s4 = sel_f.rearrange("p k (d n) -> p k d n", n=NS)
        for i, base in enumerate((0, -64)):
            nc.gpsimd.affine_select(out=s4, in_=s4, compare_op=ALU.not_equal, fill=1.0, base=base,
                                    pattern=[[-CPG, 8], [-1, CPG], [0, NS]], channel_multiplier=1) \
                .then_inc(made["masks_made"].sem, 1)
            pool.wait_ge(made["masks_made"].sem, i + 1)
        nc.gpsimd.affine_select(out=red[:, :, :], in_=red[:, :, :], compare_op=ALU.is_ge, fill=0.0,
                                base=0, pattern=[[P, 4], [-NS, 32]], channel_multiplier=1) \
            .then_inc(made["masks_made"].sem, 1)
        pool.wait_ge(made["masks_made"].sem, 3)
        nc.gpsimd.affine_select(out=red[:, :, :], in_=red[:, :, :], compare_op=ALU.is_ge, fill=0.0,
                                base=NS - 1, pattern=[[-P, 4], [NS, 32]], channel_multiplier=-1) \
            .then_inc(made["masks_made"].sem, 1)
        pool.wait_ge(made["masks_made"].sem, 4)

        def rstds_in(b):
            pool.wait_ge(statsA.sem, statsA.at(b, 2 * TILES))
            pool.sem_inc(pool_ticks.sem, 1)
            var, ve, r1, v2, r2 = mvA[:, :, 1], rsA[:, 0, :], rsA[:, 1, :], rsA[:, 2, :], rsA[:, 3, :]
            nc.gpsimd.tensor_scalar(ve, var, 1.0, EPS_IN, ALU.mult, ALU.add).then_inc(rstdA.sem, 1)
            pool.wait_ge(rstdA.sem, rstdA.at(b, 1))
            nc.gpsimd.tensor_tensor(r1, ve, mhalf[:, :], ALU.pow).then_inc(rstdA.sem, 1)
            pool.wait_ge(rstdA.sem, rstdA.at(b, 2))
            nc.gpsimd.tensor_tensor(v2, r1, r1, ALU.mult).then_inc(rstdA.sem, 1)
            pool.wait_ge(rstdA.sem, rstdA.at(b, 3))
            nc.gpsimd.tensor_tensor(v2, v2, var, ALU.mult).then_inc(rstdA.sem, 1)
            pool.wait_ge(rstdA.sem, rstdA.at(b, 4))
            pool.sem_inc(pool_ticks.sem, 1)
            nc.gpsimd.tensor_scalar(v2, v2, 1.0, EPS_IN, ALU.mult, ALU.add).then_inc(rstdA.sem, 1)
            pool.wait_ge(rstdA.sem, rstdA.at(b, 5))
            nc.gpsimd.tensor_tensor(r2, v2, mhalf[:, :], ALU.pow).then_inc(rstdA.sem, 1)

        def softplus_residue(b, u):
            pool.wait_ge(exp_ready.sem, exp_ready.at(b, u + 1))
            pool.wait_ge(back_ready.sem, back_ready.at(b, u + 1))
            nc.gpsimd.tensor_tensor(w1p[:, :, :], ex[:, :, :], w1p[:, :, :], ALU.subtract) \
                .then_inc(resid_ready.sem, 1)

        def make_u(b, u):
            pool.wait_ge(delta_copied.sem, delta_copied.at(b, u + 1))
            pool.wait_ge(xp_ready.sem, xp_ready.at(b, u + 1))
            pool.wait_ge(ulo_ready.sem, ulo_ready.at(b, u))
            nc.gpsimd.tensor_tensor(u2[:, :, :], ex[:, :, :], xp2[:, u % 2], ALU.mult) \
                .then_inc(u_ready.sem, 1)

        def low_u(b, u):
            pool.wait_ge(uhi_ready.sem, uhi_ready.at(b, u + 1))
            for half in range(NH):
                pool.wait_ge(ustack_loaded[half].sem, ustack_loaded[half].at(b, STACK_DMAS * u))
            nc.gpsimd.tensor_tensor(ulo[:, :, :], u2[:, :, :], uhi[:, :, :].bitcast(F32), ALU.subtract) \
                .then_inc(ulo_ready.sem, 1)

        def group(b, s):
            u, g = divmod(s, GROUPS)
            direction, _ = unit_of(u)
            h = hs[:, s % HRING, :]
            pool.wait_ge(h_ready.sem, h_ready.at(b, s + 1))
            pool.sem_inc(pool_ticks.sem, 1)
            if u % 2 == 0:
                last = CH - 1 if direction == 0 else 0
                at = direction * GROUPS + g
                nc.gpsimd.tensor_copy(carry[:, at:at + 1], h[:, last:last + 1]).then_inc(carry_saved.sem, 1)
                pool.wait_ge(carry_saved.sem, carry_saved.at(b, at + 1))
            if g == 0:
                pool.wait_ge(c_ready.sem, c_ready.at(b, u + 1))
            nc.gpsimd.tensor_tensor(h, h, Crep[:, u % 2, :], ALU.mult).then_inc(hc_ready.sem, 1)

        def sum_directions(b, c):
            pool.wait_ge(fb_ready.sem, fb_ready.at(b, UNITS))
            pool.wait_ge(a4_ready.sem, a4_ready.at(b, c))
            cut = slice(CH * c, CH * c + CH)
            nc.gpsimd.tensor_tensor(sfb[:, :], fbT[:, 0, cut], fbT[:, 1, cut], ALU.add) \
                .then_inc(sfb_ready.sem, 1)

        def rstds_gated(b):
            pool.wait_ge(statsG.sem, statsG.at(b, 2 * TILES))
            pool.sem_inc(pool_ticks.sem, 1)
            nc.gpsimd.tensor_scalar(rsG[:, 0, :], mvG[:, :, 1], 1.0, 16 * EPS_IN, ALU.mult, ALU.add) \
                .then_inc(rstdG.sem, 1)
            pool.wait_ge(rstdG.sem, rstdG.at(b, 1))
            nc.gpsimd.tensor_tensor(rsG[:, 1, :], rsG[:, 0, :], mhalf[:, :], ALU.pow) \
                .then_inc(rstdG.sem, 1)

        def row(b, next_row, last_end):
            for s in range(SLOTS):
                u, g = divmod(s, GROUPS)
                group(b, s)
                nb, nu = (b, u + 1) if u < UNITS - 1 else (b + 1, 0)
                if u < UNITS - 1 or next_row:
                    if g == 15:
                        softplus_residue(nb, nu)
                    if g == 19:
                        make_u(nb, nu)
                    if g == 21:
                        low_u(nb, nu)
                if u == 0 and last_end:
                    if g in (20, 24):
                        sum_directions(b - 1, (g - 20) // 4)
                    if g == 30:
                        rstds_gated(b - 1)
                if u == 2 and next_row and g == 14:
                    rstds_in(b + 1)

        rstds_in(0)
        softplus_residue(0, 0)
        make_u(0, 0)
        low_u(0, 0)
        row(0, True, False)
        with nc.gpsimd.Fori(1, ROWS - 1) as b:
            row(b, True, True)
        row(ROWS - 1, False, True)
        for c in range(NCH):
            sum_directions(ROWS - 1, c)
        rstds_gated(ROWS - 1)

    @block.scalar
    def _(act):
        act.wait_ge(made["rows_T"].sem, 1)
        nc.scalar.activation(cols[:, :], M[:, 0:124], ACT.Copy).then_inc(made["cols_made"].sem, 1)
        act.wait_ge(made["cols_made"].sem, 1)
        nc.scalar.activation(negA[:, :], cols[:, C_A:C_A + 2 * GROUPS], ACT.Exp).then_inc(made["a_made"].sem, 1)
        act.wait_ge(made["a_made"].sem, 1)
        nc.scalar.mul(negA[:, :], negA[:, :], -1.0).then_inc(made["a_made"].sem, 1)
        act.wait_ge(made["a_made"].sem, 2)
        act.wait_ge(loaded.sem, LOADS)
        for i, (dst, src, f) in enumerate((
                (halfD[:, :], cols[:, C_D:C_D + 4], 0.5),
                (halfbg[:, :], cols[:, C_BG:C_BG + 1], 0.5),
                (Wo[:, :, :, :], Wo[:, :, :, :], 0.5),
                (Wdtx[:, :, :, :], wx_raw[:, :, :, 0:RANK], 0.5))):
            nc.scalar.mul(dst, src, f).then_inc(made["half_made"].sem, 1)
        for d in range(2):
            for h in range(NH):
                for k, f in ((0, 0.25), (1, 0.5)):
                    src = wx_raw[:, d, h, RANK + NS * k:RANK + NS * k + NS]
                    src = src.rearrange("p (o n) -> p o n", o=1).to_broadcast([P, CPG, NS])
                    nc.scalar.mul(Wbc[:, d, h, k, :].rearrange("p (r n) -> p r n", n=NS), src, f) \
                        .then_inc(made["half_made"].sem, 1)

        def evacuate_x1(b):
            act.wait_ge(x1_turned.sem, x1_turned.at(b, 1))
            act.wait_ge(x1T_ready.sem, x1T_ready.at(b, 0))
            nc.scalar.activation(x1n[:, :], PW[:, :, :].rearrange("p a t -> p (a t)"), ACT.Copy) \
                .then_inc(x1n_ready.sem, 1)

        def evacuate_x2(b):
            act.wait_ge(x2_turned.sem, x2_turned.at(b, 1))
            act.wait_ge(z_mm.sem, z_mm.at(b, 0))
            nc.scalar.activation(x2T[:, PAD:PAD + STEPS], PW[:, :, :].rearrange("p a t -> p (a t)"),
                                 ACT.Copy).then_inc(x2T_ready.sem, 1)

        def take_x1(b):
            act.wait_ge(x1n_ready.sem, x1n_ready.at(b, 1))
            act.wait_ge(fb_ready.sem, fb_ready.at(b, 0))
            nc.scalar.activation(x1T[:, :], x1n[:, :], ACT.Copy).then_inc(x1T_ready.sem, 1)

        def conv(b, u, half):
            d, _ = unit_of(u)
            act.wait_ge(xp_mm.sem, xp_mm.at(b, NH * u + half + 1))
            nc.scalar.activation(PW[:, half, :], PW[:, half, :], ACT.Identity,
                                 bias=cbias[:, 2 * d + half:2 * d + half + 1]).then_inc(conv_ready.sem, 1)

        def tanh_x(b, u):
            act.wait_ge(conv_ready.sem, conv_ready.at(b, NH * (u + 1)))
            if u % 2 == 0:
                act.wait_ge(edge_done.sem, edge_done.at(b, u // 2 + 1))
            act.wait_ge(sz_ready.sem, sz_ready.at(b, u))
            nc.scalar.activation(th[:, :, :], PW[:, :, :], ACT.Tanh, scale=0.5).then_inc(thx_ready.sem, 1)

        def gate_z(b, u, half):
            d, _ = unit_of(u)
            act.wait_ge(z_mm.sem, z_mm.at(b, u + 1))
            at = d * 4 + 2 + half
            nc.scalar.activation(PW[:, half, :], PW[:, half, :], ACT.Identity, bias=bz[:, at:at + 1]) \
                .then_inc(z_ready.sem, 1)

        def tanh_z(b, u):
            act.wait_ge(z_ready.sem, z_ready.at(b, NH * (u + 1)))
            act.wait_ge(xp_ready.sem, xp_ready.at(b, u + 1))
            nc.scalar.activation(th[:, :, :], PW[:, :, :], ACT.Tanh, scale=0.5).then_inc(thz_ready.sem, 1)

        def take_dt(b, u):
            act.wait_ge(dt_mm.sem, dt_mm.at(b, u + 1))
            act.wait_ge(dp_mm.sem, dp_mm.at(b, u))
            nc.scalar.activation(dtT[:, :], M[0:RANK, :], ACT.Copy).then_inc(dt_ready.sem, 1)

        def take_b(b, u):
            act.wait_ge(b_mm.sem, b_mm.at(b, u + 1))
            act.wait_ge(dbx_ready.sem, dbx_ready.at(b, GROUPS * (u - 1)))
            nc.scalar.activation(Brep[:, u % 2, :], M[:, :], ACT.Copy).then_inc(b_ready.sem, 1)

        def take_c(b, u):
            act.wait_ge(c_mm.sem, c_mm.at(b, u + 1))
            act.wait_ge(hc_ready.sem, hc_ready.at(b, GROUPS * (u - 1)))
            nc.scalar.activation(Crep[:, u % 2, :], M[:, :], ACT.Copy).then_inc(c_ready.sem, 1)

        def absolute(b, u, half):
            d, _ = unit_of(u)
            bias = cols[:, C_BDT + 2 * d + half:C_BDT + 2 * d + half + 1]
            act.wait_ge(dp_mm.sem, dp_mm.at(b, u + 1))
            act.wait_ge(u_ready.sem, u_ready.at(b, u))
            nc.scalar.activation(ex[:, half, :], PW[:, half, :], ACT.Abs, bias=bias).then_inc(abs_ready.sem, 1)
            nc.scalar.activation(PW[:, half, :], PW[:, half, :], ACT.Relu, bias=bias).then_inc(relu_ready.sem, 1)

        def softplus_exp(b, u):
            act.wait_ge(abs_ready.sem, abs_ready.at(b, NH * (u + 1)))
            nc.scalar.activation(ex[:, :, :], ex[:, :, :], ACT.Exp, scale=-1.0).then_inc(exp_ready.sem, 1)
            act.wait_ge(exp_ready.sem, exp_ready.at(b, u + 1))
            act.wait_ge(delta_ready.sem, delta_ready.at(b, u))
            nc.scalar.activation(w1p[:, :, :], ex[:, :, :], ACT.Identity, bias=ones[:, 0:1]).then_inc(onep_ready.sem, 1)
            act.wait_ge(onep_ready.sem, onep_ready.at(b, u + 1))
            nc.scalar.activation(w1p[:, :, :], w1p[:, :, :], ACT.Identity, bias=ones[:, 1:2]).then_inc(back_ready.sem, 1)

        def softplus_ln(b, u):
            act.wait_ge(sp_sum.sem, sp_sum.at(b, u))
            nc.scalar.activation(lg[:, :, :], ex[:, :, :], ACT.Ln, bias=ones[:, 0:1]).then_inc(ln_ready.sem, 1)

        def split_delta(b, u):
            act.wait_ge(delta_ready.sem, delta_ready.at(b, u + 1))
            act.wait_ge(resid_ready.sem, resid_ready.at(b, u + 1))
            nc.scalar.activation(ex[:, :, :], PW[:, :, :], ACT.Copy).then_inc(delta_copied.sem, 1)
            for half in range(NH):
                act.wait_ge(dstack_loaded[half].sem, dstack_loaded[half].at(b, STACK_DMAS * u))
            nc.scalar.activation(dhi[:, :, :], PW[:, :, :], ACT.Copy).then_inc(dhi_ready.sem, 1)

        def split_u(b, u):
            act.wait_ge(u_ready.sem, u_ready.at(b, u + 1))
            for half in range(NH):
                act.wait_ge(ustack_loaded[half].sem, ustack_loaded[half].at(b, STACK_DMAS * u))
            nc.scalar.activation(uhi[:, :, :], u2[:, :, :], ACT.Copy).then_inc(uhi_ready.sem, 1)

        def decay(b, s):
            u, g = divmod(s, GROUPS)
            d, _ = unit_of(u)
            half, jj, *_ = group_of(g)
            at = d * GROUPS + half * GPH + jj
            act.wait_ge(drep_ready.sem, drep_ready.at(b, s + 1))
            nc.scalar.activation(D[:, s % 2, :], D[:, s % 2, :], ACT.Exp, scale=negA[:, at:at + 1]) \
                .then_inc(da_ready.sem, 1)

        def add_out_bias(b, u):
            d, _ = unit_of(u)
            act.wait_ge(out_mm.sem, out_mm.at(b, u + 1))
            nc.scalar.activation(M[:, :], M[:, :], ACT.Identity, bias=cols[:, C_BOUT + d:C_BOUT + d + 1]) \
                .then_inc(outb_ready.sem, 1)

        def gate(b, c):
            act.wait_ge(gate_mm.sem, gate_mm.at(b, c + 1))
            act.wait_ge(gated_ready.sem, gated_ready.at(b, c))
            nc.scalar.activation(tg[:, :], PW[:, 0, :], ACT.Tanh, bias=halfbg[:, 0:1], scale=0.5) \
                .then_inc(tg_ready.sem, 1)

        def row(b, next_row, last_end):
            for s in range(SLOTS):
                u, g = divmod(s, GROUPS)
                if s < SLOTS - 1:
                    decay(b, s + 1)
                elif next_row:
                    decay(b + 1, 0)
                nb, nu = (b, u + 1) if u < UNITS - 1 else (b + 1, 0)
                if u < UNITS - 1 or next_row:
                    if g == 1:
                        conv(nb, nu, 0)
                    if g == 3:
                        conv(nb, nu, 1)
                    if g == 4:
                        tanh_x(nb, nu)
                    if g == 6:
                        gate_z(nb, nu, 0)
                        gate_z(nb, nu, 1)
                    if g == 7:
                        tanh_z(nb, nu)
                        take_dt(nb, nu)
                    if g == 8:
                        take_b(nb, nu)
                    if g == 9:
                        take_c(nb, nu)
                    if g == 10:
                        absolute(nb, nu, 0)
                    if g == 11:
                        absolute(nb, nu, 1)
                    if g == 12:
                        softplus_exp(nb, nu)
                    if g == 14:
                        softplus_ln(nb, nu)
                    if g == 18:
                        split_delta(nb, nu)
                    if g == 20:
                        split_u(nb, nu)
                if g == 16 and (u > 0 or last_end):
                    add_out_bias(*((b, u - 1) if u > 0 else (b - 1, UNITS - 1)))
                if u == 0:
                    if g == 18:
                        take_x1(b)
                    if last_end and g in (22, 26):
                        gate(b - 1, (g - 22) // 4)
                if u == 2 and next_row:
                    if g == 26:
                        evacuate_x1(b + 1)
                    if g == 30:
                        evacuate_x2(b + 1)

        evacuate_x1(0)
        evacuate_x2(0)
        act.wait_ge(made["prep_dve"].sem, PREP_DVE)
        conv(0, 0, 0)
        conv(0, 0, 1)
        tanh_x(0, 0)
        gate_z(0, 0, 0)
        gate_z(0, 0, 1)
        tanh_z(0, 0)
        take_dt(0, 0)
        take_b(0, 0)
        take_c(0, 0)
        absolute(0, 0, 0)
        absolute(0, 0, 1)
        softplus_exp(0, 0)
        softplus_ln(0, 0)
        split_delta(0, 0)
        split_u(0, 0)
        decay(0, 0)
        row(0, True, False)
        with nc.scalar.Fori(1, ROWS - 1) as b:
            row(b, True, True)
        row(ROWS - 1, False, True)
        add_out_bias(ROWS - 1, UNITS - 1)
        for c in range(NCH):
            gate(ROWS - 1, c)

    @block.vector
    def _(dve):
        prep = made["prep_dve"].sem
        count = [0]

        def step(instruction):
            instruction.then_inc(prep, 1)
            count[0] += 1
            dve.wait_ge(prep, count[0])

        step(nc.vector.memset(ones[:, 0:1], 1.0))
        step(nc.vector.memset(ones[:, 1:2], -1.0))
        dve.wait_ge(made["masks_made"].sem, 4)
        step(nc.vector.tensor_copy(sel[:, :, :], sel_f))
        dve.wait_ge(made["cols_made"].sem, 1)
        dve.wait_ge(loaded.sem, LOADS)
        dve.wait_ge(made["bias_mm"].sem, 1)
        step(nc.vector.tensor_tensor(bz[:, :], M[:, 128:136], cols[:, C_BIN:C_BIN + 8], ALU.add))
        for d in range(2):
            for h in range(NH):
                at = 2 * d + h
                bias = bz[:, 4 * d + h:4 * d + h + 1]
                for k in range(TAPS):
                    tap = taps[:, d, h, k:k + 1]
                    if k == 0:
                        step(nc.vector.tensor_tensor(psum4[:, 0, at:at + 1], tap, bias, ALU.mult))
                    else:
                        step(nc.vector.scalar_tensor_tensor(psum4[:, k, at:at + 1], tap, bias,
                                                            psum4[:, k - 1, at:at + 1], ALU.mult, ALU.add))
        step(nc.vector.tensor_tensor(cbias[:, :], psum4[:, 3, :], cols[:, C_CONVB:C_CONVB + 4], ALU.add))
        for t in range(3):
            step(nc.vector.tensor_scalar(edge[:, 0, t, :], psum4[:, 2 - t, 0:2], -1.0, None, ALU.mult))
            step(nc.vector.tensor_scalar(edge[:, 1, t, :], psum4[:, t, 2:4], -1.0, None, ALU.mult))
        for d in range(2):
            w = cols[:, C_LNW + d:C_LNW + d + 1]
            step(nc.vector.tensor_scalar(Wz[:, d, :], win_raw[:, d, DI:], w, None, ALU.mult))
            step(nc.vector.tensor_scalar(win_raw[:, d, :], win_raw[:, d, :], w, None, ALU.mult))
            for k in range(TAPS):
                step(nc.vector.tensor_tensor(Wk[:, d, k, :], win_raw[:, d, 0:DI], taps_b[:, d, :, k], ALU.mult))
        assert count[0] == PREP_DVE

        def stats_in(b):
            dve.wait_ge(x_loaded.sem, x_loaded.at(b, 16))
            dve.wait_ge(rstdA.sem, rstdA.at(b, 0))
            dve.wait_ge(x2_ready.sem, x2_ready.at(b, 0))
            for t in range(TILES):
                nc.vector.bn_stats(stA[:, t, :], xt[:, t, :]).then_inc(statsA.sem, 1)
            dve.wait_ge(statsA.sem, statsA.at(b, TILES))
            dve.sem_inc(dve_ticks.sem, 1)
            for t in range(TILES):
                nc.vector.bn_aggr(mvA[:, t, :], stA[:, t, :]).then_inc(statsA.sem, 1)

        def make_x1(b):
            dve.wait_ge(rstdA.sem, rstdA.at(b, 2))
            dve.wait_ge(statsA.sem, statsA.at(b, 2 * TILES))
            for t in range(TILES):
                nc.vector.tensor_scalar(xt[:, t, :], xt[:, t, :], mvA[:, t, 0:1], rsA[:, 1, t:t + 1],
                                        ALU.subtract, ALU.mult).then_inc(x1_ready.sem, 1)

        def make_x2(b):
            dve.wait_ge(rstdA.sem, rstdA.at(b, 6))
            dve.wait_ge(x1_turned.sem, x1_turned.at(b, 1))
            dve.wait_ge(x1_ready.sem, x1_ready.at(b, TILES))
            for t in range(TILES):
                nc.vector.tensor_scalar(xt[:, t, :], xt[:, t, :], rsA[:, 3, t:t + 1], None,
                                        ALU.mult).then_inc(x2_ready.sem, 1)

        def fix_edge(b, u):
            d, _ = unit_of(u)
            dve.wait_ge(conv_ready.sem, conv_ready.at(b, NH * (u + 1)))
            at = PW[:, :, 0:3] if d == 0 else PW[:, :, CH - 3:CH]
            nc.vector.tensor_tensor(at, at, edge[:, d, :, :].rearrange("p t h -> p h t"), ALU.add) \
                .then_inc(edge_done.sem, 1)

        def silu_x(b, u):
            dve.wait_ge(thx_ready.sem, thx_ready.at(b, u + 1))
            dve.wait_ge(c_mm.sem, c_mm.at(b, u - 1))
            dve.wait_ge(u_ready.sem, u_ready.at(b, u - 1))
            dve.wait_ge(yd_ready.sem, yd_ready.at(b, NH * (u - 1)))
            nc.vector.scalar_tensor_tensor(xp2[:, u % 2], th[:, :, :], 1.0, PW[:, :, :], ALU.add, ALU.mult) \
                .then_inc(xp_ready.sem, 1)

        def silu_z(b, u):
            dve.wait_ge(thz_ready.sem, thz_ready.at(b, u + 1))
            dve.wait_ge(yg_ready.sem, yg_ready.at(b, NH * (u - 1)))
            nc.vector.scalar_tensor_tensor(sz2[:, u % 2], th[:, :, :], 1.0, PW[:, :, :], ALU.add, ALU.mult) \
                .then_inc(sz_ready.sem, 1)

        def softplus_sum(b, u):
            dve.wait_ge(ln_ready.sem, ln_ready.at(b, u + 1))
            dve.wait_ge(relu_ready.sem, relu_ready.at(b, NH * (u + 1)))
            nc.vector.tensor_tensor(PW[:, :, :], PW[:, :, :], lg[:, :, :], ALU.add).then_inc(sp_sum.sem, 1)

        def make_delta(b, u):
            dve.wait_ge(sp_sum.sem, sp_sum.at(b, u + 1))
            dve.wait_ge(resid_ready.sem, resid_ready.at(b, u + 1))
            nc.vector.tensor_tensor(PW[:, :, :], PW[:, :, :], w1p[:, :, :], ALU.add).then_inc(delta_ready.sem, 1)

        def low_delta(b, u):
            dve.wait_ge(dhi_ready.sem, dhi_ready.at(b, u + 1))
            for half in range(NH):
                dve.wait_ge(dstack_loaded[half].sem, dstack_loaded[half].at(b, STACK_DMAS * u))
            nc.vector.tensor_tensor(dlo[:, :, :], PW[:, :, :], dhi[:, :, :].bitcast(F32), ALU.subtract) \
                .then_inc(dlo_ready.sem, 1)

        def scan_input(b, s):
            u, g = divmod(s, GROUPS)
            dve.wait_ge(urep_ready.sem, urep_ready.at(b, s + 1))
            dve.wait_ge(h_ready.sem, h_ready.at(b, s + 1 - XRING))
            if g == 0:
                dve.wait_ge(b_ready.sem, b_ready.at(b, u + 1))
            nc.vector.tensor_tensor(dbx[:, s % XRING, :], U[:, s % 2, :], Brep[:, u % 2, :], ALU.mult) \
                .then_inc(dbx_ready.sem, 1)

        def scan(b, s):
            u, g = divmod(s, GROUPS)
            d, _ = unit_of(u)
            initial = 0.0
            if u % 2 == 1:
                at = d * GROUPS + g
                dve.wait_ge(carry_saved.sem, carry_saved.at(b, at + 1))
                initial = carry[:, at:at + 1]
            dve.wait_ge(dbx_ready.sem, dbx_ready.at(b, s + 1))
            dve.wait_ge(da_ready.sem, da_ready.at(b, s + 1))
            dve.wait_ge(reduced.sem, reduced.at(b, (s - HRING) // 4 + 1))
            nc.vector.tensor_tensor_scan(directed(hs[:, s % HRING, :], d), directed(D[:, s % 2, :], d),
                                         directed(dbx[:, s % XRING, :], d), initial, ALU.mult, ALU.add) \
                .then_inc(h_ready.sem, 1)

        def gate_y(b, u, half):
            d, _ = unit_of(u)
            k = NH * u + half + 1
            dve.wait_ge(reduced.sem, reduced.at(b, 4 * k))
            dve.wait_ge(out_mm.sem, out_mm.at(b, u))
            nc.vector.scalar_tensor_tensor(Y[:, :], xp2[:, u % 2, half, :], halfD[:, 2 * d + half:2 * d + half + 1],
                                           Y[:, :], ALU.mult, ALU.add).then_inc(yd_ready.sem, 1)
            dve.wait_ge(yd_ready.sem, yd_ready.at(b, k))
            nc.vector.tensor_tensor(yg[:, half, :], Y[:, :], sz2[:, u % 2, half, :], ALU.mult) \
                .then_inc(yg_ready.sem, 1)

        def add_x1(b, u):
            d, c = unit_of(u)
            dve.wait_ge(outb_ready.sem, outb_ready.at(b, u + 1))
            dve.wait_ge(x1T_ready.sem, x1T_ready.at(b, 1))
            dve.wait_ge(a4_ready.sem, a4_ready.at(b, 0))
            cut = slice(CH * c, CH * c + CH)
            nc.vector.tensor_tensor(fbT[:, d, cut], M[:, :], x1T[:, cut], ALU.add).then_inc(fb_ready.sem, 1)

        def gated_sum(b, c):
            V = PW[:, 1, :]
            dve.wait_ge(value_mm.sem, value_mm.at(b, c + 1))
            dve.wait_ge(sfb_ready.sem, sfb_ready.at(b, c + 1))
            nc.vector.scalar_tensor_tensor(V, V, cols[:, C_BV:C_BV + 1], sfb[:, :], ALU.add, ALU.subtract) \
                .then_inc(diff_ready.sem, 1)
            dve.wait_ge(diff_ready.sem, diff_ready.at(b, c + 1))
            dve.wait_ge(tg_ready.sem, tg_ready.at(b, c + 1))
            nc.vector.scalar_tensor_tensor(V, tg[:, :], 1.0, V, ALU.add, ALU.mult).then_inc(gated_ready.sem, 1)
            dve.wait_ge(gated_ready.sem, gated_ready.at(b, c + 1))
            dve.wait_ge(a4_turned.sem, a4_turned.at(b, 0))
            nc.vector.scalar_tensor_tensor(a4[:, CH * c:CH * c + CH], sfb[:, :], 2.0, V, ALU.mult, ALU.add) \
                .then_inc(a4_ready.sem, 1)

        def stats_gated(b):
            dve.wait_ge(a4_turned.sem, a4_turned.at(b, 1))
            dve.wait_ge(rstdG.sem, rstdG.at(b, 0))
            dve.wait_ge(an_ready.sem, an_ready.at(b, 0))
            V = PW[:, :, :].rearrange("p a (t d) -> p (a t) d", d=DM)
            for t in range(TILES):
                nc.vector.bn_stats(stG[:, t, :], V[:, t, :]).then_inc(statsG.sem, 1)
            dve.wait_ge(statsG.sem, statsG.at(b, TILES))
            dve.sem_inc(dve_ticks.sem, 1)
            for t in range(TILES):
                nc.vector.bn_aggr(mvG[:, t, :], stG[:, t, :]).then_inc(statsG.sem, 1)

        def make_x3(b):
            V = PW[:, :, :].rearrange("p a (t d) -> p (a t) d", d=DM)
            dve.wait_ge(rstdG.sem, rstdG.at(b, 2))
            dve.wait_ge(statsG.sem, statsG.at(b, 2 * TILES))
            for t in range(TILES):
                nc.vector.tensor_scalar(V[:, t, :], V[:, t, :], mvG[:, t, 0:1], rsG[:, 1, t:t + 1],
                                        ALU.subtract, ALU.mult).then_inc(an_ready.sem, 1)
            dve.wait_ge(an_ready.sem, an_ready.at(b, TILES))
            dve.wait_ge(xres_loaded.sem, xres_loaded.at(b, 16))
            nc.vector.tensor_tensor(x3[:, :, :], V, x3[:, :, :], ALU.add).then_inc(x3_ready.sem, 1)

        def row(b, next_row, last_end):
            for s in range(SLOTS):
                u, g = divmod(s, GROUPS)
                if s < SLOTS - 1:
                    scan_input(b, s + 1)
                elif next_row:
                    scan_input(b + 1, 0)
                scan(b, s)
                nb, nu = (b, u + 1) if u < UNITS - 1 else (b + 1, 0)
                if g == 4 and (u > 0 or last_end):
                    gate_y(*((b, u - 1) if u > 0 else (b - 1, UNITS - 1)), 1)
                if g == 20:
                    gate_y(b, u, 0)
                if u < UNITS - 1 or next_row:
                    if g == 3 and nu % 2 == 0:
                        fix_edge(nb, nu)
                    if g == 5:
                        silu_x(nb, nu)
                    if g == 7:
                        silu_z(nb, nu)
                    if g == 15:
                        softplus_sum(nb, nu)
                    if g == 17:
                        make_delta(nb, nu)
                    if g == 19:
                        low_delta(nb, nu)
                if g == 16 and (u > 0 or last_end):
                    add_x1(*((b, u - 1) if u > 0 else (b - 1, UNITS - 1)))
                if u == 0 and last_end:
                    if g in (22, 26):
                        gated_sum(b - 1, (g - 22) // 4)
                    if g == 29:
                        stats_gated(b - 1)
                    if g == 31:
                        make_x3(b - 1)
                if u == 2 and next_row:
                    if g == 13:
                        stats_in(b + 1)
                    if g == 21:
                        make_x1(b + 1)
                    if g == 27:
                        make_x2(b + 1)

        stats_in(0)
        make_x1(0)
        make_x2(0)
        fix_edge(0, 0)
        silu_x(0, 0)
        silu_z(0, 0)
        softplus_sum(0, 0)
        make_delta(0, 0)
        low_delta(0, 0)
        scan_input(0, 0)
        row(0, True, False)
        with nc.vector.Fori(1, ROWS - 1) as b:
            row(b, True, True)
        row(ROWS - 1, False, True)
        gate_y(ROWS - 1, UNITS - 1, 1)
        add_x1(ROWS - 1, UNITS - 1)
        for c in range(NCH):
            gated_sum(ROWS - 1, c)
        stats_gated(ROWS - 1)
        make_x3(ROWS - 1)

    @block.tensor
    def _(pe):
        pe.wait_ge(made["ident_made"].sem, 1)
        pe.wait_ge(loaded.sem, LOADS)
        nc.tensor.transpose(M[:, 0:124], rows[0:124, :], ident[0:124, 0:124]).then_inc(made["rows_T"].sem, 1)
        pe.wait_ge(made["cols_made"].sem, 1)
        for d in range(2):
            for m in range(4):
                last = nc.tensor.matmul(M[:, 128 + 4 * d + m:129 + 4 * d + m], win_raw[:, d, P * m:P * m + P],
                                        cols[:, C_LNB + d:C_LNB + d + 1], start=True, stop=True)
        last.then_inc(made["bias_mm"].sem, 1)

        def turn(src, dst_signal):
            for t in range(TILES):
                last = nc.tensor.transpose(PW[:, t // 4, P * (t % 4):P * (t % 4) + P], src[:, t, :], ident[:, :])
            last.then_inc(dst_signal.sem, 1)

        def wide_free(b, u):
            pe.wait_ge(dlo_ready.sem, dlo_ready.at(b, u + 1))
            pe.wait_ge(dhi_ready.sem, dhi_ready.at(b, u + 1))

        def turn_x1(b):
            wide_free(b, -1)
            pe.wait_ge(x1_ready.sem, x1_ready.at(b, TILES))
            turn(xt, x1_turned)

        def turn_x2(b):
            pe.wait_ge(x1n_ready.sem, x1n_ready.at(b, 1))
            pe.wait_ge(x2_ready.sem, x2_ready.at(b, TILES))
            turn(xt, x2_turned)

        def product_x(b, u, half):
            d, c = unit_of(u)
            if half == 0:
                pe.wait_ge(x2T_ready.sem, x2T_ready.at(b, 1))
                wide_free(b, u - 1)
                pe.wait_ge(x3_ready.sem, x3_ready.at(b, 0 if u >= 2 else -1))
            for k in range(TAPS):
                at = CH * c + k if d == 0 else CH * c + 2 * PAD - k
                last = nc.tensor.matmul(PW[:, half, :], Wk[:, d, k, P * half:P * half + P], x2T[:, at:at + CH],
                                        start=(k == 0), stop=(k == TAPS - 1))
            last.then_inc(xp_mm.sem, 1)

        def product_z(b, u):
            d, c = unit_of(u)
            pe.wait_ge(xp_ready.sem, xp_ready.at(b, u + 1))
            at = CH * c + PAD
            for half in range(NH):
                last = nc.tensor.matmul(PW[:, half, :], Wz[:, d, P * half:P * half + P], x2T[:, at:at + CH],
                                        start=True, stop=True)
            last.then_inc(z_mm.sem, 1)

        def from_x(out_ap, weights, b, u, signal):
            for half in range(NH):
                last = nc.tensor.matmul(out_ap, weights(half), xp2[:, u % 2, half, :],
                                        start=(half == 0), stop=(half == NH - 1))
            last.then_inc(signal.sem, 1)

        def product_dt(b, u, w):
            d, _ = unit_of(u)
            pe.wait_ge(xp_ready.sem, xp_ready.at(b, u + 1))
            pe.wait_ge(c_ready.sem, c_ready.at(b, u))
            pe.wait_ge(fb_ready.sem, fb_ready.at(*w))
            from_x(M[0:RANK, :], lambda h: Wdtx[:, d, h, :], b, u, dt_mm)

        def product_b(b, u):
            d, _ = unit_of(u)
            pe.wait_ge(dt_ready.sem, dt_ready.at(b, u + 1))
            from_x(M[:, :], lambda h: Wbc[:, d, h, 0, :], b, u, b_mm)

        def product_c(b, u):
            d, _ = unit_of(u)
            pe.wait_ge(b_ready.sem, b_ready.at(b, u + 1))
            from_x(M[:, :], lambda h: Wbc[:, d, h, 1, :], b, u, c_mm)

        def product_delta(b, u):
            d, _ = unit_of(u)
            pe.wait_ge(sz_ready.sem, sz_ready.at(b, u + 1))
            pe.wait_ge(dt_ready.sem, dt_ready.at(b, u + 1))
            for half in range(NH):
                last = nc.tensor.matmul(PW[:, half, :], Wdt[:, d, P * half:P * half + P], dtT[:, :],
                                        start=True, stop=True)
            last.then_inc(dp_mm.sem, 1)

        def replicate(b, s, ring, stack, loads, signal, read):
            u, g = divmod(s, GROUPS)
            _, _, k, q, _, _ = group_of(g)
            if g % GPH == 0:
                pe.wait_ge(loads[g // GPH].sem, loads[g // GPH].at(b, STACK_DMAS * (u + 1)))
            pe.wait_ge(read.sem, read.at(b, s - 1))
            nc.tensor.matmul(ring[:, s % 2, :], sel[:, k, :], stack[:, q, :], start=True, stop=True) \
                .then_inc(signal.sem, 1)

        def replicate_delta(b, s):
            replicate(b, s, D, stackD, dstack_loaded, drep_ready, h_ready)

        def replicate_u(b, s):
            replicate(b, s, U, stackU, ustack_loaded, urep_ready, dbx_ready)

        def reduce(b, m):
            for s in range(4 * m, 4 * m + 4):
                g = s % GROUPS
                _, _, _, _, tile, r = group_of(g)
                if s == 4 * m:
                    if m % 4 == 0:
                        pe.wait_ge(yg_ready.sem, yg_ready.at(b, m // 4))
                pe.wait_ge(hc_ready.sem, hc_ready.at(b, s + 1))
                last = nc.tensor.matmul(Y[32 * tile:32 * tile + 32, :], red[:, r, :], hs[:, s % HRING, :],
                                        start=(r == 0), stop=(r == 3))
            last.then_inc(reduced.sem, 1)

        def product_out(b, u, nc_ready):
            d, _ = unit_of(u)
            pe.wait_ge(yg_ready.sem, yg_ready.at(b, NH * (u + 1)))
            pe.wait_ge(fb_ready.sem, fb_ready.at(b, u))
            pe.wait_ge(c_ready.sem, c_ready.at(*nc_ready))
            for half in range(NH):
                last = nc.tensor.matmul(M[:, :], Wo[:, d, half, :], yg[:, half, :],
                                        start=(half == 0), stop=(half == NH - 1))
            last.then_inc(out_mm.sem, 1)

        def products_gated(b, c):
            pe.wait_ge(fb_ready.sem, fb_ready.at(b, UNITS))
            if c:
                pe.wait_ge(a4_ready.sem, a4_ready.at(b, c))
                pe.wait_ge(tg_ready.sem, tg_ready.at(b, c))
            cut = slice(CH * c, CH * c + CH)
            for k, (W, signal) in enumerate(((Wgs, gate_mm), (Wvs, value_mm))):
                for d in range(2):
                    last = nc.tensor.matmul(PW[:, k, :], W[:, d, :], fbT[:, d, cut], start=(d == 0), stop=(d == 1))
                last.then_inc(signal.sem, 1)

        def turn_a4(b):
            pe.wait_ge(a4_ready.sem, a4_ready.at(b, NCH))
            turn(a4[:, :].rearrange("p (t d) -> p t d", d=DM), a4_turned)

        def row(b, next_row, last_end):
            for s in range(SLOTS):
                u, g = divmod(s, GROUPS)
                if s + 1 < SLOTS:
                    replicate_delta(b, s + 1)
                elif next_row:
                    replicate_delta(b + 1, 0)
                if s + 2 < SLOTS:
                    replicate_u(b, s + 2)
                elif next_row:
                    replicate_u(b + 1, s + 2 - SLOTS)
                if (s - LAG) % 4 == 3:
                    if s - LAG >= 3:
                        reduce(b, (s - LAG) // 4)
                    elif last_end:
                        reduce(b - 1, SLOTS // 4 + (s - LAG) // 4)
                nb, nu = (b, u + 1) if u < UNITS - 1 else (b + 1, 0)
                prepares = u < UNITS - 1 or next_row
                if prepares:
                    if g == 0:
                        product_x(nb, nu, 0)
                    if g == 2:
                        product_x(nb, nu, 1)
                    if g == 5:
                        product_z(nb, nu)
                    if g == 7:
                        product_dt(nb, nu, (b, u - 1))
                    if g == 8:
                        product_b(nb, nu)
                    if g == 9:
                        product_c(nb, nu)
                    if g == 10:
                        product_delta(nb, nu)
                if g == 15 and (u > 0 or last_end):
                    product_out(*((b, u - 1) if u > 0 else (b - 1, UNITS - 1)),
                                (nb, nu + 1) if prepares else (b, UNITS))
                if u == 0 and last_end:
                    if g in (21, 25):
                        if g == 21:
                            wide_free(b, 1)
                        products_gated(b - 1, (g - 21) // 4)
                    if g == 28:
                        turn_a4(b - 1)
                if u == 2 and next_row:
                    if g == 24:
                        turn_x1(b + 1)
                    if g == 28:
                        turn_x2(b + 1)

        turn_x1(0)
        turn_x2(0)
        pe.wait_ge(made["prep_dve"].sem, PREP_DVE)
        pe.wait_ge(made["half_made"].sem, 12)
        product_x(0, 0, 0)
        product_x(0, 0, 1)
        product_z(0, 0)
        product_dt(0, 0, (0, 0))
        product_b(0, 0)
        product_c(0, 0)
        product_delta(0, 0)
        replicate_delta(0, 0)
        replicate_u(0, 0)
        replicate_u(0, 1)
        row(0, True, False)
        with nc.tensor.Fori(1, ROWS - 1) as b:
            row(b, True, True)
        row(ROWS - 1, False, True)
        reduce(ROWS - 1, SLOTS // 4 - 1)
        product_out(ROWS - 1, UNITS - 1, (ROWS - 1, UNITS))
        for c in range(NCH):
            products_gated(ROWS - 1, c)
        turn_a4(ROWS - 1)


def experts(nc, ctx, ident, cols, mhalf, router_w, w1, w2, b2, gamma, beta, x3_dram, out):
    def sb(name, shape, dt=F32):
        return ctx.enter_context(nc.sbuf_tensor(name, shape, dt))

    def sig(name, per):
        return Signal(ctx, nc, name, per)

    W1 = sb("W1", [P, NE, FF])
    W2 = sb("W2", [P, NE, FT, DM])
    w2mean = sb("w2mean", [P, NE, FT])
    gam = sb("gam", [P, NE, DM])
    router = sb("router", [P, NE])
    betad = sb("betad", [TT * NE, TT, DM])
    b2row = sb("b2row", [1, NE, DM])
    b2mean = sb("b2mean", [1, NE])
    ones1 = sb("ones1", [1, P])
    iota_i = sb("iota_i", [P, TT, NE], mybir.dt.int32)
    iota = sb("iota", [P, TT, NE])
    x3 = sb("x3c", [P, 2, TT, DM])
    xln = sb("xln", [P, 2, TT, DM])
    xlnT = sb("xlnT", [P, 2, TC])
    st = sb("st", [P, TT, 6])
    mv = sb("mv", [P, TT, 2])
    rs = sb("rs", [P, 2, TT])
    logits = sb("logits", [P, TT, NE])
    top = sb("top", [P, TT, 8])
    topi = sb("topi", [P, TT, 8], U32)
    topf = sb("topf", [P, TT, 2])
    gap = sb("gap", [P, TT])
    gw = sb("gw", [P, 2, TT])
    pick = sb("pick", [P, 2, TT, NE])
    gates = sb("gates", [P, 2, TT, NE])
    gT = sb("gT", [TT * NE, P])
    acc = sb("acc", [P, 2, TT, DM])
    hT = sb("hT", [P, 4, TC])
    sq = sb("sq", [P, 2, TT, DM])
    ssq = sb("ssq", [P, 2, TT])
    es = sb("es", [P, 2, 3, TT])
    wexp = sb("wexp", [P, 2, TT, DM])
    st2 = sb("st2", [P, TT, 6])
    mv2 = sb("mv2", [P, TT, 2])
    rs2 = sb("rs2", [P, 2, TT])

    Hb = ctx.enter_context(nc.psum_tensor("Hb", [P, 4, TC], F32))
    Ob = ctx.enter_context(nc.psum_tensor("Ob", [P, 2, TT, DM], F32))
    Ta = ctx.enter_context(nc.psum_tensor("Ta", [P, TC], F32))
    Tb = ctx.enter_context(nc.psum_tensor("Tb", [P, TC], F32))

    SMALL = (2 + TT) * 16
    JT = NE * FT
    sp_ticks, pool_ticks, dve_ticks = (sig(n, 0) for n in ("sp_ticks2", "pool_ticks2", "dve_ticks2"))
    small_loaded = sig("small_loaded", 0)
    w1_loaded = [sig(f"w1_{e}_loaded", 0) for e in range(NE)]
    w2_loaded = [sig(f"w2_{e}_loaded", 0) for e in range(NE)]
    b2_loaded = sig("b2_loaded", 0)
    w2_summed = sig("w2_summed", 0)
    w2_centred = sig("w2_centred", 0)
    b2_step = sig("b2_step", 0)
    beta_zero = sig("beta_zero", 0)
    const2 = sig("const2", 0)
    x3c_loaded = [sig(f"x3c_loaded{p}", 8) for p in range(2)]
    stats_done = sig("stats_done", 2 * TT)
    rstd_done = sig("rstd_done", 2)
    xln_ready = sig("xln_ready", TT)
    xln_turned = sig("xln_turned", 1)
    xlnT_ready = sig("xlnT_ready", 1)
    logits_mm = sig("logits_mm", 1)
    logits_ready = sig("logits_ready", 1)
    top_ready = sig("top_ready", TT)
    topi_ready = sig("topi_ready", TT)
    topf_ready = sig("topf_ready", 1)
    gap_ready = sig("gap_ready", 1)
    gtanh_ready = sig("gtanh_ready", 1)
    gw_ready = sig("gw_ready", 2)
    pick_step = sig("pick_step", 4)
    gates_ready = sig("gates_ready", 1)
    gates_turned = sig("gates_turned", 1)
    gT_ready = sig("gT_ready", 1)
    beta_mm = sig("beta_mm", 1)
    acc_ready = sig("acc_ready", 1)
    h_mm = sig("h_mm", JT)
    gelu_ready = sig("gelu_ready", JT)
    o_mm = sig("o_mm", JT)
    res_ready = sig("res_ready", NE)
    ssq_ready = sig("ssq_ready", NE * TT)
    evar_ready = sig("evar_ready", NE)
    erstd_ready = sig("erstd_ready", NE)
    escale_ready = sig("escale_ready", NE)
    wexp_ready = sig("wexp_ready", NE * TT)
    acc_added = sig("acc_added", NE)
    stats2_done = sig("stats2_done", 2 * TT)
    rstd2_done = sig("rstd2_done", 2)
    y_ready = sig("y_ready", TT)
    final_ready = sig("final_ready", 1)
    stored = [sig(f"stored{p}", 8) for p in range(2)]

    x3_v = x3_dram.rearrange("(c t p) d -> c p t d", t=TT, p=P)
    out_v = out.rearrange("r s d -> (r s) d").rearrange("(c t p) d -> c p t d", t=TT, p=P)

    def at(view, c):
        return view[c] if isinstance(c, int) else view[bass.ds(c, 1), :, :, :].rearrange("o p t d -> (o p) t d")

    def chunks(eng, prepare, body):
        prepare(0, 0)
        body(0, 0, True, False)
        body(1, 1, True, True)
        with eng.Fori(1, NTC // 2 - 1) as pair:
            body(pair * 2, 0, True, True)
            body(pair * 2 + 1, 1, True, True)
        body(NTC - 2, 0, True, True)
        body(NTC - 1, 1, False, True)

    block = ctx.enter_context(nc.Block())

    @block.sync
    def _(sp):
        sp.dma_start(x3[:, 0], x3_v[0]).then_inc(x3c_loaded[0].sem, 16)
        sp.dma_start(router[:, :], router_w).then_inc(small_loaded.sem, 16)
        sp.dma_start(b2row[:, :, :], b2.rearrange("(o e) d -> o e d", o=1)).then_inc(b2_loaded.sem, 16)
        sp.dma_start(W1[:, 0, :], w1[0]).then_inc(w1_loaded[0].sem, 16)
        sp.dma_start(W2[:, 0], w2[0].rearrange("(f p) d -> p f d", p=P)).then_inc(w2_loaded[0].sem, 16)
        sp.dma_start(gam[:, :, :].rearrange("p e d -> p (e d)"),
                     gamma.rearrange("(o e) d -> o (e d)", o=1).to_broadcast([P, NE * DM])) \
            .then_inc(small_loaded.sem, 16)
        sp.wait_ge(beta_zero.sem, 1)
        for t in range(TT):
            sp.dma_start(betad[NE * t:NE * t + NE, t, :], beta).then_inc(small_loaded.sem, 16)
        for e in range(1, NE):
            sp.dma_start(W1[:, e, :], w1[e]).then_inc(w1_loaded[e].sem, 16)
            sp.dma_start(W2[:, e], w2[e].rearrange("(f p) d -> p f d", p=P)).then_inc(w2_loaded[e].sem, 16)

        def load_x3(c, p):
            sp.wait_ge(final_ready.sem, final_ready.at(c, -1))
            sp.sem_inc(sp_ticks.sem, 1)
            sp.dma_start(x3[:, p], at(x3_v, c)).then_inc(x3c_loaded[p].sem, 16)

        def store(c, p):
            sp.wait_ge(final_ready.sem, final_ready.at(c, 1))
            sp.sem_inc(sp_ticks.sem, 1)
            sp.dma_start(at(out_v, c), acc[:, p]).then_inc(stored[p].sem, 16)

        def body(c, p, has_next, has_last):
            if has_next:
                load_x3(c + 1, 1 - p)
            if has_last:
                store(c - 1, 1 - p)

        chunks(nc.sync, lambda c, p: None, body)
        store(NTC - 1, 1)
        for p in range(2):
            sp.wait_ge(stored[p].sem, stored[p].at(NTC, 0))

    @block.gpsimd
    def _(pool):
        nc.gpsimd.memset(betad[:, :, :], 0.0).then_inc(beta_zero.sem, 1)
        nc.gpsimd.memset(ones1[:, :], 1.0).then_inc(const2.sem, 1)
        nc.gpsimd.iota(iota_i[:, :, :], pattern=[[0, TT], [1, NE]], base=0, channel_multiplier=0) \
            .then_inc(const2.sem, 1)

        def rstd(var, ve, r, scale, eps, done, c):
            nc.gpsimd.tensor_scalar(ve, var, scale, eps, ALU.mult, ALU.add).then_inc(done.sem, 1)
            pool.wait_ge(done.sem, done.at(c, 1))
            nc.gpsimd.tensor_tensor(r, ve, mhalf[:, 0:TT], ALU.pow).then_inc(done.sem, 1)

        def prepare(c, p):
            pool.wait_ge(stats_done.sem, stats_done.at(c, 2 * TT))
            pool.sem_inc(pool_ticks.sem, 1)
            rstd(mv[:, :, 1], rs[:, 0, :], rs[:, 1, :], 1.0, EPS_IN, rstd_done, c)

        def body(c, p, has_next, has_last):
            for e in range(NE):
                q = e % 2
                pool.wait_ge(ssq_ready.sem, ssq_ready.at(c, TT * (e + 1)))
                pool.sem_inc(pool_ticks.sem, 1)
                nc.gpsimd.tensor_scalar(es[:, q, 0, :], ssq[:, q, :], 1.0 / DM, EPS_OUT, ALU.mult, ALU.add) \
                    .then_inc(evar_ready.sem, 1)
                pool.wait_ge(evar_ready.sem, evar_ready.at(c, e + 1))
                pool.wait_ge(escale_ready.sem, escale_ready.at(c, e - 1))
                nc.gpsimd.tensor_tensor(es[:, q, 1, :], es[:, q, 0, :], mhalf[:, 0:TT], ALU.pow) \
                    .then_inc(erstd_ready.sem, 1)
                pool.wait_ge(wexp_ready.sem, wexp_ready.at(c, TT * (e + 1)))
                if e == 0:
                    pool.wait_ge(acc_ready.sem, acc_ready.at(c, 1))
                pool.wait_ge(acc_added.sem, acc_added.at(c, e))
                nc.gpsimd.tensor_tensor(acc[:, p], acc[:, p], wexp[:, q], ALU.add).then_inc(acc_added.sem, 1)
                if e == 0 and has_last:
                    pool.wait_ge(stats2_done.sem, stats2_done.at(c - 1, 2 * TT))
                    pool.sem_inc(pool_ticks.sem, 1)
                    rstd(mv2[:, :, 1], rs2[:, 0, :], rs2[:, 1, :], 1.0, EPS_IN, rstd2_done, c - 1)
                if e == 2 and has_next:
                    prepare(c + 1, 1 - p)

        chunks(nc.gpsimd, prepare, body)
        pool.wait_ge(stats2_done.sem, stats2_done.at(NTC - 1, 2 * TT))
        rstd(mv2[:, :, 1], rs2[:, 0, :], rs2[:, 1, :], 1.0, EPS_IN, rstd2_done, NTC - 1)

    @block.scalar
    def _(act):
        def take_xlnT(c, p):
            act.wait_ge(xln_turned.sem, xln_turned.at(c, 1))
            act.wait_ge(h_mm.sem, h_mm.at(c, -JT))
            nc.scalar.activation(xlnT[:, p, :], Ta[:, :], ACT.Copy).then_inc(xlnT_ready.sem, 1)

        def gate_tanh(c, p):
            act.wait_ge(gap_ready.sem, gap_ready.at(c, 1))
            nc.scalar.activation(gap[:, :], gap[:, :], ACT.Tanh, scale=0.5).then_inc(gtanh_ready.sem, 1)

        def take_gT(c, p):
            act.wait_ge(gates_turned.sem, gates_turned.at(c, 1))
            act.wait_ge(beta_mm.sem, beta_mm.at(c, 0))
            nc.scalar.activation(gT[:, :], Tb[0:TT * NE, 128:256], ACT.Copy).then_inc(gT_ready.sem, 1)

        def take_beta(c, p):
            act.wait_ge(beta_mm.sem, beta_mm.at(c, 1))
            act.wait_ge(stored[p].sem, stored[p].at(c, -8 * p))
            nc.scalar.activation(acc[:, p].rearrange("p t d -> p (t d)"), Ta[:, :], ACT.Copy) \
                .then_inc(acc_ready.sem, 1)

        def prepare(c, p):
            take_xlnT(c, p)
            gate_tanh(c, p)
            take_gT(c, p)
            take_beta(c, p)

        def gelu(c, t):
            act.wait_ge(h_mm.sem, h_mm.at(c, t + 1))
            act.wait_ge(o_mm.sem, o_mm.at(c, t + 1 - 4))
            e, f = divmod(t, FT)
            at = C_B1 + FT * e + f
            nc.scalar.activation(hT[:, t % 4, :], Hb[:, t % 4, :], ACT.Gelu, bias=cols[:, at:at + 1]) \
                .then_inc(gelu_ready.sem, 1)

        def squares(c, e):
            q = e % 2
            act.wait_ge(res_ready.sem, res_ready.at(c, e + 1))
            act.wait_ge(evar_ready.sem, evar_ready.at(c, e - 1))
            act.wait_ge(ssq_ready.sem, ssq_ready.at(c, TT * (e - 1)))
            for i in range(TT):
                nc.scalar.activation(sq[:, q, i, :], Ob[:, q, i, :], ACT.Square, accum_out=ssq[:, q, i:i + 1]) \
                    .then_inc(ssq_ready.sem, 1)

        def body(c, p, has_next, has_last):
            for t in range(JT):
                e, f = divmod(t, FT)
                gelu(c, t)
                if f == 2 and e > 0:
                    squares(c, e - 1)
                if has_next:
                    if t == 18:
                        take_xlnT(c + 1, 1 - p)
                    if t == 26:
                        gate_tanh(c + 1, 1 - p)
                    if t == 29:
                        take_gT(c + 1, 1 - p)
                    if t == 31:
                        take_beta(c + 1, 1 - p)
            squares(c, NE - 1)

        chunks(nc.scalar, prepare, body)

    @block.vector
    def _(dve):
        dve.wait_ge(const2.sem, 2)
        nc.vector.tensor_copy(iota[:, :, :], iota_i[:, :, :]).then_inc(b2_step.sem, 1)
        dve.wait_ge(b2_loaded.sem, 16)
        nc.vector.reduce_sum(b2mean[:, :], b2row[:, :, :], axis=mybir.AxisListType.X).then_inc(b2_step.sem, 1)
        dve.wait_ge(b2_step.sem, 2)
        nc.vector.tensor_scalar(b2mean[:, :], b2mean[:, :], 1.0 / DM, None, ALU.mult).then_inc(b2_step.sem, 1)
        dve.wait_ge(b2_step.sem, 3)
        nc.vector.tensor_tensor(b2row[:, :, :], b2row[:, :, :],
                                b2mean[:, :].rearrange("p (e o) -> p e o", o=1).to_broadcast([1, NE, DM]),
                                ALU.subtract).then_inc(b2_step.sem, 1)

        def centre(e):
            dve.wait_ge(w2_loaded[e].sem, 16)
            m = w2mean[:, e, :]
            nc.vector.reduce_sum(m, W2[:, e], axis=mybir.AxisListType.X).then_inc(w2_summed.sem, 1)
            dve.wait_ge(w2_summed.sem, 2 * e + 1)
            nc.vector.tensor_scalar(m, m, 1.0 / DM, None, ALU.mult).then_inc(w2_summed.sem, 1)
            dve.wait_ge(w2_summed.sem, 2 * e + 2)
            nc.vector.tensor_tensor(W2[:, e], W2[:, e],
                                    m.rearrange("p (f o) -> p f o", o=1).to_broadcast([P, FT, DM]),
                                    ALU.subtract).then_inc(w2_centred.sem, 1)

        def norm(c, p):
            dve.wait_ge(x3c_loaded[p].sem, x3c_loaded[p].at(c, 16 - 8 * p))
            dve.wait_ge(rstd_done.sem, rstd_done.at(c, 0))
            dve.wait_ge(xln_ready.sem, xln_ready.at(c, 0))
            for t in range(TT):
                nc.vector.bn_stats(st[:, t, :], x3[:, p, t, :]).then_inc(stats_done.sem, 1)
            dve.wait_ge(stats_done.sem, stats_done.at(c, TT))
            dve.sem_inc(dve_ticks.sem, 1)
            for t in range(TT):
                nc.vector.bn_aggr(mv[:, t, :], st[:, t, :]).then_inc(stats_done.sem, 1)

        def make_xln(c, p):
            dve.wait_ge(rstd_done.sem, rstd_done.at(c, 2))
            dve.wait_ge(stats_done.sem, stats_done.at(c, 2 * TT))
            dve.wait_ge(res_ready.sem, res_ready.at(c, -NE))
            for t in range(TT):
                nc.vector.tensor_scalar(xln[:, p, t, :], x3[:, p, t, :], mv[:, t, 0:1], rs[:, 1, t:t + 1],
                                        ALU.subtract, ALU.mult).then_inc(xln_ready.sem, 1)

        def top2(c, p):
            dve.wait_ge(logits_mm.sem, logits_mm.at(c, 1))
            dve.wait_ge(topi_ready.sem, topi_ready.at(c, 0))
            nc.vector.tensor_copy(logits[:, :, :].rearrange("p t e -> p (t e)"), Tb[:, 0:TT * NE]) \
                .then_inc(logits_ready.sem, 1)
            dve.wait_ge(logits_ready.sem, logits_ready.at(c, 1))
            dve.sem_inc(dve_ticks.sem, 1)
            for t in range(TT):
                nc.vector.max(top[:, t, :], logits[:, t, :]).then_inc(top_ready.sem, 1)
            dve.wait_ge(top_ready.sem, top_ready.at(c, TT))
            dve.sem_inc(dve_ticks.sem, 1)
            for t in range(TT):
                nc.vector.max_index(topi[:, t, :], top[:, t, :], logits[:, t, :]).then_inc(topi_ready.sem, 1)
            dve.wait_ge(gw_ready.sem, gw_ready.at(c, 0))
            nc.vector.tensor_tensor(gap[:, :], top[:, :, 0], top[:, :, 1], ALU.subtract).then_inc(gap_ready.sem, 1)
            dve.wait_ge(topi_ready.sem, topi_ready.at(c, TT))
            dve.wait_ge(gates_ready.sem, gates_ready.at(c, 0))
            nc.vector.tensor_copy(topf[:, :, :], topi[:, :, 0:2]).then_inc(topf_ready.sem, 1)
            dve.wait_ge(topf_ready.sem, topf_ready.at(c, 1))
            for k in range(2):
                nc.vector.tensor_tensor(pick[:, k], iota[:, :, :],
                                        topf[:, :, k:k + 1].to_broadcast([P, TT, NE]), ALU.is_equal) \
                    .then_inc(pick_step.sem, 1)

        def make_gates(c, p):
            dve.wait_ge(gtanh_ready.sem, gtanh_ready.at(c, 1))
            nc.vector.tensor_scalar(gw[:, 0, :], gap[:, :], 0.5, 0.5, ALU.mult, ALU.add).then_inc(gw_ready.sem, 1)
            nc.vector.tensor_scalar(gw[:, 1, :], gap[:, :], -0.5, 0.5, ALU.mult, ALU.add).then_inc(gw_ready.sem, 1)
            dve.wait_ge(gw_ready.sem, gw_ready.at(c, 2))
            dve.wait_ge(pick_step.sem, pick_step.at(c, 2))
            for k in range(2):
                nc.vector.tensor_tensor(pick[:, k], pick[:, k],
                                        gw[:, k, :].rearrange("p (t o) -> p t o", o=1).to_broadcast([P, TT, NE]),
                                        ALU.mult).then_inc(pick_step.sem, 1)
            dve.wait_ge(pick_step.sem, pick_step.at(c, 4))
            dve.wait_ge(escale_ready.sem, escale_ready.at(c, -NE))
            dve.wait_ge(gates_turned.sem, gates_turned.at(c, -1))
            nc.vector.tensor_tensor(gates[:, p], pick[:, 0], pick[:, 1], ALU.add).then_inc(gates_ready.sem, 1)

        def add_residual(c, e, p):
            q = e % 2
            dve.wait_ge(o_mm.sem, o_mm.at(c, FT * (e + 1)))
            nc.vector.tensor_tensor(Ob[:, q], Ob[:, q], xln[:, p], ALU.add).then_inc(res_ready.sem, 1)

        def scale(c, e, p):
            q = e % 2
            dve.wait_ge(erstd_ready.sem, erstd_ready.at(c, e + 1))
            if e == 0:
                dve.wait_ge(gates_ready.sem, gates_ready.at(c, 1))
            nc.vector.tensor_tensor(es[:, q, 2, :], es[:, q, 1, :], gates[:, p, :, e], ALU.mult) \
                .then_inc(escale_ready.sem, 1)
            dve.wait_ge(escale_ready.sem, escale_ready.at(c, e + 1))
            dve.wait_ge(acc_added.sem, acc_added.at(c, e - 1))
            for t in range(TT):
                nc.vector.scalar_tensor_tensor(wexp[:, q, t, :], Ob[:, q, t, :], es[:, q, 2, t:t + 1],
                                               gam[:, e, :], ALU.mult, ALU.mult).then_inc(wexp_ready.sem, 1)

        def stats_last(c, p):
            dve.wait_ge(acc_added.sem, acc_added.at(c, NE))
            dve.wait_ge(rstd2_done.sem, rstd2_done.at(c, 0))
            dve.wait_ge(y_ready.sem, y_ready.at(c, 0))
            for t in range(TT):
                nc.vector.bn_stats(st2[:, t, :], acc[:, p, t, :]).then_inc(stats2_done.sem, 1)
            dve.wait_ge(stats2_done.sem, stats2_done.at(c, TT))
            dve.sem_inc(dve_ticks.sem, 1)
            for t in range(TT):
                nc.vector.bn_aggr(mv2[:, t, :], st2[:, t, :]).then_inc(stats2_done.sem, 1)

        def finish(c, p):
            dve.wait_ge(rstd2_done.sem, rstd2_done.at(c, 2))
            dve.wait_ge(stats2_done.sem, stats2_done.at(c, 2 * TT))
            for t in range(TT):
                nc.vector.tensor_scalar(acc[:, p, t, :], acc[:, p, t, :], mv2[:, t, 0:1], rs2[:, 1, t:t + 1],
                                        ALU.subtract, ALU.mult).then_inc(y_ready.sem, 1)
            dve.wait_ge(y_ready.sem, y_ready.at(c, TT))
            nc.vector.tensor_tensor(acc[:, p], acc[:, p], x3[:, p], ALU.add).then_inc(final_ready.sem, 1)

        def prepare(c, p):
            norm(c, p)
            make_xln(c, p)
            centre(0)
            top2(c, p)
            make_gates(c, p)

        def body(c, p, has_next, has_last):
            for e in range(NE):
                if isinstance(c, int) and c == 0 and e < NE - 1:
                    if e == 0:
                        centre(1)
                    if e + 2 < NE:
                        centre(e + 2)
                add_residual(c, e, p)
                if e > 0:
                    scale(c, e - 1, p)
                if e == 0 and has_last:
                    scale(c - 1, NE - 1, 1 - p)
                    stats_last(c - 1, 1 - p)
                if e == 1 and has_last:
                    finish(c - 1, 1 - p)
                if has_next:
                    if e == 2:
                        norm(c + 1, 1 - p)
                    if e == 3:
                        make_xln(c + 1, 1 - p)
                    if e == 5:
                        top2(c + 1, 1 - p)
                    if e == 6:
                        make_gates(c + 1, 1 - p)

        chunks(nc.vector, prepare, body)
        scale(NTC - 1, NE - 1, 1)
        stats_last(NTC - 1, 1)
        finish(NTC - 1, 1)

    @block.tensor
    def _(pe):
        def turn_xln(c, p):
            pe.wait_ge(xln_ready.sem, xln_ready.at(c, TT))
            pe.wait_ge(acc_ready.sem, acc_ready.at(c, 0))
            for t in range(TT):
                last = nc.tensor.transpose(Ta[:, P * t:P * t + P], xln[:, p, t, :], ident[:, :])
            last.then_inc(xln_turned.sem, 1)

        def route(c, p):
            pe.wait_ge(xlnT_ready.sem, xlnT_ready.at(c, 1))
            pe.wait_ge(gT_ready.sem, gT_ready.at(c, 0))
            for t in range(TT):
                last = nc.tensor.matmul(Tb[:, NE * t:NE * t + NE], xlnT[:, p, P * t:P * t + P], router[:, :],
                                        start=True, stop=True)
            last.then_inc(logits_mm.sem, 1)

        def turn_gates(c, p):
            pe.wait_ge(gates_ready.sem, gates_ready.at(c, 1))
            nc.tensor.transpose(Tb[0:TT * NE, 128:256], gates[:, p].rearrange("p t e -> p (t e)"), ident[:, :]) \
                .then_inc(gates_turned.sem, 1)

        def add_beta(c, p):
            pe.wait_ge(gT_ready.sem, gT_ready.at(c, 1))
            nc.tensor.matmul(Ta[:, :], gT[:, :], betad[:, :, :].rearrange("k t d -> k (t d)"),
                             start=True, stop=True).then_inc(beta_mm.sem, 1)

        def prepare(c, p):
            turn_xln(c, p)
            pe.wait_ge(small_loaded.sem, SMALL)
            route(c, p)
            turn_gates(c, p)
            add_beta(c, p)

        def hidden(c, t, p):
            e, f = divmod(t, FT)
            if isinstance(c, int) and c == 0 and f == 0:
                pe.wait_ge(w1_loaded[e].sem, 16)
            if t == 0:
                pe.wait_ge(xlnT_ready.sem, xlnT_ready.at(c, 1))
            pe.wait_ge(gelu_ready.sem, gelu_ready.at(c, t + 1 - 4))
            nc.tensor.matmul(Hb[:, t % 4, :], W1[:, e, P * f:P * f + P], xlnT[:, p, :], start=True, stop=True) \
                .then_inc(h_mm.sem, 1)

        def outputs(c, t, p):
            e, f = divmod(t, FT)
            q = e % 2
            if f == 0:
                if isinstance(c, int) and c == 0:
                    pe.wait_ge(w2_centred.sem, e + 1)
                    pe.wait_ge(b2_step.sem, 4)
                pe.wait_ge(wexp_ready.sem, wexp_ready.at(c, TT * (e - 1)))
                nc.tensor.matmul(Ob[:, q].rearrange("p t d -> p (t d)"), ones1[:, :],
                                 b2row[:, e:e + 1, :].to_broadcast([1, TT, DM]), start=True, stop=False,
                                 skip_group_check=True)
            pe.wait_ge(gelu_ready.sem, gelu_ready.at(c, t + 1))
            for i in range(TT):
                last = nc.tensor.matmul(Ob[:, q, i, :], hT[:, t % 4, P * i:P * i + P], W2[:, e, f, :],
                                        start=False, stop=(f == FT - 1), skip_group_check=True)
            last.then_inc(o_mm.sem, 1)

        def body(c, p, has_next, has_last):
            hidden(c, 0, p)
            hidden(c, 1, p)
            for t in range(JT):
                if t + 2 < JT:
                    hidden(c, t + 2, p)
                outputs(c, t, p)
                if has_next:
                    if t == 17:
                        turn_xln(c + 1, 1 - p)
                    if t == 20:
                        route(c + 1, 1 - p)
                    if t == 28:
                        turn_gates(c + 1, 1 - p)
                    if t == 30:
                        add_beta(c + 1, 1 - p)

        chunks(nc.tensor, prepare, body)


_INS = ['L0_attn_x', 'L0_attn_ln_w', 'L0_attn_ln_b', 'L0_attn_W_in', 'L0_attn_b_in', 'L0_attn_conv_w',
        'L0_attn_conv_b', 'L0_attn_W_xproj', 'L0_attn_W_dt', 'L0_attn_b_dt', 'L0_attn_A_log', 'L0_attn_D',
        'L0_attn_W_out', 'L0_attn_b_out', 'L0_attn_Wg', 'L0_attn_bg', 'L0_attn_Wv', 'L0_attn_bv',
        'L0_ffn_router_w', 'L0_ffn_w1', 'L0_ffn_b1', 'L0_ffn_w2', 'L0_ffn_b2', 'L0_ffn_gamma',
        'L0_ffn_beta']


def kernel(**inputs):
    import numpy as np
    import concourse.bacc as bacc
    from concourse.bass_utils import run_bass_kernel_spmd

    nc = bacc.Bacc("TRN2", target_bir_lowering=False, num_devices=1)
    arrays, args = {}, []
    for name in _INS:
        a = np.ascontiguousarray(inputs[name])
        arrays[f"in_{name}"] = a
        args.append(nc.dram_tensor(f"in_{name}", a.shape, mybir.dt.from_np(a.dtype), kind="ExternalInput").ap())
    out = nc.dram_tensor("out_0", (ROWS, STEPS, DM), F32, kind="ExternalOutput").ap()
    build(nc, *args, out)
    r = run_bass_kernel_spmd(nc, [arrays], core_ids=[0])
    return r.results[0]["out_0"]
```

```python
from contextlib import ExitStack

import concourse.bass as bass
from concourse import mybir

F32 = mybir.dt.float32
F32R = mybir.dt.float32r
U32 = mybir.dt.uint32
ALU = mybir.AluOpType
ACT = mybir.ActivationFunctionType

P = 128
ROWS, STEPS, DM = 8, 1024, 128
DI, NS, RANK, TAPS = 256, 16, 64, 4
NH = DI // P
CH = 512
NCH = STEPS // CH
UNITS = 2 * NCH
CPG = P // NS
GPH = P // CPG
GROUPS = NH * GPH
SLOTS = UNITS * GROUPS
TILES = STEPS // P
PAD = TAPS - 1
HRING, XRING, DRING = 8, 4, 3
LAG = 4
EPS_IN, EPS_OUT = 1e-5, 1e-6
NE, FF = 8, 512
FT = FF // P
TC = 512
NTC = ROWS * STEPS // TC
TT = TC // P


class Signal:

    def __init__(self, ctx, nc, name, per):
        self.sem, self.per = ctx.enter_context(nc.semaphore(name)), per

    def at(self, row, count):
        value = row * self.per + count
        return max(value, 0) if isinstance(value, int) else value


def unit_of(u):
    return (0, u) if u < NCH else (1, 2 * NCH - 1 - u)


def group_of(g):
    half, j = divmod(g, GPH)
    tile, r = j % 4, j // 4
    jj = 4 * tile + r
    return half, jj, jj % 8, 2 * half + jj // 8, tile, r


def decay_buffer(s):
    if s >= DRING:
        return s % DRING, s - DRING
    return s, max(e for e in range(-DRING - 1, 0) if (SLOTS + e) % DRING == s)


def directed(ap, direction):
    return ap if direction == 0 else ap[:, ::-1]


def build(nc, x, ln_w, ln_b, W_in, b_in, conv_w, conv_b, W_xproj, W_dt, b_dt, A_log, Dp, W_out,
          b_out, Wg, bg, Wv, bv, router_w, w1, b1, w2, b2, gamma, beta, out):
    ctx = ExitStack()
    with ctx:
        x3_dram = nc.dram_tensor("x3_scratch", (ROWS * STEPS, DM), F32, kind="Internal").ap()
        ident = ctx.enter_context(nc.sbuf_tensor("ident", [P, P], F32))
        cols = ctx.enter_context(nc.sbuf_tensor("cols", [P, 124], F32))
        mhalf = ctx.enter_context(nc.sbuf_tensor("mhalf", [P, 8], F32))
        with ExitStack() as phase:
            mamba(nc, phase, ident, cols, mhalf, x, ln_w, ln_b, W_in, b_in, conv_w, conv_b, W_xproj,
                  W_dt, b_dt, A_log, Dp, W_out, b_out, Wg, bg, Wv, bv, b1, x3_dram)
        with ExitStack() as phase:
            experts(nc, phase, ident, cols, mhalf, router_w, w1, w2, b2, gamma, beta, x3_dram, out)


STACK_DMAS = 4 * 16
LOADS = 21 * 16
PREP_DVE = 39

C_LNW, C_LNB, C_BIN, C_CONVB, C_BDT, C_D, C_BOUT, C_BG, C_BV, C_B1, C_A = \
    0, 2, 4, 12, 16, 20, 24, 26, 27, 28, 60


def mamba(nc, ctx, ident, cols, mhalf, x, ln_w, ln_b, W_in, b_in, conv_w, conv_b, W_xproj, W_dt,
          b_dt, A_log, Dp, W_out, b_out, Wg, bg, Wv, bv, b1, x3_dram):
    def sb(name, shape, dt=F32):
        return ctx.enter_context(nc.sbuf_tensor(name, shape, dt))

    def pb(name, shape):
        return ctx.enter_context(nc.psum_tensor(name, shape, F32))

    def sig(name, per):
        return Signal(ctx, nc, name, per)

    rows = sb("rows", [P, P])
    sel = sb("sel", [P, 8, P], F32R)
    red = sb("red", [P, 4, 32])
    negA = sb("negA", [P, 2 * GROUPS])
    taps = sb("taps", [P, 2, NH, TAPS])
    Wk = sb("Wk", [P, 2, TAPS, DI])
    Wz = sb("Wz", [P, 2, DI])
    bz = sb("bz", [P, 2 * 4])
    cbias = sb("cbias", [P, 4])
    edge = sb("edge", [P, 2, 3, NH])
    psum4 = sb("psum4", [P, 4, 4])
    Wdtx = sb("Wdtx", [P, 2, NH, RANK])
    Wbc = sb("Wbc", [P, 2, NH, 2, P])
    Wdt = sb("Wdt", [RANK, 2, DI])
    Wo = sb("Wo", [P, 2, NH, DM])
    Wgs = sb("Wgs", [P, 2, DM])
    Wvs = sb("Wvs", [P, 2, DM])
    halfD = sb("halfD", [P, 4])
    halfbg = sb("halfbg", [P, 1])
    ones = sb("ones", [P, 2])
    xn = sb("xn", [P, TILES, DM])
    xt = sb("xt", [P, TILES, DM])
    tok = sb("tok", [P, TILES, DM])
    x2T = sb("x2T", [P, STEPS + 2 * PAD])
    stA = sb("stA", [P, TILES, 6])
    mvA = sb("mvA", [P, TILES, 2])
    rsA = sb("rsA", [P, 5, TILES])
    th = sb("th", [P, NH, CH])
    xp2 = sb("xp2", [P, 2, NH, CH])
    sz2 = sb("sz2", [P, 2, NH, CH])
    Brep = sb("Brep", [P, 2, CH])
    Crep = sb("Crep", [P, 2, CH])
    dtT = sb("dtT", [RANK, CH])
    ex = sb("ex", [P, NH, CH])
    rl = sb("rl", [P, NH, CH])
    lg = sb("lg", [P, NH, CH])
    w1p = sb("w1p", [P, NH, CH])
    u2 = sb("u2", [P, NH, CH])
    dhi = sb("dhi", [P, NH, CH], F32R)
    dlo = sb("dlo", [P, NH, CH], F32R)
    uhi = sb("uhi", [P, NH, CH], F32R)
    ulo = sb("ulo", [P, NH, CH], F32R)
    stackD = sb("stackD", [P, 4, CH], F32R)
    stackU = sb("stackU", [P, 4, CH], F32R)
    yg = sb("yg", [P, NH, CH])
    fbT = sb("fbT", [P, 2, STEPS])
    dbx = sb("dbx", [P, XRING, CH])
    hs = sb("hs", [P, HRING, CH])
    carry = sb("carry", [P, 2 * GROUPS])
    sfb = sb("sfb", [P, CH])
    tg = sb("tg", [P, CH])
    a4 = sb("a4", [P, STEPS])
    x3 = sb("x3", [P, TILES, DM])
    stG = sb("stG", [P, TILES, 6])
    mvG = sb("mvG", [P, TILES, 2])
    rsG = sb("rsG", [P, 2, TILES])

    D = pb("D", [P, DRING, CH])
    U = pb("U", [P, 2, CH])
    Y = pb("Y", [P, CH])
    W = pb("W", [P, NH, CH])

    win_raw = hs[:, 0:2, :]
    taps_b = hs[:, 2:6, :].rearrange("p a b -> p (a b)").rearrange("p (d c k) -> p d c k", d=2, k=TAPS)
    wx_raw = hs[:, 6, 0:384].rearrange("p (d h n) -> p d h n", d=2, h=NH)
    sel_f = ex[:, :, :].rearrange("p h t -> p (h t)").rearrange("p (k m) -> p k m", k=8)

    loaded = sig("loaded", 0)
    made = {n: sig(n, 0) for n in ("ident_made", "masks_made", "cols_made", "bias_mm", "prep_dve",
                                   "rows_T", "zeros_made", "a_made", "half_made")}
    sp_ticks, pool_ticks, dve_ticks = (sig(n, 0) for n in ("sp_ticks", "pool_ticks", "dve_ticks"))
    x_loaded = sig("x_loaded", 16)
    xres_loaded = sig("xres_loaded", 16)
    x3_stored = sig("x3_stored", 16)
    dstack_loaded = [sig(f"dstack{h}_loaded", UNITS * STACK_DMAS) for h in range(NH)]
    ustack_loaded = [sig(f"ustack{h}_loaded", UNITS * STACK_DMAS) for h in range(NH)]
    statsA = sig("statsA", 2 * TILES)
    rstdA = sig("rstdA", 7)
    x1_ready = sig("x1_ready", TILES)
    x2_ready = sig("x2_ready", TILES)
    x2_turned = sig("x2_turned", 1)
    x2T_ready = sig("x2T_ready", 1)
    xp_mm = sig("xp_mm", UNITS * NH)
    conv_ready = sig("conv_ready", UNITS * NH)
    edge_done = sig("edge_done", 2 * NH)
    thx_ready = sig("thx_ready", UNITS * NH)
    xp_ready = sig("xp_ready", UNITS * NH)
    z_mm = sig("z_mm", UNITS * NH)
    z_ready = sig("z_ready", UNITS * NH)
    thz_ready = sig("thz_ready", UNITS)
    sz_ready = sig("sz_ready", UNITS)
    dt_mm = sig("dt_mm", UNITS)
    dt_ready = sig("dt_ready", UNITS)
    b_mm = sig("b_mm", UNITS)
    b_ready = sig("b_ready", UNITS)
    c_mm = sig("c_mm", UNITS)
    c_ready = sig("c_ready", UNITS)
    dp_mm = sig("dp_mm", UNITS * NH)
    abs_ready = sig("abs_ready", UNITS * NH)
    relu_ready = sig("relu_ready", UNITS * NH)
    exp_ready = sig("exp_ready", UNITS)
    onep_ready = sig("onep_ready", UNITS)
    back_ready = sig("back_ready", UNITS)
    ln_ready = sig("ln_ready", UNITS)
    resid_ready = sig("resid_ready", UNITS * NH)
    sp_sum = sig("sp_sum", UNITS)
    delta_ready = sig("delta_ready", UNITS * NH)
    dhi_ready = sig("dhi_ready", UNITS * NH)
    dlo_ready = sig("dlo_ready", UNITS * NH)
    u_ready = sig("u_ready", UNITS * NH)
    uhi_ready = sig("uhi_ready", UNITS * NH)
    ulo_ready = sig("ulo_ready", UNITS * NH)
    drep_ready = sig("drep_ready", SLOTS)
    urep_ready = sig("urep_ready", SLOTS)
    da_ready = sig("da_ready", SLOTS)
    dbx_ready = sig("dbx_ready", SLOTS)
    h_ready = sig("h_ready", SLOTS)
    carry_saved = sig("carry_saved", GROUPS)
    hc_ready = sig("hc_ready", SLOTS // 2)
    reduced = sig("reduced", SLOTS // 4)
    yd_ready = sig("yd_ready", UNITS * NH)
    yg_ready = sig("yg_ready", UNITS * NH)
    out_mm = sig("out_mm", UNITS)
    fb_ready = sig("fb_ready", UNITS)
    gate_mm = sig("gate_mm", NCH)
    value_mm = sig("value_mm", NCH)
    sfb_ready = sig("sfb_ready", NCH)
    tg_ready = sig("tg_ready", NCH)
    diff_ready = sig("diff_ready", NCH)
    gated_ready = sig("gated_ready", NCH)
    a4_ready = sig("a4_ready", NCH)
    a4_turned = sig("a4_turned", 1)
    sum_copied = sig("sum_copied", 1)
    statsG = sig("statsG", 2 * TILES)
    rstdG = sig("rstdG", 2)
    an_ready = sig("an_ready", TILES)
    x3_ready = sig("x3_ready", 1)

    x_rows = x.rearrange("r (t p) d -> r p t d", p=P)
    x3_rows = x3_dram.rearrange("(r t p) d -> r p t d", r=ROWS, p=P)

    def dram_row(view, b):
        return view[b] if isinstance(b, int) else view[bass.ds(b, 1), :, :, :].rearrange("o p t d -> (o p) t d")

    block = ctx.enter_context(nc.Block())

    @block.sync
    def _(sp):
        def load(dst, src):
            sp.dma_start(dst, src).then_inc(loaded.sem, 16)
            load.n += 16

        load.n = 0
        for at, t in ((C_LNW, ln_w), (C_LNB, ln_b), (C_BIN, b_in), (C_CONVB, conv_b), (C_BDT, b_dt),
                      (C_D, Dp), (C_BOUT, b_out), (C_B1, b1)):
            n = t.shape[0] * t.shape[1] // P
            load(rows[at:at + n, :], t.rearrange("a (b c) -> (a b) c", c=P))
        load(rows[C_BG:C_BG + 1, :], bg.rearrange("(a c) -> a c", a=1))
        load(rows[C_BV:C_BV + 1, :], bv.rearrange("(a c) -> a c", a=1))
        load(rows[C_A:C_A + 2 * GROUPS, :], A_log.rearrange("d (g c) n -> (d g) (c n)", c=CPG))
        load(win_raw, W_in.rearrange("d p c -> p d c"))
        load(taps[:, :, :, :], conv_w.rearrange("d (h p) k -> p d h k", p=P))
        load(hs[:, 2:6, :].rearrange("p a b -> p (a b)"),
             conv_w.rearrange("(o d) c k -> o (d c k)", o=1).to_broadcast([P, 2 * DI * TAPS]))
        for d in range(2):
            load(wx_raw[:, d], W_xproj[d].rearrange("(h p) n -> p h n", p=P))
            load(Wo[:, d], W_out[d].rearrange("(h p) n -> p h n", p=P))
        load(Wdt[:, :, :], W_dt.rearrange("d r c -> r d c"))
        load(Wgs[:, :, :], Wg.rearrange("(h p) n -> p h n", p=P))
        load(Wvs[:, :, :], Wv.rearrange("(h p) n -> p h n", p=P))
        assert load.n == LOADS

        def load_x(b):
            sp.wait_ge(x1_ready.sem, x1_ready.at(b, 0))
            sp.sem_inc(sp_ticks.sem, 1)
            sp.wait_ge(x2_ready.sem, x2_ready.at(b, 0))
            sp.sem_inc(sp_ticks.sem, 1)
            sp.dma_start(xn[:, :, :], dram_row(x_rows, b)).then_inc(x_loaded.sem, 16)

        def stacks(b, u, half):
            sp.wait_ge(drep_ready.sem, drep_ready.at(b, GROUPS * (u - 1) + GPH * (half + 1)))
            sp.sem_inc(sp_ticks.sem, 1)
            sp.wait_ge(urep_ready.sem, urep_ready.at(b, GROUPS * (u - 1) + GPH * (half + 1)))
            sp.sem_inc(sp_ticks.sem, 1)
            for hi, lo, hi_ready, lo_ready, stack, signal in (
                    (dhi, dlo, dhi_ready, dlo_ready, stackD, dstack_loaded[half]),
                    (uhi, ulo, uhi_ready, ulo_ready, stackU, ustack_loaded[half])):
                sp.wait_ge(hi_ready.sem, hi_ready.at(b, NH * u + half + 1))
                sp.sem_inc(sp_ticks.sem, 1)
                sp.wait_ge(lo_ready.sem, lo_ready.at(b, NH * u + half + 1))
                sp.sem_inc(sp_ticks.sem, 1)
                for a in range(2):
                    for k, part in enumerate((hi, lo)):
                        sp.dma_start(stack[64 * k:64 * k + 64, 2 * half + a, :].bitcast(F32),
                                     part[64 * a:64 * a + 64, half, :].bitcast(F32)) \
                            .then_inc(signal.sem, 16)

        def load_residual(b):
            sp.dma_start(x3[:, :, :], dram_row(x_rows, b)).then_inc(xres_loaded.sem, 16)

        def store_x3(b):
            sp.wait_ge(x3_ready.sem, x3_ready.at(b, 1))
            sp.sem_inc(sp_ticks.sem, 1)
            sp.dma_start(dram_row(x3_rows, b), x3[:, :, :]).then_inc(x3_stored.sem, 16)
            sp.wait_ge(x3_stored.sem, x3_stored.at(b, 16))
            sp.sem_inc(sp_ticks.sem, 1)

        def row(b, next_row, last_end):
            for u in range(UNITS):
                stacks(b, u, 1)
                if u == 1 and next_row:
                    load_x(b + 1)
                if u == 2 and last_end:
                    load_residual(b - 1)
                if u < UNITS - 1:
                    stacks(b, u + 1, 0)
                elif next_row:
                    stacks(b + 1, 0, 0)
                if u == 3 and last_end:
                    store_x3(b - 1)

        load_x(0)
        stacks(0, 0, 0)
        row(0, True, False)
        with nc.sync.Fori(1, ROWS - 1) as b:
            row(b, True, True)
        row(ROWS - 1, False, True)
        load_residual(ROWS - 1)
        store_x3(ROWS - 1)
    @block.gpsimd
    def _(pool):
        nc.gpsimd.memset(ident[:, :], 0.0).then_inc(made["zeros_made"].sem, 1)
        nc.gpsimd.memset(sel_f, 0.0).then_inc(made["zeros_made"].sem, 1)
        nc.gpsimd.memset(red[:, :, :], 1.0).then_inc(made["zeros_made"].sem, 1)
        nc.gpsimd.memset(mhalf[:, :], -0.5).then_inc(made["zeros_made"].sem, 1)
        nc.gpsimd.memset(x2T[:, 0:PAD], 0.0).then_inc(made["zeros_made"].sem, 1)
        nc.gpsimd.memset(x2T[:, PAD + STEPS:], 0.0).then_inc(made["zeros_made"].sem, 1)
        pool.wait_ge(made["zeros_made"].sem, 6)
        nc.gpsimd.affine_select(out=ident[:, :], in_=ident[:, :], compare_op=ALU.not_equal, fill=1.0,
                                base=0, pattern=[[-1, P]], channel_multiplier=1) \
            .then_inc(made["ident_made"].sem, 1)
        s4 = sel_f.rearrange("p k (d n) -> p k d n", n=NS)
        for i, base in enumerate((0, -64)):
            nc.gpsimd.affine_select(out=s4, in_=s4, compare_op=ALU.not_equal, fill=1.0, base=base,
                                    pattern=[[-CPG, 8], [-1, CPG], [0, NS]], channel_multiplier=1) \
                .then_inc(made["masks_made"].sem, 1)
            pool.wait_ge(made["masks_made"].sem, i + 1)
        nc.gpsimd.affine_select(out=red[:, :, :], in_=red[:, :, :], compare_op=ALU.is_ge, fill=0.0,
                                base=0, pattern=[[P, 4], [-NS, 32]], channel_multiplier=1) \
            .then_inc(made["masks_made"].sem, 1)
        pool.wait_ge(made["masks_made"].sem, 3)
        nc.gpsimd.affine_select(out=red[:, :, :], in_=red[:, :, :], compare_op=ALU.is_ge, fill=0.0,
                                base=NS - 1, pattern=[[-P, 4], [NS, 32]], channel_multiplier=-1) \
            .then_inc(made["masks_made"].sem, 1)
        pool.wait_ge(made["masks_made"].sem, 4)

        def rstds_in(b):
            pool.wait_ge(statsA.sem, statsA.at(b, 2 * TILES))
            pool.sem_inc(pool_ticks.sem, 1)
            var, ve, r1, v2, r2 = mvA[:, :, 1], rsA[:, 0, :], rsA[:, 1, :], rsA[:, 2, :], rsA[:, 3, :]
            nc.gpsimd.tensor_scalar(ve, var, 1.0, EPS_IN, ALU.mult, ALU.add).then_inc(rstdA.sem, 1)
            pool.wait_ge(rstdA.sem, rstdA.at(b, 1))
            nc.gpsimd.tensor_tensor(r1, ve, mhalf[:, :], ALU.pow).then_inc(rstdA.sem, 1)
            pool.wait_ge(rstdA.sem, rstdA.at(b, 2))
            nc.gpsimd.tensor_tensor(v2, r1, r1, ALU.mult).then_inc(rstdA.sem, 1)
            pool.wait_ge(rstdA.sem, rstdA.at(b, 3))
            nc.gpsimd.tensor_tensor(v2, v2, var, ALU.mult).then_inc(rstdA.sem, 1)
            pool.wait_ge(rstdA.sem, rstdA.at(b, 4))
            pool.sem_inc(pool_ticks.sem, 1)
            nc.gpsimd.tensor_scalar(v2, v2, 1.0, EPS_IN, ALU.mult, ALU.add).then_inc(rstdA.sem, 1)
            pool.wait_ge(rstdA.sem, rstdA.at(b, 5))
            nc.gpsimd.tensor_tensor(r2, v2, mhalf[:, :], ALU.pow).then_inc(rstdA.sem, 1)
            pool.wait_ge(rstdA.sem, rstdA.at(b, 6))
            nc.gpsimd.tensor_tensor(rsA[:, 4, :], r1, r2, ALU.mult).then_inc(rstdA.sem, 1)

        def make_x1(b):
            pool.wait_ge(out_mm.sem, out_mm.at(b, 0))
            pool.wait_ge(rstdA.sem, rstdA.at(b, 7))
            pool.wait_ge(statsA.sem, statsA.at(b, 2 * TILES))
            pool.sem_inc(pool_ticks.sem, 1)
            for t in range(TILES):
                nc.gpsimd.tensor_scalar(xt[:, t, :], xn[:, t, :], mvA[:, t, 0:1], rsA[:, 1, t:t + 1],
                                        ALU.subtract, ALU.mult).then_inc(x1_ready.sem, 1)

        def softplus_residue(b, u, half):
            pool.wait_ge(exp_ready.sem, exp_ready.at(b, u + 1))
            pool.wait_ge(back_ready.sem, back_ready.at(b, u + 1))
            nc.gpsimd.tensor_tensor(w1p[:, half, :], ex[:, half, :], w1p[:, half, :], ALU.subtract) \
                .then_inc(resid_ready.sem, 1)

        def make_u(b, u, half):
            k = NH * u + half + 1
            pool.wait_ge(delta_ready.sem, delta_ready.at(b, k))
            pool.wait_ge(xp_ready.sem, xp_ready.at(b, k))
            nc.gpsimd.tensor_tensor(u2[:, half, :], lg[:, half, :], xp2[:, u % 2, half, :], ALU.mult) \
                .then_inc(u_ready.sem, 1)

        def low_u(b, u, half):
            pool.wait_ge(uhi_ready.sem, uhi_ready.at(b, NH * u + half + 1))
            pool.wait_ge(ustack_loaded[half].sem, ustack_loaded[half].at(b, STACK_DMAS * u))
            nc.gpsimd.tensor_tensor(ulo[:, half, :], u2[:, half, :], uhi[:, half, :].bitcast(F32), ALU.subtract) \
                .then_inc(ulo_ready.sem, 1)

        def two_groups(b, s):
            u, g = divmod(s, GROUPS)
            direction, _ = unit_of(u)
            h = hs[:, s % HRING:s % HRING + 2, :]
            pool.wait_ge(h_ready.sem, h_ready.at(b, s + 2))
            if u % 2 == 0:
                pool.sem_inc(pool_ticks.sem, 1)
                last = CH - 1 if direction == 0 else 0
                at = direction * GROUPS + g
                nc.gpsimd.tensor_copy(carry[:, at:at + 2], h[:, :, last]).then_inc(carry_saved.sem, 1)
                pool.wait_ge(carry_saved.sem, carry_saved.at(b, at // 2 + 1))
            if g == 0:
                pool.wait_ge(c_ready.sem, c_ready.at(b, u + 1))
            nc.gpsimd.tensor_tensor(h, h, Crep[:, u % 2:u % 2 + 1, :].to_broadcast([P, 2, CH]), ALU.mult) \
                .then_inc(hc_ready.sem, 1)

        def sum_directions(b, c):
            pool.wait_ge(fb_ready.sem, fb_ready.at(b, UNITS))
            if c:
                pool.wait_ge(a4_ready.sem, a4_ready.at(b, c))
            cut = slice(CH * c, CH * c + CH)
            nc.gpsimd.tensor_tensor(sfb[:, :], fbT[:, 0, cut], fbT[:, 1, cut], ALU.add) \
                .then_inc(sfb_ready.sem, 1)

        def rstds_gated(b):
            pool.wait_ge(statsG.sem, statsG.at(b, 2 * TILES))
            pool.sem_inc(pool_ticks.sem, 1)
            nc.gpsimd.tensor_scalar(rsG[:, 0, :], mvG[:, :, 1], 1.0, 16 * EPS_IN, ALU.mult, ALU.add) \
                .then_inc(rstdG.sem, 1)
            pool.wait_ge(rstdG.sem, rstdG.at(b, 1))
            nc.gpsimd.tensor_tensor(rsG[:, 1, :], rsG[:, 0, :], mhalf[:, :], ALU.pow) \
                .then_inc(rstdG.sem, 1)

        def row(b, next_row, last_end):
            for s in range(1, SLOTS, 2):
                u, g = divmod(s, GROUPS)
                two_groups(b, s - 1)
                nb, nu = (b, u + 1) if u < UNITS - 1 else (b + 1, 0)
                if u < UNITS - 1 or next_row:
                    if g == 17:
                        softplus_residue(nb, nu, 0)
                    if g == 19:
                        softplus_residue(nb, nu, 1)
                    if g == 21:
                        make_u(nb, nu, 0)
                    if g == 23:
                        low_u(nb, nu, 0)
                    if g == 25:
                        make_u(nb, nu, 1)
                    if g == 27:
                        low_u(nb, nu, 1)
                if u < NCH and last_end and g == 15:
                    sum_directions(b - 1, u)
                if u == 0 and g == 13 and last_end:
                    make_x1(b)
                if u == 2 and next_row and g == 3:
                    rstds_in(b + 1)
                if u == 3 and last_end and g == 29:
                    rstds_gated(b - 1)

        rstds_in(0)
        make_x1(0)
        for half in range(NH):
            softplus_residue(0, 0, half)
        for half in range(NH):
            make_u(0, 0, half)
            low_u(0, 0, half)
        row(0, True, False)
        with nc.gpsimd.Fori(1, ROWS - 1) as b:
            row(b, True, True)
        row(ROWS - 1, False, True)
        for c in range(NCH):
            sum_directions(ROWS - 1, c)
        rstds_gated(ROWS - 1)

    @block.scalar
    def _(act):
        act.wait_ge(made["rows_T"].sem, 1)
        nc.scalar.activation(cols[:, :], W[:, 0, 0:124], ACT.Copy).then_inc(made["cols_made"].sem, 1)
        act.wait_ge(made["cols_made"].sem, 1)
        nc.scalar.activation(negA[:, :], cols[:, C_A:C_A + 2 * GROUPS], ACT.Exp).then_inc(made["a_made"].sem, 1)
        act.wait_ge(made["a_made"].sem, 1)
        nc.scalar.mul(negA[:, :], negA[:, :], -1.0).then_inc(made["a_made"].sem, 1)
        act.wait_ge(made["a_made"].sem, 2)
        nc.scalar.activation(halfbg[:, :], cols[:, C_BG:C_BG + 1], ACT.Copy).then_inc(sum_copied.sem, 1)
        act.wait_ge(sum_copied.sem, 1)
        act.wait_ge(loaded.sem, LOADS)
        for i, (dst, src, f) in enumerate((
                (halfD[:, :], cols[:, C_D:C_D + 4], 0.5),
                (halfbg[:, :], halfbg[:, :], 0.5),
                (Wo[:, :, :, :], Wo[:, :, :, :], 0.5),
                (Wdtx[:, :, :, :], wx_raw[:, :, :, 0:RANK], 0.5))):
            nc.scalar.mul(dst, src, f).then_inc(made["half_made"].sem, 1)
        for d in range(2):
            for h in range(NH):
                for k, f in ((0, 0.25), (1, 0.5)):
                    src = wx_raw[:, d, h, RANK + NS * k:RANK + NS * k + NS]
                    src = src.rearrange("p (o n) -> p o n", o=1).to_broadcast([P, CPG, NS])
                    nc.scalar.mul(Wbc[:, d, h, k, :].rearrange("p (r n) -> p r n", n=NS), src, f) \
                        .then_inc(made["half_made"].sem, 1)

        def evacuate_x2(b):
            act.wait_ge(x2_turned.sem, x2_turned.at(b, 1))
            act.wait_ge(z_mm.sem, z_mm.at(b, 0))
            nc.scalar.activation(x2T[:, PAD:PAD + STEPS], W[:, :, :].rearrange("p a t -> p (a t)"),
                                 ACT.Copy).then_inc(x2T_ready.sem, 1)

        def conv(b, u, half):
            d, _ = unit_of(u)
            act.wait_ge(xp_mm.sem, xp_mm.at(b, NH * u + half + 1))
            nc.scalar.activation(W[:, half, :], W[:, half, :], ACT.Identity,
                                 bias=cbias[:, 2 * d + half:2 * d + half + 1]).then_inc(conv_ready.sem, 1)

        def tanh_x(b, u, half):
            act.wait_ge(conv_ready.sem, conv_ready.at(b, NH * u + half + 1))
            if u % 2 == 0:
                act.wait_ge(edge_done.sem, edge_done.at(b, NH * (u // 2) + half + 1))
            act.wait_ge(sz_ready.sem, sz_ready.at(b, u))
            nc.scalar.activation(th[:, half, :], W[:, half, :], ACT.Tanh, scale=0.5).then_inc(thx_ready.sem, 1)

        def gate_z(b, u, half):
            d, _ = unit_of(u)
            act.wait_ge(z_mm.sem, z_mm.at(b, NH * u + half + 1))
            at = d * 4 + 2 + half
            nc.scalar.activation(W[:, half, :], W[:, half, :], ACT.Identity, bias=bz[:, at:at + 1]) \
                .then_inc(z_ready.sem, 1)

        def tanh_z(b, u):
            act.wait_ge(z_ready.sem, z_ready.at(b, NH * (u + 1)))
            act.wait_ge(xp_ready.sem, xp_ready.at(b, NH * (u + 1)))
            nc.scalar.activation(th[:, :, :], W[:, :, :], ACT.Tanh, scale=0.5).then_inc(thz_ready.sem, 1)

        def take_dt(b, u):
            act.wait_ge(dt_mm.sem, dt_mm.at(b, u + 1))
            act.wait_ge(dp_mm.sem, dp_mm.at(b, NH * u))
            nc.scalar.activation(dtT[:, :], W[0:RANK, 0, :], ACT.Copy).then_inc(dt_ready.sem, 1)

        def take_b(b, u):
            act.wait_ge(b_mm.sem, b_mm.at(b, u + 1))
            act.wait_ge(dbx_ready.sem, dbx_ready.at(b, GROUPS * (u - 1)))
            nc.scalar.activation(Brep[:, u % 2, :], W[:, 0, :], ACT.Copy).then_inc(b_ready.sem, 1)

        def take_c(b, u):
            act.wait_ge(c_mm.sem, c_mm.at(b, u + 1))
            act.wait_ge(hc_ready.sem, hc_ready.at(b, GROUPS // 2 * (u - 1)))
            nc.scalar.activation(Crep[:, u % 2, :], W[:, 1, :], ACT.Copy).then_inc(c_ready.sem, 1)

        def absolute(b, u, half):
            d, _ = unit_of(u)
            bias = cols[:, C_BDT + 2 * d + half:C_BDT + 2 * d + half + 1]
            act.wait_ge(dp_mm.sem, dp_mm.at(b, NH * u + half + 1))
            act.wait_ge(resid_ready.sem, resid_ready.at(b, NH * u))
            nc.scalar.activation(ex[:, half, :], W[:, half, :], ACT.Abs, bias=bias).then_inc(abs_ready.sem, 1)
            act.wait_ge(sp_sum.sem, sp_sum.at(b, u))
            nc.scalar.activation(rl[:, half, :], W[:, half, :], ACT.Relu, bias=bias).then_inc(relu_ready.sem, 1)

        def softplus_exp(b, u):
            act.wait_ge(abs_ready.sem, abs_ready.at(b, NH * (u + 1)))
            nc.scalar.activation(ex[:, :, :], ex[:, :, :], ACT.Exp, scale=-1.0).then_inc(exp_ready.sem, 1)

        def softplus_one(b, u):
            act.wait_ge(exp_ready.sem, exp_ready.at(b, u + 1))
            act.wait_ge(delta_ready.sem, delta_ready.at(b, NH * u))
            nc.scalar.activation(w1p[:, :, :], ex[:, :, :], ACT.Identity, bias=ones[:, 0:1]).then_inc(onep_ready.sem, 1)

        def softplus_back(b, u):
            act.wait_ge(onep_ready.sem, onep_ready.at(b, u + 1))
            nc.scalar.activation(w1p[:, :, :], w1p[:, :, :], ACT.Identity, bias=ones[:, 1:2]).then_inc(back_ready.sem, 1)

        def softplus_ln(b, u):
            act.wait_ge(u_ready.sem, u_ready.at(b, NH * u))
            act.wait_ge(dlo_ready.sem, dlo_ready.at(b, NH * u))
            nc.scalar.activation(lg[:, :, :], ex[:, :, :], ACT.Ln, bias=ones[:, 0:1]).then_inc(ln_ready.sem, 1)

        def split_delta(b, u, half):
            act.wait_ge(delta_ready.sem, delta_ready.at(b, NH * u + half + 1))
            act.wait_ge(dstack_loaded[half].sem, dstack_loaded[half].at(b, STACK_DMAS * u))
            nc.scalar.activation(dhi[:, half, :], lg[:, half, :], ACT.Copy).then_inc(dhi_ready.sem, 1)

        def split_u(b, u, half):
            act.wait_ge(u_ready.sem, u_ready.at(b, NH * u + half + 1))
            act.wait_ge(ustack_loaded[half].sem, ustack_loaded[half].at(b, STACK_DMAS * u))
            nc.scalar.activation(uhi[:, half, :], u2[:, half, :], ACT.Copy).then_inc(uhi_ready.sem, 1)

        def decay(b, s):
            u, g = divmod(s, GROUPS)
            d, _ = unit_of(u)
            half, jj, *_ = group_of(g)
            at = d * GROUPS + half * GPH + jj
            k, _ = decay_buffer(s)
            act.wait_ge(drep_ready.sem, drep_ready.at(b, s + 1))
            nc.scalar.activation(D[:, k, :], D[:, k, :], ACT.Exp, scale=negA[:, at:at + 1]) \
                .then_inc(da_ready.sem, 1)

        def take_out(b, u):
            d, c = unit_of(u)
            act.wait_ge(out_mm.sem, out_mm.at(b, u + 1))
            if u < UNITS - 1:
                act.wait_ge(a4_ready.sem, a4_ready.at(b - 1, c + 1))
            nc.scalar.activation(fbT[:, d, CH * c:CH * c + CH], W[:, 1, :], ACT.Identity,
                                 bias=cols[:, C_BOUT + d:C_BOUT + d + 1]).then_inc(fb_ready.sem, 1)

        def gate(b, c):
            act.wait_ge(gate_mm.sem, gate_mm.at(b, c + 1))
            if c:
                act.wait_ge(gated_ready.sem, gated_ready.at(b, c))
            nc.scalar.activation(tg[:, :], W[:, 0, :], ACT.Tanh, bias=halfbg[:, 0:1], scale=0.5) \
                .then_inc(tg_ready.sem, 1)

        def take_sum(b, next_row):
            act.wait_ge(a4_turned.sem, a4_turned.at(b, 1))
            if next_row:
                act.wait_ge(x2_turned.sem, x2_turned.at(b + 2, 1))
            else:
                act.wait_ge(x3_ready.sem, x3_ready.at(b, 0))
            nc.scalar.activation(tok[:, :, :].rearrange("p t d -> p (t d)"), W[:, :, :].rearrange("p a t -> p (a t)"),
                                 ACT.Copy).then_inc(sum_copied.sem, 1)

        def row(b, next_row, last_end):
            for s in range(SLOTS):
                u, g = divmod(s, GROUPS)
                if s < SLOTS - 1:
                    decay(b, s + 1)
                elif next_row:
                    decay(b + 1, 0)
                nb, nu = (b, u + 1) if u < UNITS - 1 else (b + 1, 0)
                pb, pu = (b, u - 1) if u > 0 else (b - 1, UNITS - 1)
                prepares = u < UNITS - 1 or next_row
                if prepares:
                    if g == 3:
                        conv(nb, nu, 0)
                    if g == 4:
                        tanh_x(nb, nu, 0)
                    if g == 6:
                        conv(nb, nu, 1)
                    if g == 7:
                        tanh_x(nb, nu, 1)
                    if g == 10:
                        take_dt(nb, nu)
                    if g == 12:
                        absolute(nb, nu, 0)
                if g == 13 and (u > 0 or last_end):
                    take_out(pb, pu)
                if prepares:
                    if g == 15:
                        absolute(nb, nu, 1)
                        softplus_exp(nb, nu)
                    if g == 16:
                        softplus_one(nb, nu)
                        softplus_back(nb, nu)
                    if g == 17:
                        softplus_ln(nb, nu)
                    if g == 18:
                        take_b(nb, nu)
                    if g == 19:
                        take_c(nb, nu)
                    if g == 20:
                        split_delta(nb, nu, 0)
                    if g == 22:
                        split_u(nb, nu, 0)
                        gate_z(nb, nu, 0)
                    if g == 23:
                        gate_z(nb, nu, 1)
                    if g == 24:
                        tanh_z(nb, nu)
                        split_delta(nb, nu, 1)
                    if g == 26:
                        split_u(nb, nu, 1)
                if u < NCH and last_end and g == 28:
                    gate(b - 1, u)
                if u == 2 and next_row and g == 27:
                    evacuate_x2(b + 1)
                if u == 3 and last_end and g == 27:
                    take_sum(b - 1, next_row)

        evacuate_x2(0)
        act.wait_ge(made["prep_dve"].sem, PREP_DVE)
        for half in range(NH):
            conv(0, 0, half)
            tanh_x(0, 0, half)
        take_dt(0, 0)
        absolute(0, 0, 0)
        absolute(0, 0, 1)
        softplus_exp(0, 0)
        softplus_one(0, 0)
        softplus_back(0, 0)
        softplus_ln(0, 0)
        take_b(0, 0)
        take_c(0, 0)
        split_delta(0, 0, 0)
        split_u(0, 0, 0)
        gate_z(0, 0, 0)
        gate_z(0, 0, 1)
        tanh_z(0, 0)
        split_delta(0, 0, 1)
        split_u(0, 0, 1)
        decay(0, 0)
        row(0, True, False)
        with nc.scalar.Fori(1, ROWS - 1) as b:
            row(b, True, True)
        row(ROWS - 1, False, True)
        take_out(ROWS - 1, UNITS - 1)
        for c in range(NCH):
            gate(ROWS - 1, c)
        take_sum(ROWS - 1, False)

    @block.vector
    def _(dve):
        prep = made["prep_dve"].sem
        count = [0]

        def step(instruction):
            instruction.then_inc(prep, 1)
            count[0] += 1
            dve.wait_ge(prep, count[0])

        step(nc.vector.memset(ones[:, 0:1], 1.0))
        step(nc.vector.memset(ones[:, 1:2], -1.0))
        dve.wait_ge(made["masks_made"].sem, 4)
        step(nc.vector.tensor_copy(sel[:, :, :], sel_f))
        dve.wait_ge(made["cols_made"].sem, 1)
        dve.wait_ge(loaded.sem, LOADS)
        dve.wait_ge(made["bias_mm"].sem, 1)
        step(nc.vector.tensor_tensor(bz[:, :], W[:, 0, 128:136], cols[:, C_BIN:C_BIN + 8], ALU.add))
        for d in range(2):
            for h in range(NH):
                at = 2 * d + h
                bias = bz[:, 4 * d + h:4 * d + h + 1]
                for k in range(TAPS):
                    tap = taps[:, d, h, k:k + 1]
                    if k == 0:
                        step(nc.vector.tensor_tensor(psum4[:, 0, at:at + 1], tap, bias, ALU.mult))
                    else:
                        step(nc.vector.scalar_tensor_tensor(psum4[:, k, at:at + 1], tap, bias,
                                                            psum4[:, k - 1, at:at + 1], ALU.mult, ALU.add))
        step(nc.vector.tensor_tensor(cbias[:, :], psum4[:, 3, :], cols[:, C_CONVB:C_CONVB + 4], ALU.add))
        for t in range(3):
            step(nc.vector.tensor_scalar(edge[:, 0, t, :], psum4[:, 2 - t, 0:2], -1.0, None, ALU.mult))
            step(nc.vector.tensor_scalar(edge[:, 1, t, :], psum4[:, t, 2:4], -1.0, None, ALU.mult))
        for d in range(2):
            w = cols[:, C_LNW + d:C_LNW + d + 1]
            step(nc.vector.tensor_scalar(Wz[:, d, :], win_raw[:, d, DI:], w, None, ALU.mult))
            step(nc.vector.tensor_scalar(win_raw[:, d, :], win_raw[:, d, :], w, None, ALU.mult))
            for k in range(TAPS):
                step(nc.vector.tensor_tensor(Wk[:, d, k, :], win_raw[:, d, 0:DI], taps_b[:, d, :, k], ALU.mult))
        assert count[0] == PREP_DVE

        def stats_in(b):
            dve.wait_ge(x_loaded.sem, x_loaded.at(b, 16))
            dve.wait_ge(rstdA.sem, rstdA.at(b, 0))
            dve.wait_ge(x1_ready.sem, x1_ready.at(b, 0))
            dve.wait_ge(x2_ready.sem, x2_ready.at(b, 0))
            for t in range(TILES):
                nc.vector.bn_stats(stA[:, t, :], xn[:, t, :]).then_inc(statsA.sem, 1)
            dve.wait_ge(statsA.sem, statsA.at(b, TILES))
            dve.sem_inc(dve_ticks.sem, 1)
            for t in range(TILES):
                nc.vector.bn_aggr(mvA[:, t, :], stA[:, t, :]).then_inc(statsA.sem, 1)

        def make_x2(b):
            dve.wait_ge(rstdA.sem, rstdA.at(b, 7))
            dve.wait_ge(statsA.sem, statsA.at(b, 2 * TILES))
            for t in range(TILES):
                nc.vector.tensor_scalar(tok[:, t, :], xn[:, t, :], mvA[:, t, 0:1], rsA[:, 4, t:t + 1],
                                        ALU.subtract, ALU.mult).then_inc(x2_ready.sem, 1)

        def fix_edge(b, u, half):
            d, _ = unit_of(u)
            dve.wait_ge(conv_ready.sem, conv_ready.at(b, NH * u + half + 1))
            at = W[:, half, 0:3] if d == 0 else W[:, half, CH - 3:CH]
            nc.vector.tensor_tensor(at, at, edge[:, d, :, half], ALU.add).then_inc(edge_done.sem, 1)

        def silu_x(b, u, half):
            dve.wait_ge(thx_ready.sem, thx_ready.at(b, NH * u + half + 1))
            dve.wait_ge(c_mm.sem, c_mm.at(b, u - 1))
            dve.wait_ge(u_ready.sem, u_ready.at(b, NH * (u - 1)))
            dve.wait_ge(yd_ready.sem, yd_ready.at(b, NH * (u - 1)))
            nc.vector.scalar_tensor_tensor(xp2[:, u % 2, half, :], th[:, half, :], 1.0, W[:, half, :],
                                           ALU.add, ALU.mult).then_inc(xp_ready.sem, 1)

        def silu_z(b, u):
            dve.wait_ge(thz_ready.sem, thz_ready.at(b, u + 1))
            dve.wait_ge(yg_ready.sem, yg_ready.at(b, NH * (u - 1)))
            nc.vector.scalar_tensor_tensor(sz2[:, u % 2], th[:, :, :], 1.0, W[:, :, :], ALU.add, ALU.mult) \
                .then_inc(sz_ready.sem, 1)

        def softplus_sum(b, u):
            dve.wait_ge(ln_ready.sem, ln_ready.at(b, u + 1))
            dve.wait_ge(relu_ready.sem, relu_ready.at(b, NH * (u + 1)))
            nc.vector.tensor_tensor(lg[:, :, :], lg[:, :, :], rl[:, :, :], ALU.add).then_inc(sp_sum.sem, 1)

        def make_delta(b, u, half):
            dve.wait_ge(sp_sum.sem, sp_sum.at(b, u + 1))
            dve.wait_ge(resid_ready.sem, resid_ready.at(b, NH * u + half + 1))
            nc.vector.tensor_tensor(lg[:, half, :], lg[:, half, :], w1p[:, half, :], ALU.add) \
                .then_inc(delta_ready.sem, 1)

        def low_delta(b, u, half):
            dve.wait_ge(dhi_ready.sem, dhi_ready.at(b, NH * u + half + 1))
            dve.wait_ge(dstack_loaded[half].sem, dstack_loaded[half].at(b, STACK_DMAS * u))
            nc.vector.tensor_tensor(dlo[:, half, :], lg[:, half, :], dhi[:, half, :].bitcast(F32), ALU.subtract) \
                .then_inc(dlo_ready.sem, 1)

        def scan_input(b, s):
            u, g = divmod(s, GROUPS)
            dve.wait_ge(urep_ready.sem, urep_ready.at(b, s + 1))
            dve.wait_ge(h_ready.sem, h_ready.at(b, s + 1 - XRING))
            if g == 0:
                dve.wait_ge(b_ready.sem, b_ready.at(b, u + 1))
            nc.vector.tensor_tensor(dbx[:, s % XRING, :], U[:, s % 2, :], Brep[:, u % 2, :], ALU.mult) \
                .then_inc(dbx_ready.sem, 1)

        def scan(b, s):
            u, g = divmod(s, GROUPS)
            d, _ = unit_of(u)
            initial = 0.0
            if u % 2 == 1:
                at = d * GROUPS + g
                if g % 2 == 0:
                    dve.wait_ge(carry_saved.sem, carry_saved.at(b, at // 2 + 1))
                initial = carry[:, at:at + 1]
            dve.wait_ge(dbx_ready.sem, dbx_ready.at(b, s + 1))
            dve.wait_ge(da_ready.sem, da_ready.at(b, s + 1))
            dve.wait_ge(reduced.sem, reduced.at(b, (s - HRING) // 4 + 1))
            nc.vector.tensor_tensor_scan(directed(hs[:, s % HRING, :], d), directed(D[:, decay_buffer(s)[0], :], d),
                                         directed(dbx[:, s % XRING, :], d), initial, ALU.mult, ALU.add) \
                .then_inc(h_ready.sem, 1)

        def gate_y(b, u, half):
            d, _ = unit_of(u)
            k = NH * u + half + 1
            dve.wait_ge(reduced.sem, reduced.at(b, 4 * k))
            dve.wait_ge(out_mm.sem, out_mm.at(b, u))
            nc.vector.scalar_tensor_tensor(Y[:, :], xp2[:, u % 2, half, :], halfD[:, 2 * d + half:2 * d + half + 1],
                                           Y[:, :], ALU.mult, ALU.add).then_inc(yd_ready.sem, 1)
            dve.wait_ge(yd_ready.sem, yd_ready.at(b, k))
            nc.vector.tensor_tensor(yg[:, half, :], Y[:, :], sz2[:, u % 2, half, :], ALU.mult) \
                .then_inc(yg_ready.sem, 1)

        def gated_sum(b, c):
            V = W[:, 1, :]
            dve.wait_ge(value_mm.sem, value_mm.at(b, c + 1))
            dve.wait_ge(sfb_ready.sem, sfb_ready.at(b, c + 1))
            nc.vector.scalar_tensor_tensor(V, V, cols[:, C_BV:C_BV + 1], sfb[:, :], ALU.add, ALU.subtract) \
                .then_inc(diff_ready.sem, 1)
            dve.wait_ge(diff_ready.sem, diff_ready.at(b, c + 1))
            dve.wait_ge(tg_ready.sem, tg_ready.at(b, c + 1))
            nc.vector.scalar_tensor_tensor(V, tg[:, :], 1.0, V, ALU.add, ALU.mult).then_inc(gated_ready.sem, 1)
            dve.wait_ge(gated_ready.sem, gated_ready.at(b, c + 1))
            nc.vector.scalar_tensor_tensor(a4[:, CH * c:CH * c + CH], sfb[:, :], 2.0, V, ALU.mult, ALU.add) \
                .then_inc(a4_ready.sem, 1)

        def stats_gated(b):
            dve.wait_ge(sum_copied.sem, sum_copied.at(b, 2))
            for t in range(TILES):
                nc.vector.bn_stats(stG[:, t, :], tok[:, t, :]).then_inc(statsG.sem, 1)
            dve.wait_ge(statsG.sem, statsG.at(b, TILES))
            dve.sem_inc(dve_ticks.sem, 1)
            for t in range(TILES):
                nc.vector.bn_aggr(mvG[:, t, :], stG[:, t, :]).then_inc(statsG.sem, 1)

        def make_x3(b):
            dve.wait_ge(rstdG.sem, rstdG.at(b, 2))
            dve.wait_ge(statsG.sem, statsG.at(b, 2 * TILES))
            for t in range(TILES):
                nc.vector.tensor_scalar(tok[:, t, :], tok[:, t, :], mvG[:, t, 0:1], rsG[:, 1, t:t + 1],
                                        ALU.subtract, ALU.mult).then_inc(an_ready.sem, 1)
            dve.wait_ge(an_ready.sem, an_ready.at(b, TILES))
            dve.wait_ge(xres_loaded.sem, xres_loaded.at(b, 16))
            nc.vector.tensor_tensor(x3[:, :, :], tok[:, :, :], x3[:, :, :], ALU.add).then_inc(x3_ready.sem, 1)

        def row(b, next_row, last_end):
            for s in range(SLOTS):
                u, g = divmod(s, GROUPS)
                if s < SLOTS - 1:
                    scan_input(b, s + 1)
                elif next_row:
                    scan_input(b + 1, 0)
                scan(b, s)
                nb, nu = (b, u + 1) if u < UNITS - 1 else (b + 1, 0)
                if g == 5 and (u > 0 or last_end):
                    gate_y(*((b, u - 1) if u > 0 else (b - 1, UNITS - 1)), 1)
                if g == 21:
                    gate_y(b, u, 0)
                if u < UNITS - 1 or next_row:
                    if g in (3, 6) and nu % 2 == 0:
                        fix_edge(nb, nu, (g - 3) // 3)
                    if g == 5:
                        silu_x(nb, nu, 0)
                    if g == 8:
                        silu_x(nb, nu, 1)
                    if g == 19:
                        softplus_sum(nb, nu)
                    if g in (20, 22):
                        make_delta(nb, nu, (g - 20) // 2)
                    if g == 21:
                        low_delta(nb, nu, 0)
                    if g == 25:
                        silu_z(nb, nu)
                    if g == 26:
                        low_delta(nb, nu, 1)
                if u < NCH and last_end and g == 29:
                    gated_sum(b - 1, u)
                if u == 2 and next_row:
                    if g == 1:
                        stats_in(b + 1)
                    if g == 14:
                        make_x2(b + 1)
                if u == 3 and last_end:
                    if g == 28:
                        stats_gated(b - 1)
                    if g == 31:
                        make_x3(b - 1)

        stats_in(0)
        make_x2(0)
        for half in range(NH):
            fix_edge(0, 0, half)
            silu_x(0, 0, half)
        softplus_sum(0, 0)
        for half in range(NH):
            make_delta(0, 0, half)
            low_delta(0, 0, half)
        silu_z(0, 0)
        scan_input(0, 0)
        row(0, True, False)
        with nc.vector.Fori(1, ROWS - 1) as b:
            row(b, True, True)
        row(ROWS - 1, False, True)
        gate_y(ROWS - 1, UNITS - 1, 1)
        for c in range(NCH):
            gated_sum(ROWS - 1, c)
        stats_gated(ROWS - 1)
        make_x3(ROWS - 1)

    @block.tensor
    def _(pe):
        pe.wait_ge(made["ident_made"].sem, 1)
        pe.wait_ge(loaded.sem, LOADS)
        nc.tensor.transpose(W[:, 0, 0:124], rows[0:124, :], ident[0:124, 0:124]).then_inc(made["rows_T"].sem, 1)
        pe.wait_ge(made["cols_made"].sem, 1)
        for d in range(2):
            for m in range(4):
                last = nc.tensor.matmul(W[:, 0, 128 + 4 * d + m:129 + 4 * d + m], win_raw[:, d, P * m:P * m + P],
                                        cols[:, C_LNB + d:C_LNB + d + 1], start=True, stop=True)
        last.then_inc(made["bias_mm"].sem, 1)

        def turn(src, signal):
            for t in range(TILES):
                last = nc.tensor.transpose(W[:, t // 4, P * (t % 4):P * (t % 4) + P], src[:, t, :], ident[:, :])
            last.then_inc(signal.sem, 1)

        def turn_x2(b):
            pe.wait_ge(sz_ready.sem, sz_ready.at(b, 0))
            pe.wait_ge(x2_ready.sem, x2_ready.at(b, TILES))
            turn(tok, x2_turned)

        def product_x(b, u, half, k):
            d, c = unit_of(u)
            if k == 0:
                pe.wait_ge(x2T_ready.sem, x2T_ready.at(b, 1))
                pe.wait_ge(sz_ready.sem, sz_ready.at(b, u))
                if u == 1:
                    pe.wait_ge(sum_copied.sem, sum_copied.at(b, 0))
                elif u >= 2 and half == 0:
                    pe.wait_ge(tg_ready.sem, tg_ready.at(b - 1, u - 1))
                elif u >= 2:
                    pe.wait_ge(a4_ready.sem, a4_ready.at(b - 1, u - 1))
            at = CH * c + k if d == 0 else CH * c + 2 * PAD - k
            product = nc.tensor.matmul(W[:, half, :], Wk[:, d, k, P * half:P * half + P], x2T[:, at:at + CH],
                                       start=(k == 0), stop=(k == TAPS - 1))
            if k == TAPS - 1:
                product.then_inc(xp_mm.sem, 1)

        def product_z(b, u, half):
            d, c = unit_of(u)
            if half == 0:
                pe.wait_ge(b_ready.sem, b_ready.at(b, u + 1))
            else:
                pe.wait_ge(c_ready.sem, c_ready.at(b, u + 1))
            at = CH * c + PAD
            nc.tensor.matmul(W[:, half, :], Wz[:, d, P * half:P * half + P], x2T[:, at:at + CH],
                             start=True, stop=True).then_inc(z_mm.sem, 1)

        def product_dt(b, u, half):
            d, _ = unit_of(u)
            pe.wait_ge(xp_ready.sem, xp_ready.at(b, NH * u + half + 1))
            product = nc.tensor.matmul(W[0:RANK, 0, :], Wdtx[:, d, half, :], xp2[:, u % 2, half, :],
                                       start=(half == 0), stop=(half == NH - 1))
            if half == NH - 1:
                product.then_inc(dt_mm.sem, 1)

        def product_b(b, u, half):
            d, _ = unit_of(u)
            if half == 0:
                pe.wait_ge(abs_ready.sem, abs_ready.at(b, NH * u + 1))
                pe.wait_ge(relu_ready.sem, relu_ready.at(b, NH * u + 1))
            product = nc.tensor.matmul(W[:, 0, :], Wbc[:, d, half, 0, :], xp2[:, u % 2, half, :],
                                       start=(half == 0), stop=(half == NH - 1))
            if half == NH - 1:
                product.then_inc(b_mm.sem, 1)

        def product_c(b, u, half):
            d, _ = unit_of(u)
            if half == 0:
                pe.wait_ge(abs_ready.sem, abs_ready.at(b, NH * u + 2))
                pe.wait_ge(relu_ready.sem, relu_ready.at(b, NH * u + 2))
            product = nc.tensor.matmul(W[:, 1, :], Wbc[:, d, half, 1, :], xp2[:, u % 2, half, :],
                                       start=(half == 0), stop=(half == NH - 1))
            if half == NH - 1:
                product.then_inc(c_mm.sem, 1)

        def product_delta(b, u, half):
            d, _ = unit_of(u)
            pe.wait_ge(dt_ready.sem, dt_ready.at(b, u + 1))
            if half == 1:
                pe.wait_ge(fb_ready.sem, fb_ready.at(b, u - 1))
            nc.tensor.matmul(W[:, half, :], Wdt[:, d, P * half:P * half + P], dtT[:, :],
                             start=True, stop=True).then_inc(dp_mm.sem, 1)

        def replicate_delta(b, s):
            u, g = divmod(s, GROUPS)
            _, _, k, q, _, _ = group_of(g)
            to, before = decay_buffer(s)
            if g % GPH == 0:
                loads = dstack_loaded[g // GPH]
                pe.wait_ge(loads.sem, loads.at(b, STACK_DMAS * (u + 1)))
            pe.wait_ge(h_ready.sem, h_ready.at(b, before + 1))
            nc.tensor.matmul(D[:, to, :], sel[:, k, :], stackD[:, q, :], start=True, stop=True) \
                .then_inc(drep_ready.sem, 1)

        def replicate_u(b, s):
            u, g = divmod(s, GROUPS)
            _, _, k, q, _, _ = group_of(g)
            if g % GPH == 0:
                loads = ustack_loaded[g // GPH]
                pe.wait_ge(loads.sem, loads.at(b, STACK_DMAS * (u + 1)))
            pe.wait_ge(dbx_ready.sem, dbx_ready.at(b, s - 1))
            nc.tensor.matmul(U[:, s % 2, :], sel[:, k, :], stackU[:, q, :], start=True, stop=True) \
                .then_inc(urep_ready.sem, 1)

        def reduce(b, m):
            for s in range(4 * m, 4 * m + 4):
                g = s % GROUPS
                _, _, _, _, tile, r = group_of(g)
                if s == 4 * m and m % 4 == 0:
                    pe.wait_ge(yg_ready.sem, yg_ready.at(b, m // 4))
                if s % 2 == 0:
                    pe.wait_ge(hc_ready.sem, hc_ready.at(b, s // 2 + 1))
                last = nc.tensor.matmul(Y[32 * tile:32 * tile + 32, :], red[:, r, :], hs[:, s % HRING, :],
                                        start=(r == 0), stop=(r == 3))
            last.then_inc(reduced.sem, 1)

        def product_out(b, u, part):
            d, c = unit_of(u)
            if part < NH:
                if part == 0:
                    pe.wait_ge(yg_ready.sem, yg_ready.at(b, NH * (u + 1)))
                nc.tensor.matmul(W[:, 1, :], Wo[:, d, part, :], yg[:, part, :], start=(part == 0), stop=False,
                                 skip_group_check=True)
                return
            pe.wait_ge(x1_ready.sem, x1_ready.at(b, TILES))
            for i in range(CH // P):
                last = nc.tensor.matmul(W[:, 1, P * i:P * i + P], xt[:, CH // P * c + i, :], ident[:, :],
                                        start=False, stop=(i == CH // P - 1), skip_group_check=True)
            last.then_inc(out_mm.sem, 1)

        def products_gated(b, c, k):
            if k == 0:
                pe.wait_ge(fb_ready.sem, fb_ready.at(b, UNITS))
            cut = slice(CH * c, CH * c + CH)
            weights, signal = ((Wgs, gate_mm), (Wvs, value_mm))[k]
            for d in range(2):
                last = nc.tensor.matmul(W[:, k, :], weights[:, d, :], fbT[:, d, cut], start=(d == 0), stop=(d == 1))
            last.then_inc(signal.sem, 1)

        def turn_sum(b):
            pe.wait_ge(a4_ready.sem, a4_ready.at(b, NCH))
            turn(a4[:, :].rearrange("p (t d) -> p t d", d=DM), a4_turned)

        def row(b, next_row, last_end):
            for s in range(SLOTS):
                u, g = divmod(s, GROUPS)
                if s + 2 < SLOTS:
                    replicate_u(b, s + 2)
                    replicate_delta(b, s + 2)
                elif next_row:
                    replicate_u(b + 1, s + 2 - SLOTS)
                    replicate_delta(b + 1, s + 2 - SLOTS)
                if (s - LAG) % 4 == 3:
                    if s - LAG >= 3:
                        reduce(b, (s - LAG) // 4)
                    elif last_end:
                        reduce(b - 1, SLOTS // 4 + (s - LAG) // 4)
                nb, nu = (b, u + 1) if u < UNITS - 1 else (b + 1, 0)
                prepares = u < UNITS - 1 or next_row
                if prepares:
                    for k in {0: (0,), 1: (1, 2), 2: (3,), 3: (4,), 4: (5, 6), 5: (7,)}.get(g, ()):
                        product_x(nb, nu, k // TAPS, k % TAPS)
                    if g == 7:
                        product_dt(nb, nu, 0)
                    if g == 9:
                        product_dt(nb, nu, 1)
                if g in (10, 11, 12) and (u > 0 or last_end):
                    if g == 10 and not prepares:
                        pe.wait_ge(sz_ready.sem, sz_ready.at(b + 1, 0))
                    product_out(*((b, u - 1) if u > 0 else (b - 1, UNITS - 1)), g - 10)
                if prepares:
                    if g == 11:
                        product_delta(nb, nu, 0)
                    if g == 14:
                        product_delta(nb, nu, 1)
                    if g in (15, 16):
                        product_b(nb, nu, g - 15)
                    if g in (17, 18):
                        product_c(nb, nu, g - 17)
                    if g in (20, 21):
                        product_z(nb, nu, g - 20)
                if u < NCH and last_end and g in (26, 27):
                    if g == 26:
                        pe.wait_ge(sz_ready.sem, sz_ready.at(nb, nu + 1))
                    products_gated(b - 1, u, g - 26)
                if u == 2 and next_row and g == 26:
                    turn_x2(b + 1)
                if u == 3 and last_end and g == 26:
                    if prepares:
                        pe.wait_ge(sz_ready.sem, sz_ready.at(nb, nu + 1))
                    else:
                        pe.wait_ge(fb_ready.sem, fb_ready.at(b, UNITS - 1))
                    turn_sum(b - 1)

        turn_x2(0)
        pe.wait_ge(made["prep_dve"].sem, PREP_DVE)
        pe.wait_ge(made["half_made"].sem, 12)
        for half in range(NH):
            for k in range(TAPS):
                product_x(0, 0, half, k)
        for half in range(NH):
            product_dt(0, 0, half)
        for half in range(NH):
            product_delta(0, 0, half)
        for half in range(NH):
            product_b(0, 0, half)
        for half in range(NH):
            product_c(0, 0, half)
        for half in range(NH):
            product_z(0, 0, half)
        for s in range(2):
            replicate_u(0, s)
            replicate_delta(0, s)
        row(0, True, False)
        with nc.tensor.Fori(1, ROWS - 1) as b:
            row(b, True, True)
        row(ROWS - 1, False, True)
        reduce(ROWS - 1, SLOTS // 4 - 1)
        pe.wait_ge(sum_copied.sem, sum_copied.at(ROWS, 0))
        for part in range(NH + 1):
            product_out(ROWS - 1, UNITS - 1, part)
        for c in range(NCH):
            if c:
                pe.wait_ge(tg_ready.sem, tg_ready.at(ROWS - 1, c))
                pe.wait_ge(a4_ready.sem, a4_ready.at(ROWS - 1, c))
            for k in range(2):
                products_gated(ROWS - 1, c, k)
        turn_sum(ROWS - 1)


def experts(nc, ctx, ident, cols, mhalf, router_w, w1, w2, b2, gamma, beta, x3_dram, out):
    def sb(name, shape, dt=F32):
        return ctx.enter_context(nc.sbuf_tensor(name, shape, dt))

    def sig(name, per):
        return Signal(ctx, nc, name, per)

    W1 = sb("W1", [P, NE, FF])
    W2 = sb("W2", [P, NE, FT, DM])
    w2mean = sb("w2mean", [P, NE, FT])
    gam = sb("gam", [P, NE, DM])
    router = sb("router", [P, NE])
    betad = sb("betad", [TT * NE, TT, DM])
    b2row = sb("b2row", [1, NE, DM])
    b2mean = sb("b2mean", [1, NE])
    ones1 = sb("ones1", [1, P])
    iota_i = sb("iota_i", [P, TT, NE], mybir.dt.int32)
    iota = sb("iota", [P, TT, NE])
    x3 = sb("x3c", [P, 2, TT, DM])
    xln = sb("xln", [P, 2, TT, DM])
    xlnT = sb("xlnT", [P, 2, TC])
    st = sb("st", [P, TT, 6])
    mv = sb("mv", [P, TT, 2])
    rs = sb("rs", [P, 2, TT])
    logits = sb("logits", [P, TT, NE])
    top = sb("top", [P, TT, 8])
    topi = sb("topi", [P, TT, 8], U32)
    topf = sb("topf", [P, TT, 2])
    gap = sb("gap", [P, TT])
    gw = sb("gw", [P, 2, TT])
    pick = sb("pick", [P, 2, TT, NE])
    gates = sb("gates", [P, 2, TT, NE])
    gT = sb("gT", [TT * NE, P])
    acc = sb("acc", [P, 2, TT, DM])
    hT = sb("hT", [P, 4, TC])
    sq = sb("sq", [P, 2, TT, DM])
    ssq = sb("ssq", [P, 2, TT])
    es = sb("es", [P, 2, 3, TT])
    wexp = sb("wexp", [P, 2, TT, DM])
    st2 = sb("st2", [P, TT, 6])
    mv2 = sb("mv2", [P, TT, 2])
    rs2 = sb("rs2", [P, 2, TT])

    Hb = ctx.enter_context(nc.psum_tensor("Hb", [P, 4, TC], F32))
    Ob = ctx.enter_context(nc.psum_tensor("Ob", [P, 2, TT, DM], F32))
    Ta = ctx.enter_context(nc.psum_tensor("Ta", [P, TC], F32))
    Tb = ctx.enter_context(nc.psum_tensor("Tb", [P, TC], F32))

    SMALL = (2 + TT) * 16
    JT = NE * FT
    sp_ticks, pool_ticks, dve_ticks = (sig(n, 0) for n in ("sp_ticks2", "pool_ticks2", "dve_ticks2"))
    small_loaded = sig("small_loaded", 0)
    w1_loaded = [sig(f"w1_{e}_loaded", 0) for e in range(NE)]
    w2_loaded = [sig(f"w2_{e}_loaded", 0) for e in range(NE)]
    b2_loaded = sig("b2_loaded", 0)
    w2_summed = sig("w2_summed", 0)
    w2_centred = sig("w2_centred", 0)
    b2_step = sig("b2_step", 0)
    beta_zero = sig("beta_zero", 0)
    const2 = sig("const2", 0)
    x3c_loaded = [sig(f"x3c_loaded{p}", 8) for p in range(2)]
    stats_done = sig("stats_done", 2 * TT)
    rstd_done = sig("rstd_done", 2)
    xln_ready = sig("xln_ready", TT)
    xln_turned = sig("xln_turned", 1)
    xlnT_ready = sig("xlnT_ready", 1)
    logits_mm = sig("logits_mm", 1)
    logits_ready = sig("logits_ready", 1)
    top_ready = sig("top_ready", TT)
    topi_ready = sig("topi_ready", TT)
    topf_ready = sig("topf_ready", 1)
    gap_ready = sig("gap_ready", 1)
    gtanh_ready = sig("gtanh_ready", 1)
    gw_ready = sig("gw_ready", 2)
    pick_step = sig("pick_step", 4)
    gates_ready = sig("gates_ready", 1)
    gates_turned = sig("gates_turned", 1)
    gT_ready = sig("gT_ready", 1)
    beta_mm = sig("beta_mm", 1)
    acc_ready = sig("acc_ready", 1)
    h_mm = sig("h_mm", JT)
    gelu_ready = sig("gelu_ready", JT)
    o_mm = sig("o_mm", JT)
    res_ready = sig("res_ready", NE)
    ssq_ready = sig("ssq_ready", NE * TT)
    evar_ready = sig("evar_ready", NE)
    erstd_ready = sig("erstd_ready", NE)
    escale_ready = sig("escale_ready", NE)
    wexp_ready = sig("wexp_ready", NE * TT)
    acc_added = sig("acc_added", NE)
    stats2_done = sig("stats2_done", 2 * TT)
    rstd2_done = sig("rstd2_done", 2)
    y_ready = sig("y_ready", TT)
    final_ready = sig("final_ready", 1)
    stored = [sig(f"stored{p}", 8) for p in range(2)]

    x3_v = x3_dram.rearrange("(c t p) d -> c p t d", t=TT, p=P)
    out_v = out.rearrange("r s d -> (r s) d").rearrange("(c t p) d -> c p t d", t=TT, p=P)

    def at(view, c):
        return view[c] if isinstance(c, int) else view[bass.ds(c, 1), :, :, :].rearrange("o p t d -> (o p) t d")

    def chunks(eng, prepare, body):
        prepare(0, 0)
        body(0, 0, True, False)
        body(1, 1, True, True)
        with eng.Fori(1, NTC // 2 - 1) as pair:
            body(pair * 2, 0, True, True)
            body(pair * 2 + 1, 1, True, True)
        body(NTC - 2, 0, True, True)
        body(NTC - 1, 1, False, True)

    block = ctx.enter_context(nc.Block())

    @block.sync
    def _(sp):
        sp.dma_start(x3[:, 0], x3_v[0]).then_inc(x3c_loaded[0].sem, 16)
        sp.dma_start(router[:, :], router_w).then_inc(small_loaded.sem, 16)
        sp.dma_start(b2row[:, :, :], b2.rearrange("(o e) d -> o e d", o=1)).then_inc(b2_loaded.sem, 16)
        sp.dma_start(W1[:, 0, :], w1[0]).then_inc(w1_loaded[0].sem, 16)
        sp.dma_start(W2[:, 0], w2[0].rearrange("(f p) d -> p f d", p=P)).then_inc(w2_loaded[0].sem, 16)
        sp.dma_start(gam[:, :, :].rearrange("p e d -> p (e d)"),
                     gamma.rearrange("(o e) d -> o (e d)", o=1).to_broadcast([P, NE * DM])) \
            .then_inc(small_loaded.sem, 16)
        sp.wait_ge(beta_zero.sem, 1)
        for t in range(TT):
            sp.dma_start(betad[NE * t:NE * t + NE, t, :], beta).then_inc(small_loaded.sem, 16)
        for e in range(1, NE):
            sp.dma_start(W1[:, e, :], w1[e]).then_inc(w1_loaded[e].sem, 16)
            sp.dma_start(W2[:, e], w2[e].rearrange("(f p) d -> p f d", p=P)).then_inc(w2_loaded[e].sem, 16)

        def load_x3(c, p):
            sp.wait_ge(final_ready.sem, final_ready.at(c, -1))
            sp.sem_inc(sp_ticks.sem, 1)
            sp.dma_start(x3[:, p], at(x3_v, c)).then_inc(x3c_loaded[p].sem, 16)

        def store(c, p):
            sp.wait_ge(final_ready.sem, final_ready.at(c, 1))
            sp.sem_inc(sp_ticks.sem, 1)
            sp.dma_start(at(out_v, c), acc[:, p]).then_inc(stored[p].sem, 16)

        def body(c, p, has_next, has_last):
            if has_next:
                load_x3(c + 1, 1 - p)
            if has_last:
                store(c - 1, 1 - p)

        chunks(nc.sync, lambda c, p: None, body)
        store(NTC - 1, 1)
        for p in range(2):
            sp.wait_ge(stored[p].sem, stored[p].at(NTC, 0))

    @block.gpsimd
    def _(pool):
        nc.gpsimd.memset(betad[:, :, :], 0.0).then_inc(beta_zero.sem, 1)
        nc.gpsimd.memset(ones1[:, :], 1.0).then_inc(const2.sem, 1)
        nc.gpsimd.iota(iota_i[:, :, :], pattern=[[0, TT], [1, NE]], base=0, channel_multiplier=0) \
            .then_inc(const2.sem, 1)

        def rstd(var, ve, r, scale, eps, done, c):
            nc.gpsimd.tensor_scalar(ve, var, scale, eps, ALU.mult, ALU.add).then_inc(done.sem, 1)
            pool.wait_ge(done.sem, done.at(c, 1))
            nc.gpsimd.tensor_tensor(r, ve, mhalf[:, 0:TT], ALU.pow).then_inc(done.sem, 1)

        def prepare(c, p):
            pool.wait_ge(stats_done.sem, stats_done.at(c, 2 * TT))
            pool.sem_inc(pool_ticks.sem, 1)
            rstd(mv[:, :, 1], rs[:, 0, :], rs[:, 1, :], 1.0, EPS_IN, rstd_done, c)

        def body(c, p, has_next, has_last):
            for e in range(NE):
                q = e % 2
                pool.wait_ge(ssq_ready.sem, ssq_ready.at(c, TT * (e + 1)))
                pool.sem_inc(pool_ticks.sem, 1)
                nc.gpsimd.tensor_scalar(es[:, q, 0, :], ssq[:, q, :], 1.0 / DM, EPS_OUT, ALU.mult, ALU.add) \
                    .then_inc(evar_ready.sem, 1)
                pool.wait_ge(evar_ready.sem, evar_ready.at(c, e + 1))
                pool.wait_ge(escale_ready.sem, escale_ready.at(c, e - 1))
                nc.gpsimd.tensor_tensor(es[:, q, 1, :], es[:, q, 0, :], mhalf[:, 0:TT], ALU.pow) \
                    .then_inc(erstd_ready.sem, 1)
                pool.wait_ge(wexp_ready.sem, wexp_ready.at(c, TT * (e + 1)))
                if e == 0:
                    pool.wait_ge(acc_ready.sem, acc_ready.at(c, 1))
                pool.wait_ge(acc_added.sem, acc_added.at(c, e))
                nc.gpsimd.tensor_tensor(acc[:, p], acc[:, p], wexp[:, q], ALU.add).then_inc(acc_added.sem, 1)
                if e == 0 and has_last:
                    pool.wait_ge(stats2_done.sem, stats2_done.at(c - 1, 2 * TT))
                    pool.sem_inc(pool_ticks.sem, 1)
                    rstd(mv2[:, :, 1], rs2[:, 0, :], rs2[:, 1, :], 1.0, EPS_IN, rstd2_done, c - 1)
                if e == 2 and has_next:
                    prepare(c + 1, 1 - p)

        chunks(nc.gpsimd, prepare, body)
        pool.wait_ge(stats2_done.sem, stats2_done.at(NTC - 1, 2 * TT))
        rstd(mv2[:, :, 1], rs2[:, 0, :], rs2[:, 1, :], 1.0, EPS_IN, rstd2_done, NTC - 1)

    @block.scalar
    def _(act):
        def take_xlnT(c, p):
            act.wait_ge(xln_turned.sem, xln_turned.at(c, 1))
            act.wait_ge(h_mm.sem, h_mm.at(c, -JT))
            nc.scalar.activation(xlnT[:, p, :], Ta[:, :], ACT.Copy).then_inc(xlnT_ready.sem, 1)

        def gate_tanh(c, p):
            act.wait_ge(gap_ready.sem, gap_ready.at(c, 1))
            nc.scalar.activation(gap[:, :], gap[:, :], ACT.Tanh, scale=0.5).then_inc(gtanh_ready.sem, 1)

        def take_gT(c, p):
            act.wait_ge(gates_turned.sem, gates_turned.at(c, 1))
            act.wait_ge(beta_mm.sem, beta_mm.at(c, 0))
            nc.scalar.activation(gT[:, :], Tb[0:TT * NE, 128:256], ACT.Copy).then_inc(gT_ready.sem, 1)

        def take_beta(c, p):
            act.wait_ge(beta_mm.sem, beta_mm.at(c, 1))
            act.wait_ge(stored[p].sem, stored[p].at(c, -8 * p))
            nc.scalar.activation(acc[:, p].rearrange("p t d -> p (t d)"), Ta[:, :], ACT.Copy) \
                .then_inc(acc_ready.sem, 1)

        def prepare(c, p):
            take_xlnT(c, p)
            gate_tanh(c, p)
            take_gT(c, p)
            take_beta(c, p)

        def gelu(c, t):
            act.wait_ge(h_mm.sem, h_mm.at(c, t + 1))
            act.wait_ge(o_mm.sem, o_mm.at(c, t + 1 - 4))
            e, f = divmod(t, FT)
            at = C_B1 + FT * e + f
            nc.scalar.activation(hT[:, t % 4, :], Hb[:, t % 4, :], ACT.Gelu, bias=cols[:, at:at + 1]) \
                .then_inc(gelu_ready.sem, 1)

        def squares(c, e):
            q = e % 2
            act.wait_ge(res_ready.sem, res_ready.at(c, e + 1))
            act.wait_ge(evar_ready.sem, evar_ready.at(c, e - 1))
            act.wait_ge(ssq_ready.sem, ssq_ready.at(c, TT * (e - 1)))
            for i in range(TT):
                nc.scalar.activation(sq[:, q, i, :], Ob[:, q, i, :], ACT.Square, accum_out=ssq[:, q, i:i + 1]) \
                    .then_inc(ssq_ready.sem, 1)

        def body(c, p, has_next, has_last):
            for t in range(JT):
                e, f = divmod(t, FT)
                gelu(c, t)
                if f == 2 and e > 0:
                    squares(c, e - 1)
                if has_next:
                    if t == 18:
                        take_xlnT(c + 1, 1 - p)
                    if t == 26:
                        gate_tanh(c + 1, 1 - p)
                    if t == 29:
                        take_gT(c + 1, 1 - p)
                    if t == 31:
                        take_beta(c + 1, 1 - p)
            squares(c, NE - 1)

        chunks(nc.scalar, prepare, body)

    @block.vector
    def _(dve):
        dve.wait_ge(const2.sem, 2)
        nc.vector.tensor_copy(iota[:, :, :], iota_i[:, :, :]).then_inc(b2_step.sem, 1)
        dve.wait_ge(b2_loaded.sem, 16)
        nc.vector.reduce_sum(b2mean[:, :], b2row[:, :, :], axis=mybir.AxisListType.X).then_inc(b2_step.sem, 1)
        dve.wait_ge(b2_step.sem, 2)
        nc.vector.tensor_scalar(b2mean[:, :], b2mean[:, :], 1.0 / DM, None, ALU.mult).then_inc(b2_step.sem, 1)
        dve.wait_ge(b2_step.sem, 3)
        nc.vector.tensor_tensor(b2row[:, :, :], b2row[:, :, :],
                                b2mean[:, :].rearrange("p (e o) -> p e o", o=1).to_broadcast([1, NE, DM]),
                                ALU.subtract).then_inc(b2_step.sem, 1)

        def centre(e):
            dve.wait_ge(w2_loaded[e].sem, 16)
            m = w2mean[:, e, :]
            nc.vector.reduce_sum(m, W2[:, e], axis=mybir.AxisListType.X).then_inc(w2_summed.sem, 1)
            dve.wait_ge(w2_summed.sem, 2 * e + 1)
            nc.vector.tensor_scalar(m, m, 1.0 / DM, None, ALU.mult).then_inc(w2_summed.sem, 1)
            dve.wait_ge(w2_summed.sem, 2 * e + 2)
            nc.vector.tensor_tensor(W2[:, e], W2[:, e],
                                    m.rearrange("p (f o) -> p f o", o=1).to_broadcast([P, FT, DM]),
                                    ALU.subtract).then_inc(w2_centred.sem, 1)

        def norm(c, p):
            dve.wait_ge(x3c_loaded[p].sem, x3c_loaded[p].at(c, 16 - 8 * p))
            dve.wait_ge(rstd_done.sem, rstd_done.at(c, 0))
            dve.wait_ge(xln_ready.sem, xln_ready.at(c, 0))
            for t in range(TT):
                nc.vector.bn_stats(st[:, t, :], x3[:, p, t, :]).then_inc(stats_done.sem, 1)
            dve.wait_ge(stats_done.sem, stats_done.at(c, TT))
            dve.sem_inc(dve_ticks.sem, 1)
            for t in range(TT):
                nc.vector.bn_aggr(mv[:, t, :], st[:, t, :]).then_inc(stats_done.sem, 1)

        def make_xln(c, p):
            dve.wait_ge(rstd_done.sem, rstd_done.at(c, 2))
            dve.wait_ge(stats_done.sem, stats_done.at(c, 2 * TT))
            dve.wait_ge(res_ready.sem, res_ready.at(c, -NE))
            for t in range(TT):
                nc.vector.tensor_scalar(xln[:, p, t, :], x3[:, p, t, :], mv[:, t, 0:1], rs[:, 1, t:t + 1],
                                        ALU.subtract, ALU.mult).then_inc(xln_ready.sem, 1)

        def top2(c, p):
            dve.wait_ge(logits_mm.sem, logits_mm.at(c, 1))
            dve.wait_ge(topi_ready.sem, topi_ready.at(c, 0))
            nc.vector.tensor_copy(logits[:, :, :].rearrange("p t e -> p (t e)"), Tb[:, 0:TT * NE]) \
                .then_inc(logits_ready.sem, 1)
            dve.wait_ge(logits_ready.sem, logits_ready.at(c, 1))
            dve.sem_inc(dve_ticks.sem, 1)
            for t in range(TT):
                nc.vector.max(top[:, t, :], logits[:, t, :]).then_inc(top_ready.sem, 1)
            dve.wait_ge(top_ready.sem, top_ready.at(c, TT))
            dve.sem_inc(dve_ticks.sem, 1)
            for t in range(TT):
                nc.vector.max_index(topi[:, t, :], top[:, t, :], logits[:, t, :]).then_inc(topi_ready.sem, 1)
            dve.wait_ge(gw_ready.sem, gw_ready.at(c, 0))
            nc.vector.tensor_tensor(gap[:, :], top[:, :, 0], top[:, :, 1], ALU.subtract).then_inc(gap_ready.sem, 1)
            dve.wait_ge(topi_ready.sem, topi_ready.at(c, TT))
            dve.wait_ge(gates_ready.sem, gates_ready.at(c, 0))
            nc.vector.tensor_copy(topf[:, :, :], topi[:, :, 0:2]).then_inc(topf_ready.sem, 1)
            dve.wait_ge(topf_ready.sem, topf_ready.at(c, 1))
            for k in range(2):
                nc.vector.tensor_tensor(pick[:, k], iota[:, :, :],
                                        topf[:, :, k:k + 1].to_broadcast([P, TT, NE]), ALU.is_equal) \
                    .then_inc(pick_step.sem, 1)

        def make_gates(c, p):
            dve.wait_ge(gtanh_ready.sem, gtanh_ready.at(c, 1))
            nc.vector.tensor_scalar(gw[:, 0, :], gap[:, :], 0.5, 0.5, ALU.mult, ALU.add).then_inc(gw_ready.sem, 1)
            nc.vector.tensor_scalar(gw[:, 1, :], gap[:, :], -0.5, 0.5, ALU.mult, ALU.add).then_inc(gw_ready.sem, 1)
            dve.wait_ge(gw_ready.sem, gw_ready.at(c, 2))
            dve.wait_ge(pick_step.sem, pick_step.at(c, 2))
            for k in range(2):
                nc.vector.tensor_tensor(pick[:, k], pick[:, k],
                                        gw[:, k, :].rearrange("p (t o) -> p t o", o=1).to_broadcast([P, TT, NE]),
                                        ALU.mult).then_inc(pick_step.sem, 1)
            dve.wait_ge(pick_step.sem, pick_step.at(c, 4))
            dve.wait_ge(escale_ready.sem, escale_ready.at(c, -NE))
            dve.wait_ge(gates_turned.sem, gates_turned.at(c, -1))
            nc.vector.tensor_tensor(gates[:, p], pick[:, 0], pick[:, 1], ALU.add).then_inc(gates_ready.sem, 1)

        def add_residual(c, e, p):
            q = e % 2
            dve.wait_ge(o_mm.sem, o_mm.at(c, FT * (e + 1)))
            nc.vector.tensor_tensor(Ob[:, q], Ob[:, q], xln[:, p], ALU.add).then_inc(res_ready.sem, 1)

        def scale(c, e, p):
            q = e % 2
            dve.wait_ge(erstd_ready.sem, erstd_ready.at(c, e + 1))
            if e == 0:
                dve.wait_ge(gates_ready.sem, gates_ready.at(c, 1))
            nc.vector.tensor_tensor(es[:, q, 2, :], es[:, q, 1, :], gates[:, p, :, e], ALU.mult) \
                .then_inc(escale_ready.sem, 1)
            dve.wait_ge(escale_ready.sem, escale_ready.at(c, e + 1))
            dve.wait_ge(acc_added.sem, acc_added.at(c, e - 1))
            for t in range(TT):
                nc.vector.scalar_tensor_tensor(wexp[:, q, t, :], Ob[:, q, t, :], es[:, q, 2, t:t + 1],
                                               gam[:, e, :], ALU.mult, ALU.mult).then_inc(wexp_ready.sem, 1)

        def stats_last(c, p):
            dve.wait_ge(acc_added.sem, acc_added.at(c, NE))
            dve.wait_ge(rstd2_done.sem, rstd2_done.at(c, 0))
            dve.wait_ge(y_ready.sem, y_ready.at(c, 0))
            for t in range(TT):
                nc.vector.bn_stats(st2[:, t, :], acc[:, p, t, :]).then_inc(stats2_done.sem, 1)
            dve.wait_ge(stats2_done.sem, stats2_done.at(c, TT))
            dve.sem_inc(dve_ticks.sem, 1)
            for t in range(TT):
                nc.vector.bn_aggr(mv2[:, t, :], st2[:, t, :]).then_inc(stats2_done.sem, 1)

        def finish(c, p):
            dve.wait_ge(rstd2_done.sem, rstd2_done.at(c, 2))
            dve.wait_ge(stats2_done.sem, stats2_done.at(c, 2 * TT))
            for t in range(TT):
                nc.vector.tensor_scalar(acc[:, p, t, :], acc[:, p, t, :], mv2[:, t, 0:1], rs2[:, 1, t:t + 1],
                                        ALU.subtract, ALU.mult).then_inc(y_ready.sem, 1)
            dve.wait_ge(y_ready.sem, y_ready.at(c, TT))
            nc.vector.tensor_tensor(acc[:, p], acc[:, p], x3[:, p], ALU.add).then_inc(final_ready.sem, 1)

        def prepare(c, p):
            norm(c, p)
            make_xln(c, p)
            centre(0)
            top2(c, p)
            make_gates(c, p)

        def body(c, p, has_next, has_last):
            for e in range(NE):
                if isinstance(c, int) and c == 0 and e < NE - 1:
                    if e == 0:
                        centre(1)
                    if e + 2 < NE:
                        centre(e + 2)
                add_residual(c, e, p)
                if e > 0:
                    scale(c, e - 1, p)
                if e == 0 and has_last:
                    scale(c - 1, NE - 1, 1 - p)
                    stats_last(c - 1, 1 - p)
                if e == 1 and has_last:
                    finish(c - 1, 1 - p)
                if has_next:
                    if e == 2:
                        norm(c + 1, 1 - p)
                    if e == 3:
                        make_xln(c + 1, 1 - p)
                    if e == 5:
                        top2(c + 1, 1 - p)
                    if e == 6:
                        make_gates(c + 1, 1 - p)

        chunks(nc.vector, prepare, body)
        scale(NTC - 1, NE - 1, 1)
        stats_last(NTC - 1, 1)
        finish(NTC - 1, 1)

    @block.tensor
    def _(pe):
        def turn_xln(c, p):
            pe.wait_ge(xln_ready.sem, xln_ready.at(c, TT))
            pe.wait_ge(acc_ready.sem, acc_ready.at(c, 0))
            for t in range(TT):
                last = nc.tensor.transpose(Ta[:, P * t:P * t + P], xln[:, p, t, :], ident[:, :])
            last.then_inc(xln_turned.sem, 1)

        def route(c, p):
            pe.wait_ge(xlnT_ready.sem, xlnT_ready.at(c, 1))
            pe.wait_ge(gT_ready.sem, gT_ready.at(c, 0))
            for t in range(TT):
                last = nc.tensor.matmul(Tb[:, NE * t:NE * t + NE], xlnT[:, p, P * t:P * t + P], router[:, :],
                                        start=True, stop=True)
            last.then_inc(logits_mm.sem, 1)

        def turn_gates(c, p):
            pe.wait_ge(gates_ready.sem, gates_ready.at(c, 1))
            nc.tensor.transpose(Tb[0:TT * NE, 128:256], gates[:, p].rearrange("p t e -> p (t e)"), ident[:, :]) \
                .then_inc(gates_turned.sem, 1)

        def add_beta(c, p):
            pe.wait_ge(gT_ready.sem, gT_ready.at(c, 1))
            nc.tensor.matmul(Ta[:, :], gT[:, :], betad[:, :, :].rearrange("k t d -> k (t d)"),
                             start=True, stop=True).then_inc(beta_mm.sem, 1)

        def prepare(c, p):
            turn_xln(c, p)
            pe.wait_ge(small_loaded.sem, SMALL)
            route(c, p)
            turn_gates(c, p)
            add_beta(c, p)

        def hidden(c, t, p):
            e, f = divmod(t, FT)
            if isinstance(c, int) and c == 0 and f == 0:
                pe.wait_ge(w1_loaded[e].sem, 16)
            if t == 0:
                pe.wait_ge(xlnT_ready.sem, xlnT_ready.at(c, 1))
            pe.wait_ge(gelu_ready.sem, gelu_ready.at(c, t + 1 - 4))
            nc.tensor.matmul(Hb[:, t % 4, :], W1[:, e, P * f:P * f + P], xlnT[:, p, :], start=True, stop=True) \
                .then_inc(h_mm.sem, 1)

        def outputs(c, t, p):
            e, f = divmod(t, FT)
            q = e % 2
            if f == 0:
                if isinstance(c, int) and c == 0:
                    pe.wait_ge(w2_centred.sem, e + 1)
                    pe.wait_ge(b2_step.sem, 4)
                pe.wait_ge(wexp_ready.sem, wexp_ready.at(c, TT * (e - 1)))
                nc.tensor.matmul(Ob[:, q].rearrange("p t d -> p (t d)"), ones1[:, :],
                                 b2row[:, e:e + 1, :].to_broadcast([1, TT, DM]), start=True, stop=False,
                                 skip_group_check=True)
            pe.wait_ge(gelu_ready.sem, gelu_ready.at(c, t + 1))
            for i in range(TT):
                last = nc.tensor.matmul(Ob[:, q, i, :], hT[:, t % 4, P * i:P * i + P], W2[:, e, f, :],
                                        start=False, stop=(f == FT - 1), skip_group_check=True)
            last.then_inc(o_mm.sem, 1)

        def body(c, p, has_next, has_last):
            hidden(c, 0, p)
            hidden(c, 1, p)
            for t in range(JT):
                if t + 2 < JT:
                    hidden(c, t + 2, p)
                outputs(c, t, p)
                if has_next:
                    if t == 17:
                        turn_xln(c + 1, 1 - p)
                    if t == 20:
                        route(c + 1, 1 - p)
                    if t == 28:
                        turn_gates(c + 1, 1 - p)
                    if t == 30:
                        add_beta(c + 1, 1 - p)

        chunks(nc.tensor, prepare, body)


_INS = ['L0_attn_x', 'L0_attn_ln_w', 'L0_attn_ln_b', 'L0_attn_W_in', 'L0_attn_b_in', 'L0_attn_conv_w',
        'L0_attn_conv_b', 'L0_attn_W_xproj', 'L0_attn_W_dt', 'L0_attn_b_dt', 'L0_attn_A_log', 'L0_attn_D',
        'L0_attn_W_out', 'L0_attn_b_out', 'L0_attn_Wg', 'L0_attn_bg', 'L0_attn_Wv', 'L0_attn_bv',
        'L0_ffn_router_w', 'L0_ffn_w1', 'L0_ffn_b1', 'L0_ffn_w2', 'L0_ffn_b2', 'L0_ffn_gamma',
        'L0_ffn_beta']


def kernel(**inputs):
    import numpy as np
    import concourse.bacc as bacc
    from concourse.bass_utils import run_bass_kernel_spmd

    nc = bacc.Bacc("TRN2", target_bir_lowering=False, num_devices=1)
    arrays, args = {}, []
    for name in _INS:
        a = np.ascontiguousarray(inputs[name])
        arrays[f"in_{name}"] = a
        args.append(nc.dram_tensor(f"in_{name}", a.shape, mybir.dt.from_np(a.dtype), kind="ExternalInput").ap())
    out = nc.dram_tensor("out_0", (ROWS, STEPS, DM), F32, kind="ExternalOutput").ap()
    build(nc, *args, out)
    r = run_bass_kernel_spmd(nc, [arrays], core_ids=[0])
    return r.results[0]["out_0"]
```

```python
from contextlib import ExitStack

import concourse.bass as bass
from concourse import mybir

F32 = mybir.dt.float32
F32R = mybir.dt.float32r
U32 = mybir.dt.uint32
ALU = mybir.AluOpType
ACT = mybir.ActivationFunctionType

P = 128
ROWS, STEPS, DM = 8, 1024, 128
DI, NS, RANK, TAPS = 256, 16, 64, 4
NH = DI // P
CH = 512
NCH = STEPS // CH
UNITS = 2 * NCH
CPG = P // NS
GPH = P // CPG
GROUPS = NH * GPH
SLOTS = UNITS * GROUPS
TILES = STEPS // P
PAD = TAPS - 1
HRING, XRING, DRING = 8, 8, 3
LAG = 4
EPS_IN, EPS_OUT = 1e-5, 1e-6
NE, FF = 8, 512
FT = FF // P
TC = 512
NTC = ROWS * STEPS // TC
TT = TC // P


class Signal:

    def __init__(self, ctx, nc, name, per):
        self.sem, self.per = ctx.enter_context(nc.semaphore(name)), per

    def at(self, row, count):
        value = row * self.per + count
        return max(value, 0) if isinstance(value, int) else value


def unit_of(u):
    return (0, u) if u < NCH else (1, 2 * NCH - 1 - u)


def group_of(g):
    half, j = divmod(g, GPH)
    tile, r = j % 4, j // 4
    jj = 4 * tile + r
    return half, jj, jj % 8, 2 * half + jj // 8, tile, r


SHIFT = GROUPS + 9
DECAY_BUFFER = [(s + SLOTS) % DRING if s < SHIFT else s % DRING for s in range(SLOTS)]


def decay_buffer(s):
    own = DECAY_BUFFER[s]
    return own, max(e for e in range(s - 2 * DRING, s) if DECAY_BUFFER[e % SLOTS] == own)


AHEAD = [0] * 14 + [1, 2, 3, 4, 4, 3, 2, 1] + [0] * 10


def inputs_made(s):
    return range(s + 1 + AHEAD[(s - 1) % GROUPS], s + 2 + AHEAD[s % GROUPS])


def directed(ap, direction):
    return ap if direction == 0 else ap[:, ::-1]


def build(nc, x, ln_w, ln_b, W_in, b_in, conv_w, conv_b, W_xproj, W_dt, b_dt, A_log, Dp, W_out,
          b_out, Wg, bg, Wv, bv, router_w, w1, b1, w2, b2, gamma, beta, out):
    ctx = ExitStack()
    with ctx:
        x3_dram = nc.dram_tensor("x3_scratch", (ROWS * STEPS, DM), F32, kind="Internal").ap()
        ident = ctx.enter_context(nc.sbuf_tensor("ident", [P, P], F32))
        cols = ctx.enter_context(nc.sbuf_tensor("cols", [P, 124], F32))
        mhalf = ctx.enter_context(nc.sbuf_tensor("mhalf", [P, 8], F32))
        with ExitStack() as phase:
            mamba(nc, phase, ident, cols, mhalf, x, ln_w, ln_b, W_in, b_in, conv_w, conv_b, W_xproj,
                  W_dt, b_dt, A_log, Dp, W_out, b_out, Wg, bg, Wv, bv, b1, x3_dram)
        with ExitStack() as phase:
            experts(nc, phase, ident, cols, mhalf, router_w, w1, w2, b2, gamma, beta, x3_dram, out)


STACK_DMAS = 4 * 16
LOADS = 21 * 16
PREP_DVE = 39

C_LNW, C_LNB, C_BIN, C_CONVB, C_BDT, C_D, C_BOUT, C_BG, C_BV, C_B1, C_A = \
    0, 2, 4, 12, 16, 20, 24, 26, 27, 28, 60


def mamba(nc, ctx, ident, cols, mhalf, x, ln_w, ln_b, W_in, b_in, conv_w, conv_b, W_xproj, W_dt,
          b_dt, A_log, Dp, W_out, b_out, Wg, bg, Wv, bv, b1, x3_dram):
    def sb(name, shape, dt=F32):
        return ctx.enter_context(nc.sbuf_tensor(name, shape, dt))

    def pb(name, shape):
        return ctx.enter_context(nc.psum_tensor(name, shape, F32))

    def sig(name, per):
        return Signal(ctx, nc, name, per)

    rows = sb("rows", [P, P])
    sel = sb("sel", [P, 8, P], F32R)
    red = sb("red", [P, 4, 32])
    negA = sb("negA", [P, 2 * GROUPS])
    taps = sb("taps", [P, 2, NH, TAPS])
    Wk = sb("Wk", [P, 2, TAPS, DI])
    Wz = sb("Wz", [P, 2, DI])
    bz = sb("bz", [P, 2 * 4])
    cbias = sb("cbias", [P, 4])
    edge = sb("edge", [P, 2, 3, NH])
    psum4 = sb("psum4", [P, 4, 4])
    Wdtx = sb("Wdtx", [P, 2, NH, RANK])
    Wbc = sb("Wbc", [P, 2, NH, 2, P])
    Wdt = sb("Wdt", [RANK, 2, DI])
    Wo = sb("Wo", [P, 2, NH, DM])
    Wgs = sb("Wgs", [P, 2, DM])
    Wvs = sb("Wvs", [P, 2, DM])
    halfD = sb("halfD", [P, 4])
    halfbg = sb("halfbg", [P, 1])
    ones = sb("ones", [P, 2])
    xn = sb("xn", [P, TILES, DM])
    xt = sb("xt", [P, TILES, DM])
    tok = sb("tok", [P, TILES, DM])
    x2T = sb("x2T", [P, STEPS + 2 * PAD])
    stA = sb("stA", [P, TILES, 6])
    mvA = sb("mvA", [P, TILES, 2])
    rsA = sb("rsA", [P, 5, TILES])
    th = sb("th", [P, NH, CH])
    xp2 = sb("xp2", [P, 2, NH, CH])
    sz2 = sb("sz2", [P, 2, NH, CH])
    Brep = sb("Brep", [P, 2, CH])
    Crep = sb("Crep", [P, 2, CH])
    dtT = sb("dtT", [RANK, CH])
    ex = sb("ex", [P, NH, CH])
    rl = sb("rl", [P, NH, CH])
    lg = sb("lg", [P, NH, CH])
    w1p = sb("w1p", [P, NH, CH])
    u2 = sb("u2", [P, NH, CH])
    dhi = sb("dhi", [P, NH, CH], F32R)
    dlo = sb("dlo", [P, NH, CH], F32R)
    uhi = sb("uhi", [P, NH, CH], F32R)
    ulo = sb("ulo", [P, NH, CH], F32R)
    stackD = sb("stackD", [P, 4, CH], F32R)
    stackU = sb("stackU", [P, 4, CH], F32R)
    yg = sb("yg", [P, NH, CH])
    fbT = sb("fbT", [P, 2, STEPS])
    dbx = sb("dbx", [P, XRING, CH])
    hs = sb("hs", [P, HRING, CH])
    carry = sb("carry", [P, 2 * GROUPS])
    sfb = sb("sfb", [P, CH])
    tg = sb("tg", [P, CH])
    a4 = sb("a4", [P, STEPS])
    x3 = sb("x3", [P, TILES, DM])
    stG = sb("stG", [P, TILES, 6])
    mvG = sb("mvG", [P, TILES, 2])
    rsG = sb("rsG", [P, 2, TILES])

    D = pb("D", [P, DRING, CH])
    U = pb("U", [P, 2, CH])
    Y = pb("Y", [P, CH])
    W = pb("W", [P, NH, CH])

    win_raw = hs[:, 0:2, :]
    taps_b = hs[:, 2:6, :].rearrange("p a b -> p (a b)").rearrange("p (d c k) -> p d c k", d=2, k=TAPS)
    wx_raw = hs[:, 6, 0:384].rearrange("p (d h n) -> p d h n", d=2, h=NH)
    sel_f = ex[:, :, :].rearrange("p h t -> p (h t)").rearrange("p (k m) -> p k m", k=8)

    loaded = sig("loaded", 0)
    made = {n: sig(n, 0) for n in ("ident_made", "masks_made", "cols_made", "bias_mm", "prep_dve",
                                   "rows_T", "zeros_made", "a_made", "half_made")}
    sp_ticks, pool_ticks, dve_ticks = (sig(n, 0) for n in ("sp_ticks", "pool_ticks", "dve_ticks"))
    x_loaded = sig("x_loaded", 16)
    xres_loaded = sig("xres_loaded", 16)
    x3_stored = sig("x3_stored", 16)
    dstack_loaded = [sig(f"dstack{h}_loaded", UNITS * STACK_DMAS) for h in range(NH)]
    ustack_loaded = [sig(f"ustack{h}_loaded", UNITS * STACK_DMAS) for h in range(NH)]
    statsA = sig("statsA", 2 * TILES)
    rstdA = sig("rstdA", 7)
    x1_ready = sig("x1_ready", TILES)
    x2_ready = sig("x2_ready", TILES)
    x2_turned = sig("x2_turned", 1)
    x2T_ready = sig("x2T_ready", 1)
    xp_mm = sig("xp_mm", UNITS * NH)
    conv_ready = sig("conv_ready", UNITS * NH)
    edge_done = sig("edge_done", 2 * NH)
    thx_ready = sig("thx_ready", UNITS * NH)
    xp_ready = sig("xp_ready", UNITS * NH)
    z_mm = sig("z_mm", UNITS * NH)
    z_ready = sig("z_ready", UNITS * NH)
    thz_ready = sig("thz_ready", UNITS)
    sz_ready = sig("sz_ready", UNITS)
    dt_mm = sig("dt_mm", UNITS)
    dt_ready = sig("dt_ready", UNITS)
    b_mm = sig("b_mm", UNITS)
    b_ready = sig("b_ready", UNITS)
    c_mm = sig("c_mm", UNITS)
    c_ready = sig("c_ready", UNITS)
    dp_mm = sig("dp_mm", UNITS * NH)
    abs_ready = sig("abs_ready", UNITS * NH)
    relu_ready = sig("relu_ready", UNITS * NH)
    exp_ready = sig("exp_ready", UNITS)
    onep_ready = sig("onep_ready", UNITS)
    back_ready = sig("back_ready", UNITS)
    ln_ready = sig("ln_ready", UNITS)
    resid_ready = sig("resid_ready", UNITS * NH)
    sp_sum = sig("sp_sum", UNITS)
    delta_ready = sig("delta_ready", UNITS * NH)
    dhi_ready = sig("dhi_ready", UNITS * NH)
    dlo_ready = [sig(f"dlo{h}_ready", UNITS) for h in range(NH)]
    u_ready = sig("u_ready", UNITS * NH)
    uhi_ready = sig("uhi_ready", UNITS * NH)
    ulo_ready = sig("ulo_ready", UNITS * NH)
    drep_ready = sig("drep_ready", SLOTS)
    urep_ready = sig("urep_ready", SLOTS)
    da_ready = sig("da_ready", SLOTS)
    dbx_ready = sig("dbx_ready", SLOTS)
    h_ready = sig("h_ready", SLOTS)
    carry_saved = sig("carry_saved", GROUPS)
    hc_ready = sig("hc_ready", SLOTS // 2)
    reduced = sig("reduced", SLOTS // 4)
    yd_ready = sig("yd_ready", UNITS * NH)
    yg_ready = sig("yg_ready", UNITS * NH)
    out_mm = sig("out_mm", UNITS)
    fb_ready = sig("fb_ready", UNITS)
    gate_mm = sig("gate_mm", NCH)
    value_mm = sig("value_mm", NCH)
    sfb_ready = sig("sfb_ready", NCH)
    tg_ready = sig("tg_ready", NCH)
    diff_ready = sig("diff_ready", NCH)
    gated_ready = sig("gated_ready", NCH)
    a4_ready = sig("a4_ready", NCH)
    a4_turned = sig("a4_turned", 1)
    sum_copied = sig("sum_copied", 1)
    statsG = sig("statsG", 2 * TILES)
    rstdG = sig("rstdG", 2)
    an_ready = sig("an_ready", TILES)
    x3_ready = sig("x3_ready", 1)

    x_rows = x.rearrange("r (t p) d -> r p t d", p=P)
    x3_rows = x3_dram.rearrange("(r t p) d -> r p t d", r=ROWS, p=P)

    def dram_row(view, b):
        return view[b] if isinstance(b, int) else view[bass.ds(b, 1), :, :, :].rearrange("o p t d -> (o p) t d")

    block = ctx.enter_context(nc.Block())

    @block.sync
    def _(sp):
        def load(dst, src):
            sp.dma_start(dst, src).then_inc(loaded.sem, 16)
            load.n += 16

        load.n = 0
        sp.dma_start(xn[:, :, :], dram_row(x_rows, 0)).then_inc(x_loaded.sem, 16)
        for at, t in ((C_LNW, ln_w), (C_LNB, ln_b), (C_BIN, b_in), (C_CONVB, conv_b), (C_BDT, b_dt),
                      (C_D, Dp), (C_BOUT, b_out), (C_B1, b1)):
            n = t.shape[0] * t.shape[1] // P
            load(rows[at:at + n, :], t.rearrange("a (b c) -> (a b) c", c=P))
        load(rows[C_BG:C_BG + 1, :], bg.rearrange("(a c) -> a c", a=1))
        load(rows[C_BV:C_BV + 1, :], bv.rearrange("(a c) -> a c", a=1))
        load(rows[C_A:C_A + 2 * GROUPS, :], A_log.rearrange("d (g c) n -> (d g) (c n)", c=CPG))
        load(win_raw, W_in.rearrange("d p c -> p d c"))
        load(taps[:, :, :, :], conv_w.rearrange("d (h p) k -> p d h k", p=P))
        load(hs[:, 2:6, :].rearrange("p a b -> p (a b)"),
             conv_w.rearrange("(o d) c k -> o (d c k)", o=1).to_broadcast([P, 2 * DI * TAPS]))
        for d in range(2):
            load(wx_raw[:, d], W_xproj[d].rearrange("(h p) n -> p h n", p=P))
            load(Wo[:, d], W_out[d].rearrange("(h p) n -> p h n", p=P))
        load(Wdt[:, :, :], W_dt.rearrange("d r c -> r d c"))
        load(Wgs[:, :, :], Wg.rearrange("(h p) n -> p h n", p=P))
        load(Wvs[:, :, :], Wv.rearrange("(h p) n -> p h n", p=P))
        assert load.n == LOADS

        def load_x(b):
            sp.wait_ge(x1_ready.sem, x1_ready.at(b, 0))
            sp.sem_inc(sp_ticks.sem, 1)
            sp.wait_ge(x2_ready.sem, x2_ready.at(b, 0))
            sp.sem_inc(sp_ticks.sem, 1)
            sp.dma_start(xn[:, :, :], dram_row(x_rows, b)).then_inc(x_loaded.sem, 16)

        def stacks(b, u, half):
            sp.wait_ge(drep_ready.sem, drep_ready.at(b, GROUPS * (u - 1) + GPH * (half + 1)))
            sp.sem_inc(sp_ticks.sem, 1)
            sp.wait_ge(urep_ready.sem, urep_ready.at(b, GROUPS * (u - 1) + GPH * (half + 1)))
            sp.sem_inc(sp_ticks.sem, 1)
            k = NH * u + half + 1
            for hi, lo, hi_ready, lo_ready, made_lo, stack, signal in (
                    (dhi, dlo, dhi_ready, dlo_ready[half], u + 1, stackD, dstack_loaded[half]),
                    (uhi, ulo, uhi_ready, ulo_ready, k, stackU, ustack_loaded[half])):
                sp.wait_ge(hi_ready.sem, hi_ready.at(b, k))
                sp.sem_inc(sp_ticks.sem, 1)
                sp.wait_ge(lo_ready.sem, lo_ready.at(b, made_lo))
                sp.sem_inc(sp_ticks.sem, 1)
                for a in range(2):
                    for level, part in enumerate((hi, lo)):
                        sp.dma_start(stack[64 * level:64 * level + 64, 2 * half + a, :].bitcast(F32),
                                     part[64 * a:64 * a + 64, half, :].bitcast(F32)) \
                            .then_inc(signal.sem, 16)

        def load_residual(b):
            sp.dma_start(x3[:, :, :], dram_row(x_rows, b)).then_inc(xres_loaded.sem, 16)

        def store_x3(b):
            sp.wait_ge(x3_ready.sem, x3_ready.at(b, 1))
            sp.sem_inc(sp_ticks.sem, 1)
            sp.dma_start(dram_row(x3_rows, b), x3[:, :, :]).then_inc(x3_stored.sem, 16)
            sp.wait_ge(x3_stored.sem, x3_stored.at(b, 16))
            sp.sem_inc(sp_ticks.sem, 1)

        def row(b, next_row, last_end):
            for u in range(UNITS):
                stacks(b, u, 1)
                if u == 1 and next_row:
                    load_x(b + 1)
                if u == 2 and last_end:
                    load_residual(b - 1)
                if u < UNITS - 1:
                    stacks(b, u + 1, 0)
                elif next_row:
                    stacks(b + 1, 0, 0)
                if u == 3 and last_end:
                    store_x3(b - 1)

        stacks(0, 0, 0)
        row(0, True, False)
        with nc.sync.Fori(1, ROWS - 1) as b:
            row(b, True, True)
        row(ROWS - 1, False, True)
        load_residual(ROWS - 1)
        store_x3(ROWS - 1)
    @block.gpsimd
    def _(pool):
        nc.gpsimd.memset(ident[:, :], 0.0).then_inc(made["zeros_made"].sem, 1)
        nc.gpsimd.memset(sel_f, 0.0).then_inc(made["zeros_made"].sem, 1)
        nc.gpsimd.memset(red[:, :, :], 1.0).then_inc(made["zeros_made"].sem, 1)
        nc.gpsimd.memset(mhalf[:, :], -0.5).then_inc(made["zeros_made"].sem, 1)
        nc.gpsimd.memset(x2T[:, 0:PAD], 0.0).then_inc(made["zeros_made"].sem, 1)
        nc.gpsimd.memset(x2T[:, PAD + STEPS:], 0.0).then_inc(made["zeros_made"].sem, 1)
        pool.wait_ge(made["zeros_made"].sem, 6)
        nc.gpsimd.affine_select(out=ident[:, :], in_=ident[:, :], compare_op=ALU.not_equal, fill=1.0,
                                base=0, pattern=[[-1, P]], channel_multiplier=1) \
            .then_inc(made["ident_made"].sem, 1)
        s4 = sel_f.rearrange("p k (d n) -> p k d n", n=NS)
        for i, base in enumerate((0, -64)):
            nc.gpsimd.affine_select(out=s4, in_=s4, compare_op=ALU.not_equal, fill=1.0, base=base,
                                    pattern=[[-CPG, 8], [-1, CPG], [0, NS]], channel_multiplier=1) \
                .then_inc(made["masks_made"].sem, 1)
            pool.wait_ge(made["masks_made"].sem, i + 1)
        nc.gpsimd.affine_select(out=red[:, :, :], in_=red[:, :, :], compare_op=ALU.is_ge, fill=0.0,
                                base=0, pattern=[[P, 4], [-NS, 32]], channel_multiplier=1) \
            .then_inc(made["masks_made"].sem, 1)
        pool.wait_ge(made["masks_made"].sem, 3)
        nc.gpsimd.affine_select(out=red[:, :, :], in_=red[:, :, :], compare_op=ALU.is_ge, fill=0.0,
                                base=NS - 1, pattern=[[-P, 4], [NS, 32]], channel_multiplier=-1) \
            .then_inc(made["masks_made"].sem, 1)
        pool.wait_ge(made["masks_made"].sem, 4)

        def rstds_in(b):
            pool.wait_ge(statsA.sem, statsA.at(b, 2 * TILES))
            pool.sem_inc(pool_ticks.sem, 1)
            var, ve, r1, v2, r2 = mvA[:, :, 1], rsA[:, 0, :], rsA[:, 1, :], rsA[:, 2, :], rsA[:, 3, :]
            nc.gpsimd.tensor_scalar(ve, var, 1.0, EPS_IN, ALU.mult, ALU.add).then_inc(rstdA.sem, 1)
            pool.wait_ge(rstdA.sem, rstdA.at(b, 1))
            nc.gpsimd.tensor_tensor(r1, ve, mhalf[:, :], ALU.pow).then_inc(rstdA.sem, 1)
            pool.wait_ge(rstdA.sem, rstdA.at(b, 2))
            nc.gpsimd.tensor_tensor(v2, r1, r1, ALU.mult).then_inc(rstdA.sem, 1)
            pool.wait_ge(rstdA.sem, rstdA.at(b, 3))
            nc.gpsimd.tensor_tensor(v2, v2, var, ALU.mult).then_inc(rstdA.sem, 1)
            pool.wait_ge(rstdA.sem, rstdA.at(b, 4))
            pool.sem_inc(pool_ticks.sem, 1)
            nc.gpsimd.tensor_scalar(v2, v2, 1.0, EPS_IN, ALU.mult, ALU.add).then_inc(rstdA.sem, 1)
            pool.wait_ge(rstdA.sem, rstdA.at(b, 5))
            nc.gpsimd.tensor_tensor(r2, v2, mhalf[:, :], ALU.pow).then_inc(rstdA.sem, 1)
            pool.wait_ge(rstdA.sem, rstdA.at(b, 6))
            nc.gpsimd.tensor_tensor(rsA[:, 4, :], r1, r2, ALU.mult).then_inc(rstdA.sem, 1)

        def softplus_residue(b, u, half):
            pool.wait_ge(exp_ready.sem, exp_ready.at(b, u + 1))
            pool.wait_ge(back_ready.sem, back_ready.at(b, u + 1))
            nc.gpsimd.tensor_tensor(w1p[:, half, :], ex[:, half, :], w1p[:, half, :], ALU.subtract) \
                .then_inc(resid_ready.sem, 1)

        def make_u(b, u, half):
            k = NH * u + half + 1
            pool.wait_ge(delta_ready.sem, delta_ready.at(b, k))
            pool.wait_ge(xp_ready.sem, xp_ready.at(b, k))
            nc.gpsimd.tensor_tensor(u2[:, half, :], lg[:, half, :], xp2[:, u % 2, half, :], ALU.mult) \
                .then_inc(u_ready.sem, 1)

        def low_delta_second(b, u):
            pool.wait_ge(dhi_ready.sem, dhi_ready.at(b, NH * u + 2))
            pool.wait_ge(dstack_loaded[1].sem, dstack_loaded[1].at(b, STACK_DMAS * u))
            nc.gpsimd.tensor_tensor(dlo[:, 1, :], lg[:, 1, :], dhi[:, 1, :].bitcast(F32), ALU.subtract) \
                .then_inc(dlo_ready[1].sem, 1)

        def low_u(b, u, half):
            pool.wait_ge(uhi_ready.sem, uhi_ready.at(b, NH * u + half + 1))
            pool.wait_ge(ustack_loaded[half].sem, ustack_loaded[half].at(b, STACK_DMAS * u))
            nc.gpsimd.tensor_tensor(ulo[:, half, :], u2[:, half, :], uhi[:, half, :].bitcast(F32), ALU.subtract) \
                .then_inc(ulo_ready.sem, 1)

        def two_groups(b, s):
            u, g = divmod(s, GROUPS)
            direction, _ = unit_of(u)
            h = hs[:, s % HRING:s % HRING + 2, :]
            pool.wait_ge(h_ready.sem, h_ready.at(b, s + 2))
            if u % 2 == 0:
                pool.sem_inc(pool_ticks.sem, 1)
                last = CH - 1 if direction == 0 else 0
                at = direction * GROUPS + g
                nc.gpsimd.tensor_copy(carry[:, at:at + 2], h[:, :, last]).then_inc(carry_saved.sem, 1)
                pool.wait_ge(carry_saved.sem, carry_saved.at(b, at // 2 + 1))
            if g == 0:
                pool.wait_ge(c_ready.sem, c_ready.at(b, u + 1))
            nc.gpsimd.tensor_tensor(h, h, Crep[:, u % 2:u % 2 + 1, :].to_broadcast([P, 2, CH]), ALU.mult) \
                .then_inc(hc_ready.sem, 1)

        def sum_directions(b, c):
            pool.wait_ge(fb_ready.sem, fb_ready.at(b, UNITS))
            if c:
                pool.wait_ge(a4_ready.sem, a4_ready.at(b, c))
            cut = slice(CH * c, CH * c + CH)
            nc.gpsimd.tensor_tensor(sfb[:, :], fbT[:, 0, cut], fbT[:, 1, cut], ALU.add) \
                .then_inc(sfb_ready.sem, 1)

        def rstds_gated(b):
            pool.wait_ge(statsG.sem, statsG.at(b, 2 * TILES))
            pool.sem_inc(pool_ticks.sem, 1)
            nc.gpsimd.tensor_scalar(rsG[:, 0, :], mvG[:, :, 1], 1.0, 16 * EPS_IN, ALU.mult, ALU.add) \
                .then_inc(rstdG.sem, 1)
            pool.wait_ge(rstdG.sem, rstdG.at(b, 1))
            nc.gpsimd.tensor_tensor(rsG[:, 1, :], rsG[:, 0, :], mhalf[:, :], ALU.pow) \
                .then_inc(rstdG.sem, 1)

        def row(b, next_row, last_end):
            for s in range(1, SLOTS, 2):
                u, g = divmod(s, GROUPS)
                nb, nu = (b, u + 1) if u < UNITS - 1 else (b + 1, 0)
                if u < UNITS - 1 or next_row:
                    if g == 17:
                        softplus_residue(nb, nu, 0)
                    if g == 21:
                        make_u(nb, nu, 0)
                    if g == 25:
                        low_u(nb, nu, 0)
                    if g == 27:
                        softplus_residue(nb, nu, 1)
                if g == 1:
                    make_u(b, u, 1)
                if g == 3:
                    low_delta_second(b, u)
                if g == 5:
                    low_u(b, u, 1)
                if u < NCH and last_end and g == 29:
                    sum_directions(b - 1, u)
                if u == 2 and next_row and g == 7:
                    rstds_in(b + 1)
                if u == 3 and last_end and g == 5:
                    rstds_gated(b - 1)
                two_groups(b, s - 1)

        rstds_in(0)
        for half in range(NH):
            softplus_residue(0, 0, half)
        make_u(0, 0, 0)
        low_u(0, 0, 0)
        row(0, True, False)
        with nc.gpsimd.Fori(1, ROWS - 1) as b:
            row(b, True, True)
        row(ROWS - 1, False, True)
        for c in range(NCH):
            sum_directions(ROWS - 1, c)
        rstds_gated(ROWS - 1)

    @block.scalar
    def _(act):
        act.wait_ge(made["rows_T"].sem, 1)
        nc.scalar.activation(cols[:, :], W[:, 0, 0:124], ACT.Copy).then_inc(made["cols_made"].sem, 1)
        act.wait_ge(made["cols_made"].sem, 1)
        nc.scalar.activation(negA[:, :], cols[:, C_A:C_A + 2 * GROUPS], ACT.Exp).then_inc(made["a_made"].sem, 1)
        act.wait_ge(made["a_made"].sem, 1)
        nc.scalar.mul(negA[:, :], negA[:, :], -1.0).then_inc(made["a_made"].sem, 1)
        act.wait_ge(made["a_made"].sem, 2)
        nc.scalar.activation(halfbg[:, :], cols[:, C_BG:C_BG + 1], ACT.Copy).then_inc(sum_copied.sem, 1)
        act.wait_ge(sum_copied.sem, 1)
        act.wait_ge(loaded.sem, LOADS)
        for i, (dst, src, f) in enumerate((
                (halfD[:, :], cols[:, C_D:C_D + 4], 0.5),
                (halfbg[:, :], halfbg[:, :], 0.5),
                (Wo[:, :, :, :], Wo[:, :, :, :], 0.5),
                (Wdtx[:, :, :, :], wx_raw[:, :, :, 0:RANK], 0.5))):
            nc.scalar.mul(dst, src, f).then_inc(made["half_made"].sem, 1)
        for d in range(2):
            for h in range(NH):
                for k, f in ((0, 0.25), (1, 0.5)):
                    src = wx_raw[:, d, h, RANK + NS * k:RANK + NS * k + NS]
                    src = src.rearrange("p (o n) -> p o n", o=1).to_broadcast([P, CPG, NS])
                    nc.scalar.mul(Wbc[:, d, h, k, :].rearrange("p (r n) -> p r n", n=NS), src, f) \
                        .then_inc(made["half_made"].sem, 1)

        def evacuate_x2(b):
            act.wait_ge(x2_turned.sem, x2_turned.at(b, 1))
            act.wait_ge(z_mm.sem, z_mm.at(b, 0))
            nc.scalar.activation(x2T[:, PAD:PAD + STEPS], W[:, :, :].rearrange("p a t -> p (a t)"),
                                 ACT.Copy).then_inc(x2T_ready.sem, 1)

        def conv(b, u, half):
            d, _ = unit_of(u)
            act.wait_ge(xp_mm.sem, xp_mm.at(b, NH * u + half + 1))
            nc.scalar.activation(W[:, half, :], W[:, half, :], ACT.Identity,
                                 bias=cbias[:, 2 * d + half:2 * d + half + 1]).then_inc(conv_ready.sem, 1)

        def tanh_x(b, u, half):
            act.wait_ge(conv_ready.sem, conv_ready.at(b, NH * u + half + 1))
            if u % 2 == 0:
                act.wait_ge(edge_done.sem, edge_done.at(b, NH * (u // 2) + half + 1))
            act.wait_ge(sz_ready.sem, sz_ready.at(b, u))
            nc.scalar.activation(th[:, half, :], W[:, half, :], ACT.Tanh, scale=0.5).then_inc(thx_ready.sem, 1)

        def gate_z(b, u, half):
            d, _ = unit_of(u)
            act.wait_ge(z_mm.sem, z_mm.at(b, NH * u + NH - half))
            at = d * 4 + 2 + half
            nc.scalar.activation(W[:, half, :], W[:, half, :], ACT.Identity, bias=bz[:, at:at + 1]) \
                .then_inc(z_ready.sem, 1)

        def tanh_z(b, u):
            act.wait_ge(z_ready.sem, z_ready.at(b, NH * (u + 1)))
            act.wait_ge(xp_ready.sem, xp_ready.at(b, NH * (u + 1)))
            nc.scalar.activation(th[:, :, :], W[:, :, :], ACT.Tanh, scale=0.5).then_inc(thz_ready.sem, 1)

        def take_dt(b, u):
            act.wait_ge(dt_mm.sem, dt_mm.at(b, u + 1))
            act.wait_ge(dp_mm.sem, dp_mm.at(b, NH * u))
            nc.scalar.activation(dtT[:, :], W[0:RANK, 0, :], ACT.Copy).then_inc(dt_ready.sem, 1)

        def take_b(b, u):
            act.wait_ge(b_mm.sem, b_mm.at(b, u + 1))
            act.wait_ge(dbx_ready.sem, dbx_ready.at(b, GROUPS * (u - 1)))
            nc.scalar.activation(Brep[:, u % 2, :], W[:, 0, :], ACT.Copy).then_inc(b_ready.sem, 1)

        def take_c(b, u):
            act.wait_ge(c_mm.sem, c_mm.at(b, u + 1))
            act.wait_ge(hc_ready.sem, hc_ready.at(b, GROUPS // 2 * (u - 1)))
            nc.scalar.activation(Crep[:, u % 2, :], W[:, 0, :], ACT.Copy).then_inc(c_ready.sem, 1)

        def absolute(b, u, half):
            d, _ = unit_of(u)
            bias = cols[:, C_BDT + 2 * d + half:C_BDT + 2 * d + half + 1]
            act.wait_ge(dp_mm.sem, dp_mm.at(b, NH * u + half + 1))
            act.wait_ge(resid_ready.sem, resid_ready.at(b, NH * u))
            nc.scalar.activation(ex[:, half, :], W[:, half, :], ACT.Abs, bias=bias).then_inc(abs_ready.sem, 1)
            act.wait_ge(sp_sum.sem, sp_sum.at(b, u))
            nc.scalar.activation(rl[:, half, :], W[:, half, :], ACT.Relu, bias=bias).then_inc(relu_ready.sem, 1)

        def softplus_exp(b, u):
            act.wait_ge(abs_ready.sem, abs_ready.at(b, NH * (u + 1)))
            nc.scalar.activation(ex[:, :, :], ex[:, :, :], ACT.Exp, scale=-1.0).then_inc(exp_ready.sem, 1)

        def softplus_one(b, u):
            act.wait_ge(exp_ready.sem, exp_ready.at(b, u + 1))
            act.wait_ge(delta_ready.sem, delta_ready.at(b, NH * u))
            nc.scalar.activation(w1p[:, :, :], ex[:, :, :], ACT.Identity, bias=ones[:, 0:1]).then_inc(onep_ready.sem, 1)

        def softplus_back(b, u):
            act.wait_ge(onep_ready.sem, onep_ready.at(b, u + 1))
            nc.scalar.activation(w1p[:, :, :], w1p[:, :, :], ACT.Identity, bias=ones[:, 1:2]).then_inc(back_ready.sem, 1)

        def softplus_ln(b, u):
            act.wait_ge(u_ready.sem, u_ready.at(b, NH * u))
            for half in range(NH):
                act.wait_ge(dlo_ready[half].sem, dlo_ready[half].at(b, u))
            nc.scalar.activation(lg[:, :, :], ex[:, :, :], ACT.Ln, bias=ones[:, 0:1]).then_inc(ln_ready.sem, 1)

        def split_delta(b, u, half):
            act.wait_ge(delta_ready.sem, delta_ready.at(b, NH * u + half + 1))
            act.wait_ge(dstack_loaded[half].sem, dstack_loaded[half].at(b, STACK_DMAS * u))
            nc.scalar.activation(dhi[:, half, :], lg[:, half, :], ACT.Copy).then_inc(dhi_ready.sem, 1)

        def split_u(b, u, half):
            act.wait_ge(u_ready.sem, u_ready.at(b, NH * u + half + 1))
            act.wait_ge(ustack_loaded[half].sem, ustack_loaded[half].at(b, STACK_DMAS * u))
            nc.scalar.activation(uhi[:, half, :], u2[:, half, :], ACT.Copy).then_inc(uhi_ready.sem, 1)

        def decay(b, s):
            u, g = divmod(s, GROUPS)
            d, _ = unit_of(u)
            half, jj, *_ = group_of(g)
            at = d * GROUPS + half * GPH + jj
            k, _ = decay_buffer(s)
            act.wait_ge(drep_ready.sem, drep_ready.at(b, s + 1))
            nc.scalar.activation(D[:, k, :], D[:, k, :], ACT.Exp, scale=negA[:, at:at + 1]) \
                .then_inc(da_ready.sem, 1)

        def take_out(b, u):
            d, c = unit_of(u)
            act.wait_ge(out_mm.sem, out_mm.at(b, u + 1))
            if u < UNITS - 1:
                act.wait_ge(a4_ready.sem, a4_ready.at(b - 1, c + 1))
            nc.scalar.activation(fbT[:, d, CH * c:CH * c + CH], W[:, 1, :], ACT.Identity,
                                 bias=cols[:, C_BOUT + d:C_BOUT + d + 1]).then_inc(fb_ready.sem, 1)

        def gate(b, c):
            act.wait_ge(gate_mm.sem, gate_mm.at(b, c + 1))
            if c:
                act.wait_ge(gated_ready.sem, gated_ready.at(b, c))
            nc.scalar.activation(tg[:, :], W[:, 0, :], ACT.Tanh, bias=halfbg[:, 0:1], scale=0.5) \
                .then_inc(tg_ready.sem, 1)

        def take_sum(b, next_row):
            act.wait_ge(a4_turned.sem, a4_turned.at(b, 1))
            if next_row:
                act.wait_ge(x2_turned.sem, x2_turned.at(b + 2, 1))
            else:
                act.wait_ge(x3_ready.sem, x3_ready.at(b, 0))
            nc.scalar.activation(tok[:, :, :].rearrange("p t d -> p (t d)"), W[:, :, :].rearrange("p a t -> p (a t)"),
                                 ACT.Copy).then_inc(sum_copied.sem, 1)

        def row(b, next_row, last_end):
            for s in range(SLOTS):
                u, g = divmod(s, GROUPS)
                if s < SLOTS - 1:
                    decay(b, s + 1)
                elif next_row:
                    decay(b + 1, 0)
                nb, nu = (b, u + 1) if u < UNITS - 1 else (b + 1, 0)
                pb, pu = (b, u - 1) if u > 0 else (b - 1, UNITS - 1)
                prepares = u < UNITS - 1 or next_row
                if g == 3:
                    split_u(b, u, 1)
                if prepares:
                    if g == 3:
                        conv(nb, nu, 0)
                    if g == 4:
                        tanh_x(nb, nu, 0)
                    if g == 7:
                        conv(nb, nu, 1)
                    if g == 8:
                        tanh_x(nb, nu, 1)
                    if g == 11:
                        take_dt(nb, nu)
                    if g == 13:
                        absolute(nb, nu, 0)
                    if g == 14:
                        absolute(nb, nu, 1)
                    if g == 15:
                        nc.scalar.preload_act_table_set("natural_log_exp_and_others")
                    if g == 16:
                        softplus_exp(nb, nu)
                    if g == 17:
                        softplus_one(nb, nu)
                        softplus_ln(nb, nu)
                    if g == 18:
                        take_b(nb, nu)
                        softplus_back(nb, nu)
                if g == 20 and (u > 0 or last_end):
                    take_out(pb, pu)
                if prepares:
                    if g == 21:
                        split_delta(nb, nu, 0)
                    if g == 22:
                        take_c(nb, nu)
                    if g == 23:
                        split_u(nb, nu, 0)
                    if g == 24:
                        gate_z(nb, nu, 1)
                    if g == 25:
                        nc.scalar.preload_act_table_set("exp_and_others")
                    if g == 26:
                        gate_z(nb, nu, 0)
                    if g == 27:
                        tanh_z(nb, nu)
                    if g == 31:
                        split_delta(nb, nu, 1)
                if u < NCH and last_end and g == 31:
                    gate(b - 1, u)
                if u == 2 and next_row and g == 30:
                    evacuate_x2(b + 1)
                if u == 2 and last_end and g == 31:
                    take_sum(b - 1, next_row)

        evacuate_x2(0)
        act.wait_ge(made["prep_dve"].sem, PREP_DVE)
        for half in range(NH):
            conv(0, 0, half)
            tanh_x(0, 0, half)
        take_dt(0, 0)
        absolute(0, 0, 0)
        absolute(0, 0, 1)
        softplus_exp(0, 0)
        softplus_one(0, 0)
        softplus_back(0, 0)
        softplus_ln(0, 0)
        take_b(0, 0)
        take_c(0, 0)
        split_delta(0, 0, 0)
        split_u(0, 0, 0)
        gate_z(0, 0, 1)
        gate_z(0, 0, 0)
        tanh_z(0, 0)
        split_delta(0, 0, 1)
        decay(0, 0)
        row(0, True, False)
        with nc.scalar.Fori(1, ROWS - 1) as b:
            row(b, True, True)
        row(ROWS - 1, False, True)
        take_out(ROWS - 1, UNITS - 1)
        for c in range(NCH):
            gate(ROWS - 1, c)
        take_sum(ROWS - 1, False)

    @block.vector
    def _(dve):
        prep = made["prep_dve"].sem
        count = [0]

        def step(instruction):
            instruction.then_inc(prep, 1)
            count[0] += 1
            dve.wait_ge(prep, count[0])

        def stats_in(b):
            dve.wait_ge(x_loaded.sem, x_loaded.at(b, 16))
            dve.wait_ge(rstdA.sem, rstdA.at(b, 0))
            dve.wait_ge(x2_ready.sem, x2_ready.at(b, 0))
            for t in range(TILES):
                nc.vector.bn_stats(stA[:, t, :], xn[:, t, :]).then_inc(statsA.sem, 1)

        def aggregate_in(b):
            dve.wait_ge(statsA.sem, statsA.at(b, TILES))
            dve.sem_inc(dve_ticks.sem, 1)
            for t in range(TILES):
                nc.vector.bn_aggr(mvA[:, t, :], stA[:, t, :]).then_inc(statsA.sem, 1)

        def make_x1(b, tiles):
            if tiles[0] == 0:
                dve.wait_ge(out_mm.sem, out_mm.at(b, 0))
                dve.wait_ge(rstdA.sem, rstdA.at(b, 7))
                dve.wait_ge(statsA.sem, statsA.at(b, 2 * TILES))
            for t in tiles:
                nc.vector.tensor_scalar(xt[:, t, :], xn[:, t, :], mvA[:, t, 0:1], rsA[:, 1, t:t + 1],
                                        ALU.subtract, ALU.mult).then_inc(x1_ready.sem, 1)

        def make_x2(b, tiles):
            if tiles[0] == 0:
                dve.wait_ge(rstdA.sem, rstdA.at(b, 7))
                dve.wait_ge(statsA.sem, statsA.at(b, 2 * TILES))
            for t in tiles:
                nc.vector.tensor_scalar(tok[:, t, :], xn[:, t, :], mvA[:, t, 0:1], rsA[:, 4, t:t + 1],
                                        ALU.subtract, ALU.mult).then_inc(x2_ready.sem, 1)

        step(nc.vector.memset(ones[:, 0:1], 1.0))
        step(nc.vector.memset(ones[:, 1:2], -1.0))
        dve.wait_ge(made["masks_made"].sem, 4)
        step(nc.vector.tensor_copy(sel[:, :, :], sel_f))
        stats_in(0)
        aggregate_in(0)
        dve.wait_ge(made["cols_made"].sem, 1)
        dve.wait_ge(loaded.sem, LOADS)
        dve.wait_ge(made["bias_mm"].sem, 1)
        step(nc.vector.tensor_tensor(bz[:, :], W[:, 0, 128:136], cols[:, C_BIN:C_BIN + 8], ALU.add))
        make_x2(0, range(TILES))
        for d in range(2):
            for h in range(NH):
                at = 2 * d + h
                bias = bz[:, 4 * d + h:4 * d + h + 1]
                for k in range(TAPS):
                    tap = taps[:, d, h, k:k + 1]
                    if k == 0:
                        step(nc.vector.tensor_tensor(psum4[:, 0, at:at + 1], tap, bias, ALU.mult))
                    else:
                        step(nc.vector.scalar_tensor_tensor(psum4[:, k, at:at + 1], tap, bias,
                                                            psum4[:, k - 1, at:at + 1], ALU.mult, ALU.add))
        step(nc.vector.tensor_tensor(cbias[:, :], psum4[:, 3, :], cols[:, C_CONVB:C_CONVB + 4], ALU.add))
        for t in range(3):
            step(nc.vector.tensor_scalar(edge[:, 0, t, :], psum4[:, 2 - t, 0:2], -1.0, None, ALU.mult))
            step(nc.vector.tensor_scalar(edge[:, 1, t, :], psum4[:, t, 2:4], -1.0, None, ALU.mult))
        for d in range(2):
            w = cols[:, C_LNW + d:C_LNW + d + 1]
            step(nc.vector.tensor_scalar(Wz[:, d, :], win_raw[:, d, DI:], w, None, ALU.mult))
            step(nc.vector.tensor_scalar(win_raw[:, d, :], win_raw[:, d, :], w, None, ALU.mult))
            for k in range(TAPS):
                step(nc.vector.tensor_tensor(Wk[:, d, k, :], win_raw[:, d, 0:DI], taps_b[:, d, :, k], ALU.mult))
        assert count[0] == PREP_DVE

        def fix_edge(b, u, half):
            d, _ = unit_of(u)
            dve.wait_ge(conv_ready.sem, conv_ready.at(b, NH * u + half + 1))
            at = W[:, half, 0:3] if d == 0 else W[:, half, CH - 3:CH]
            nc.vector.tensor_tensor(at, at, edge[:, d, :, half], ALU.add).then_inc(edge_done.sem, 1)

        def silu_x(b, u, half):
            dve.wait_ge(thx_ready.sem, thx_ready.at(b, NH * u + half + 1))
            dve.wait_ge(c_mm.sem, c_mm.at(b, u - 1))
            dve.wait_ge(u_ready.sem, u_ready.at(b, NH * (u - 1)))
            dve.wait_ge(yd_ready.sem, yd_ready.at(b, NH * (u - 1)))
            nc.vector.scalar_tensor_tensor(xp2[:, u % 2, half, :], th[:, half, :], 1.0, W[:, half, :],
                                           ALU.add, ALU.mult).then_inc(xp_ready.sem, 1)

        def silu_z(b, u):
            dve.wait_ge(thz_ready.sem, thz_ready.at(b, u + 1))
            dve.wait_ge(yg_ready.sem, yg_ready.at(b, NH * (u - 1)))
            nc.vector.scalar_tensor_tensor(sz2[:, u % 2], th[:, :, :], 1.0, W[:, :, :], ALU.add, ALU.mult) \
                .then_inc(sz_ready.sem, 1)

        def softplus_sum(b, u):
            dve.wait_ge(ln_ready.sem, ln_ready.at(b, u + 1))
            dve.wait_ge(relu_ready.sem, relu_ready.at(b, NH * (u + 1)))
            nc.vector.tensor_tensor(lg[:, :, :], lg[:, :, :], rl[:, :, :], ALU.add).then_inc(sp_sum.sem, 1)

        def make_delta(b, u, half):
            dve.wait_ge(sp_sum.sem, sp_sum.at(b, u + 1))
            dve.wait_ge(resid_ready.sem, resid_ready.at(b, NH * u + half + 1))
            nc.vector.tensor_tensor(lg[:, half, :], lg[:, half, :], w1p[:, half, :], ALU.add) \
                .then_inc(delta_ready.sem, 1)

        def low_delta(b, u):
            dve.wait_ge(dhi_ready.sem, dhi_ready.at(b, NH * u + 1))
            dve.wait_ge(dstack_loaded[0].sem, dstack_loaded[0].at(b, STACK_DMAS * u))
            nc.vector.tensor_tensor(dlo[:, 0, :], lg[:, 0, :], dhi[:, 0, :].bitcast(F32), ALU.subtract) \
                .then_inc(dlo_ready[0].sem, 1)

        def scan_input(b, s):
            u, g = divmod(s, GROUPS)
            dve.wait_ge(urep_ready.sem, urep_ready.at(b, s + 1))
            dve.wait_ge(h_ready.sem, h_ready.at(b, s + 1 - XRING))
            if g == 0:
                dve.wait_ge(b_ready.sem, b_ready.at(b, u + 1))
            nc.vector.tensor_tensor(dbx[:, s % XRING, :], U[:, s % 2, :], Brep[:, u % 2, :], ALU.mult) \
                .then_inc(dbx_ready.sem, 1)

        def scan(b, s):
            u, g = divmod(s, GROUPS)
            d, _ = unit_of(u)
            initial = 0.0
            if u % 2 == 1:
                at = d * GROUPS + g
                if g % 2 == 0:
                    dve.wait_ge(carry_saved.sem, carry_saved.at(b, at // 2 + 1))
                initial = carry[:, at:at + 1]
            dve.wait_ge(dbx_ready.sem, dbx_ready.at(b, s + 1))
            dve.wait_ge(da_ready.sem, da_ready.at(b, s + 1))
            dve.wait_ge(reduced.sem, reduced.at(b, (s - HRING) // 4 + 1))
            nc.vector.tensor_tensor_scan(directed(hs[:, s % HRING, :], d), directed(D[:, decay_buffer(s)[0], :], d),
                                         directed(dbx[:, s % XRING, :], d), initial, ALU.mult, ALU.add) \
                .then_inc(h_ready.sem, 1)

        def gate_y(b, u, half):
            d, _ = unit_of(u)
            k = NH * u + half + 1
            dve.wait_ge(reduced.sem, reduced.at(b, 4 * k))
            dve.wait_ge(out_mm.sem, out_mm.at(b, u))
            nc.vector.scalar_tensor_tensor(Y[:, :], xp2[:, u % 2, half, :], halfD[:, 2 * d + half:2 * d + half + 1],
                                           Y[:, :], ALU.mult, ALU.add).then_inc(yd_ready.sem, 1)
            dve.wait_ge(yd_ready.sem, yd_ready.at(b, k))
            nc.vector.tensor_tensor(yg[:, half, :], Y[:, :], sz2[:, u % 2, half, :], ALU.mult) \
                .then_inc(yg_ready.sem, 1)

        def gated_sum(b, c):
            V = W[:, 1, :]
            dve.wait_ge(value_mm.sem, value_mm.at(b, c + 1))
            dve.wait_ge(sfb_ready.sem, sfb_ready.at(b, c + 1))
            nc.vector.scalar_tensor_tensor(V, V, cols[:, C_BV:C_BV + 1], sfb[:, :], ALU.add, ALU.subtract) \
                .then_inc(diff_ready.sem, 1)
            dve.wait_ge(diff_ready.sem, diff_ready.at(b, c + 1))
            dve.wait_ge(tg_ready.sem, tg_ready.at(b, c + 1))
            nc.vector.scalar_tensor_tensor(V, tg[:, :], 1.0, V, ALU.add, ALU.mult).then_inc(gated_ready.sem, 1)
            dve.wait_ge(gated_ready.sem, gated_ready.at(b, c + 1))
            nc.vector.scalar_tensor_tensor(a4[:, CH * c:CH * c + CH], sfb[:, :], 2.0, V, ALU.mult, ALU.add) \
                .then_inc(a4_ready.sem, 1)

        def stats_gated(b):
            dve.wait_ge(sum_copied.sem, sum_copied.at(b, 2))
            for t in range(TILES):
                nc.vector.bn_stats(stG[:, t, :], tok[:, t, :]).then_inc(statsG.sem, 1)
            dve.wait_ge(statsG.sem, statsG.at(b, TILES))
            dve.sem_inc(dve_ticks.sem, 1)
            for t in range(TILES):
                nc.vector.bn_aggr(mvG[:, t, :], stG[:, t, :]).then_inc(statsG.sem, 1)

        def normalise_sum(b, tiles):
            if tiles[0] == 0:
                dve.wait_ge(rstdG.sem, rstdG.at(b, 2))
                dve.wait_ge(statsG.sem, statsG.at(b, 2 * TILES))
            for t in tiles:
                nc.vector.tensor_scalar(tok[:, t, :], tok[:, t, :], mvG[:, t, 0:1], rsG[:, 1, t:t + 1],
                                        ALU.subtract, ALU.mult).then_inc(an_ready.sem, 1)

        def make_x3(b):
            dve.wait_ge(an_ready.sem, an_ready.at(b, TILES))
            dve.wait_ge(xres_loaded.sem, xres_loaded.at(b, 16))
            nc.vector.tensor_tensor(x3[:, :, :], tok[:, :, :], x3[:, :, :], ALU.add).then_inc(x3_ready.sem, 1)

        def two_tiles(g, first):
            return range(g - first, g - first + 2) if first <= g < first + TILES and (g - first) % 2 == 0 else ()

        def row(b, next_row, last_end):
            for s in range(SLOTS):
                u, g = divmod(s, GROUPS)
                for n in inputs_made(s):
                    if n < SLOTS:
                        scan_input(b, n)
                    elif next_row:
                        scan_input(b + 1, n - SLOTS)
                scan(b, s)
                nb, nu = (b, u + 1) if u < UNITS - 1 else (b + 1, 0)
                if g == 5 and (u > 0 or last_end):
                    gate_y(*((b, u - 1) if u > 0 else (b - 1, UNITS - 1)), 1)
                if g == 21:
                    gate_y(b, u, 0)
                if u < UNITS - 1 or next_row:
                    if g in (3, 7) and nu % 2 == 0:
                        fix_edge(nb, nu, (g - 3) // 4)
                    if g == 5:
                        silu_x(nb, nu, 0)
                    if g == 9:
                        silu_x(nb, nu, 1)
                    if g == 19:
                        softplus_sum(nb, nu)
                    if g in (20, 30):
                        make_delta(nb, nu, (g - 20) // 10)
                    if g == 22:
                        low_delta(nb, nu)
                    if g == 28:
                        silu_z(nb, nu)
                if 0 < u <= NCH and last_end and g == 1:
                    gated_sum(b - 1, u - 1)
                if u == 0 and last_end and two_tiles(g, 22):
                    make_x1(b, two_tiles(g, 22))
                if u == 2 and next_row:
                    if g == 3:
                        stats_in(b + 1)
                    if g == 4:
                        aggregate_in(b + 1)
                    if two_tiles(g, 12):
                        make_x2(b + 1, two_tiles(g, 12))
                if u == 3 and last_end:
                    if g == 2:
                        stats_gated(b - 1)
                    if two_tiles(g, 10):
                        normalise_sum(b - 1, two_tiles(g, 10))
                    if g == 24:
                        make_x3(b - 1)

        make_x1(0, range(TILES))
        for half in range(NH):
            fix_edge(0, 0, half)
            silu_x(0, 0, half)
        softplus_sum(0, 0)
        make_delta(0, 0, 0)
        low_delta(0, 0)
        make_delta(0, 0, 1)
        silu_z(0, 0)
        scan_input(0, 0)
        row(0, True, False)
        with nc.vector.Fori(1, ROWS - 1) as b:
            row(b, True, True)
        row(ROWS - 1, False, True)
        gate_y(ROWS - 1, UNITS - 1, 1)
        for c in range(NCH):
            gated_sum(ROWS - 1, c)
        stats_gated(ROWS - 1)
        normalise_sum(ROWS - 1, range(TILES))
        make_x3(ROWS - 1)

    @block.tensor
    def _(pe):
        pe.wait_ge(made["ident_made"].sem, 1)
        pe.wait_ge(loaded.sem, LOADS)
        nc.tensor.transpose(W[:, 0, 0:124], rows[0:124, :], ident[0:124, 0:124]).then_inc(made["rows_T"].sem, 1)
        pe.wait_ge(made["cols_made"].sem, 1)
        for d in range(2):
            for m in range(4):
                last = nc.tensor.matmul(W[:, 0, 128 + 4 * d + m:129 + 4 * d + m], win_raw[:, d, P * m:P * m + P],
                                        cols[:, C_LNB + d:C_LNB + d + 1], start=True, stop=True)
        last.then_inc(made["bias_mm"].sem, 1)

        def turn(src, signal):
            for t in range(TILES):
                last = nc.tensor.transpose(W[:, t // 4, P * (t % 4):P * (t % 4) + P], src[:, t, :], ident[:, :])
            last.then_inc(signal.sem, 1)

        def turn_x2(b):
            pe.wait_ge(sz_ready.sem, sz_ready.at(b, 0))
            pe.wait_ge(x2_ready.sem, x2_ready.at(b, TILES))
            turn(tok, x2_turned)

        def product_x(b, u, half, k):
            d, c = unit_of(u)
            if k == 0:
                pe.wait_ge(x2T_ready.sem, x2T_ready.at(b, 1))
                pe.wait_ge(sz_ready.sem, sz_ready.at(b, u))
                if u == 0:
                    pe.wait_ge(sum_copied.sem, sum_copied.at(b, 0))
                elif u >= 2 and half == 0:
                    pe.wait_ge(tg_ready.sem, tg_ready.at(b - 1, u - 1))
                elif u >= 2:
                    pe.wait_ge(a4_ready.sem, a4_ready.at(b - 1, u - 1))
            at = CH * c + k if d == 0 else CH * c + 2 * PAD - k
            product = nc.tensor.matmul(W[:, half, :], Wk[:, d, k, P * half:P * half + P], x2T[:, at:at + CH],
                                       start=(k == 0), stop=(k == TAPS - 1))
            if k == TAPS - 1:
                product.then_inc(xp_mm.sem, 1)

        def product_z(b, u, half):
            d, c = unit_of(u)
            if half == 0:
                pe.wait_ge(c_ready.sem, c_ready.at(b, u + 1))
            else:
                pe.wait_ge(abs_ready.sem, abs_ready.at(b, NH * (u + 1)))
                pe.wait_ge(relu_ready.sem, relu_ready.at(b, NH * (u + 1)))
                pe.wait_ge(fb_ready.sem, fb_ready.at(b, u - 1))
            at = CH * c + PAD
            nc.tensor.matmul(W[:, half, :], Wz[:, d, P * half:P * half + P], x2T[:, at:at + CH],
                             start=True, stop=True).then_inc(z_mm.sem, 1)

        def product_dt(b, u, half):
            d, _ = unit_of(u)
            pe.wait_ge(xp_ready.sem, xp_ready.at(b, NH * u + half + 1))
            product = nc.tensor.matmul(W[0:RANK, 0, :], Wdtx[:, d, half, :], xp2[:, u % 2, half, :],
                                       start=(half == 0), stop=(half == NH - 1))
            if half == NH - 1:
                product.then_inc(dt_mm.sem, 1)

        def product_b(b, u, half):
            d, _ = unit_of(u)
            if half == 0:
                pe.wait_ge(abs_ready.sem, abs_ready.at(b, NH * u + 1))
                pe.wait_ge(relu_ready.sem, relu_ready.at(b, NH * u + 1))
            product = nc.tensor.matmul(W[:, 0, :], Wbc[:, d, half, 0, :], xp2[:, u % 2, half, :],
                                       start=(half == 0), stop=(half == NH - 1))
            if half == NH - 1:
                product.then_inc(b_mm.sem, 1)

        def product_c(b, u, half):
            d, _ = unit_of(u)
            if half == 0:
                pe.wait_ge(b_ready.sem, b_ready.at(b, u + 1))
            product = nc.tensor.matmul(W[:, 0, :], Wbc[:, d, half, 1, :], xp2[:, u % 2, half, :],
                                       start=(half == 0), stop=(half == NH - 1))
            if half == NH - 1:
                product.then_inc(c_mm.sem, 1)

        def product_delta(b, u, half):
            d, _ = unit_of(u)
            pe.wait_ge(dt_ready.sem, dt_ready.at(b, u + 1))
            nc.tensor.matmul(W[:, half, :], Wdt[:, d, P * half:P * half + P], dtT[:, :],
                             start=True, stop=True).then_inc(dp_mm.sem, 1)

        def replicate_delta(b, s):
            u, g = divmod(s, GROUPS)
            _, _, k, q, _, _ = group_of(g)
            to, before = decay_buffer(s)
            if g % GPH == 0:
                loads = dstack_loaded[g // GPH]
                pe.wait_ge(loads.sem, loads.at(b, STACK_DMAS * (u + 1)))
            pe.wait_ge(h_ready.sem, h_ready.at(b, before + 1))
            nc.tensor.matmul(D[:, to, :], sel[:, k, :], stackD[:, q, :], start=True, stop=True) \
                .then_inc(drep_ready.sem, 1)

        def replicate_u(b, s):
            u, g = divmod(s, GROUPS)
            _, _, k, q, _, _ = group_of(g)
            if g % GPH == 0:
                loads = ustack_loaded[g // GPH]
                pe.wait_ge(loads.sem, loads.at(b, STACK_DMAS * (u + 1)))
            pe.wait_ge(dbx_ready.sem, dbx_ready.at(b, s - 1))
            nc.tensor.matmul(U[:, s % 2, :], sel[:, k, :], stackU[:, q, :], start=True, stop=True) \
                .then_inc(urep_ready.sem, 1)

        def reduce(b, m):
            for s in range(4 * m, 4 * m + 4):
                g = s % GROUPS
                _, _, _, _, tile, r = group_of(g)
                if s == 4 * m and m % 4 == 0:
                    pe.wait_ge(yg_ready.sem, yg_ready.at(b, m // 4))
                if s % 2 == 0:
                    pe.wait_ge(hc_ready.sem, hc_ready.at(b, s // 2 + 1))
                last = nc.tensor.matmul(Y[32 * tile:32 * tile + 32, :], red[:, r, :], hs[:, s % HRING, :],
                                        start=(r == 0), stop=(r == 3))
            last.then_inc(reduced.sem, 1)

        def product_out(b, u, part):
            d, c = unit_of(u)
            if part < NH:
                if part == 0:
                    pe.wait_ge(yg_ready.sem, yg_ready.at(b, NH * (u + 1)))
                nc.tensor.matmul(W[:, 1, :], Wo[:, d, part, :], yg[:, part, :], start=(part == 0), stop=False,
                                 skip_group_check=True)
                return
            pe.wait_ge(x1_ready.sem, x1_ready.at(b, TILES))
            for i in range(CH // P):
                last = nc.tensor.matmul(W[:, 1, P * i:P * i + P], xt[:, CH // P * c + i, :], ident[:, :],
                                        start=False, stop=(i == CH // P - 1), skip_group_check=True)
            last.then_inc(out_mm.sem, 1)

        def products_gated(b, c, k):
            if k == 0:
                pe.wait_ge(fb_ready.sem, fb_ready.at(b, UNITS))
            cut = slice(CH * c, CH * c + CH)
            weights, signal = ((Wgs, gate_mm), (Wvs, value_mm))[k]
            for d in range(2):
                last = nc.tensor.matmul(W[:, k, :], weights[:, d, :], fbT[:, d, cut], start=(d == 0), stop=(d == 1))
            last.then_inc(signal.sem, 1)

        def turn_sum(b):
            pe.wait_ge(a4_ready.sem, a4_ready.at(b, NCH))
            turn(a4[:, :].rearrange("p (t d) -> p t d", d=DM), a4_turned)

        def row(b, next_row, last_end):
            for s in range(SLOTS):
                u, g = divmod(s, GROUPS)
                for n in inputs_made(s):
                    if n + 1 < SLOTS:
                        replicate_u(b, n + 1)
                    elif next_row:
                        replicate_u(b + 1, n + 1 - SLOTS)
                if s + 2 < SLOTS:
                    replicate_delta(b, s + 2)
                elif next_row:
                    replicate_delta(b + 1, s + 2 - SLOTS)
                if (s - LAG) % 4 == 3:
                    if s - LAG >= 3:
                        reduce(b, (s - LAG) // 4)
                    elif last_end:
                        reduce(b - 1, SLOTS // 4 + (s - LAG) // 4)
                nb, nu = (b, u + 1) if u < UNITS - 1 else (b + 1, 0)
                prepares = u < UNITS - 1 or next_row
                if prepares:
                    for k in {0: (0,), 1: (1, 2), 2: (3,), 4: (4, 5), 5: (6,), 6: (7,)}.get(g, ()):
                        product_x(nb, nu, k // TAPS, k % TAPS)
                    if g in (8, 10):
                        product_dt(nb, nu, (g - 8) // 2)
                    if g in (12, 13):
                        product_delta(nb, nu, g - 12)
                    if g in (14, 16):
                        product_b(nb, nu, (g - 14) // 2)
                if g in (16, 17, 18) and (u > 0 or last_end):
                    if g == 16 and prepares:
                        pe.wait_ge(abs_ready.sem, abs_ready.at(nb, NH * (nu + 1)))
                        pe.wait_ge(relu_ready.sem, relu_ready.at(nb, NH * (nu + 1)))
                    elif g == 16:
                        pe.wait_ge(sz_ready.sem, sz_ready.at(b + 1, 0))
                    product_out(*((b, u - 1) if u > 0 else (b - 1, UNITS - 1)), g - 16)
                if prepares:
                    if g in (20, 21):
                        product_c(nb, nu, g - 20)
                    if g == 22:
                        product_z(nb, nu, 1)
                    if g == 25:
                        product_z(nb, nu, 0)
                if u < NCH and last_end and g in (29, 30):
                    if g == 29:
                        pe.wait_ge(sz_ready.sem, sz_ready.at(nb, nu + 1))
                    products_gated(b - 1, u, g - 29)
                if u == 2 and next_row and g == 29:
                    turn_x2(b + 1)
                if u == 2 and last_end and g == 31:
                    if next_row:
                        pe.wait_ge(x2T_ready.sem, x2T_ready.at(b + 1, 1))
                    else:
                        pe.wait_ge(sz_ready.sem, sz_ready.at(nb, nu + 1))
                    turn_sum(b - 1)

        turn_x2(0)
        pe.wait_ge(made["prep_dve"].sem, PREP_DVE)
        pe.wait_ge(made["half_made"].sem, 12)
        for half in range(NH):
            for k in range(TAPS):
                product_x(0, 0, half, k)
        for half in range(NH):
            product_dt(0, 0, half)
        for half in range(NH):
            product_delta(0, 0, half)
        for half in range(NH):
            product_b(0, 0, half)
        for half in range(NH):
            product_c(0, 0, half)
        for half in (1, 0):
            product_z(0, 0, half)
        for s in range(2):
            replicate_u(0, s)
            replicate_delta(0, s)
        row(0, True, False)
        with nc.tensor.Fori(1, ROWS - 1) as b:
            row(b, True, True)
        row(ROWS - 1, False, True)
        reduce(ROWS - 1, SLOTS // 4 - 1)
        pe.wait_ge(sum_copied.sem, sum_copied.at(ROWS, 0))
        for part in range(NH + 1):
            product_out(ROWS - 1, UNITS - 1, part)
        for c in range(NCH):
            if c:
                pe.wait_ge(tg_ready.sem, tg_ready.at(ROWS - 1, c))
                pe.wait_ge(a4_ready.sem, a4_ready.at(ROWS - 1, c))
            for k in range(2):
                products_gated(ROWS - 1, c, k)
        turn_sum(ROWS - 1)


def experts(nc, ctx, ident, cols, mhalf, router_w, w1, w2, b2, gamma, beta, x3_dram, out):
    def sb(name, shape, dt=F32):
        return ctx.enter_context(nc.sbuf_tensor(name, shape, dt))

    def sig(name, per):
        return Signal(ctx, nc, name, per)

    HB = 4
    LEAD = 3
    W1 = sb("W1", [P, NE, FF])
    W2 = sb("W2", [P, NE, FT, DM])
    W1hi = sb("W1hi", [P, NE, FF], F32R)
    W1lo = sb("W1lo", [P, NE, FF], F32R)
    w2mean = sb("w2mean", [P, NE, FT])
    gam = sb("gam", [P, NE, DM])
    router = sb("router", [P, NE])
    betad = sb("betad", [TT * NE, TT, DM])
    b2all = sb("b2all", [P, NE, DM])
    b2mean = sb("b2mean", [P, NE])
    iota_i = sb("iota_i", [P, TT, NE], mybir.dt.int32)
    iota = sb("iota", [P, TT, NE])
    x3 = sb("x3c", [P, 2, TT, DM])
    xln = sb("xln", [P, 2, TT, DM])
    xlnT = sb("xlnT", [P, TC])
    xhi = sb("xhi", [P, 2, TC], F32R)
    xlo = sb("xlo", [P, 2, TC], F32R)
    st = sb("st", [P, TT, 6])
    mv = sb("mv", [P, TT, 2])
    rs = sb("rs", [P, 2, TT])
    logits = sb("logits", [P, TT, NE])
    top = sb("top", [P, TT, 8])
    topi = sb("topi", [P, TT, 8], U32)
    topf = sb("topf", [P, TT, 2])
    gap = sb("gap", [P, TT])
    gw = sb("gw", [P, 2, TT])
    pick = sb("pick", [P, 2, TT, NE])
    gates = sb("gates", [P, 2, TT, NE])
    gT = sb("gT", [TT * NE, P])
    acc = sb("acc", [P, 2, TT, DM])
    hT = sb("hT", [P, HB, TC])
    sq = sb("sq", [P, 2, TT, DM])
    ssq = sb("ssq", [P, 2, TT])
    es = sb("es", [P, 2, 3, TT])
    wexp = sb("wexp", [P, 2, TT, DM])
    st2 = sb("st2", [P, TT, 6])
    mv2 = sb("mv2", [P, TT, 2])
    rs2 = sb("rs2", [P, 2, TT])

    Hb = ctx.enter_context(nc.psum_tensor("Hb", [P, 4, TC], F32))
    Ob = ctx.enter_context(nc.psum_tensor("Ob", [P, 2, TT, DM], F32))
    Ta = ctx.enter_context(nc.psum_tensor("Ta", [P, TC], F32))
    Tb = ctx.enter_context(nc.psum_tensor("Tb", [P, TC], F32))

    SMALL = (2 + TT) * 16
    JT = NE * FT
    sp_ticks, pool_ticks, dve_ticks = (sig(n, 0) for n in ("sp_ticks2", "pool_ticks2", "dve_ticks2"))
    small_loaded = sig("small_loaded", 0)
    w1_loaded = [sig(f"w1_{e}_loaded", 0) for e in range(NE)]
    w2_loaded = [sig(f"w2_{e}_loaded", 0) for e in range(NE)]
    b2_loaded = sig("b2_loaded", 0)
    w2_summed = sig("w2_summed", 0)
    w2_centred = sig("w2_centred", 0)
    b2_step = sig("b2_step", 0)
    beta_zero = sig("beta_zero", 0)
    const2 = sig("const2", 0)
    x3c_loaded = [sig(f"x3c_loaded{p}", 8) for p in range(2)]
    stats_done = sig("stats_done", 2 * TT)
    rstd_done = sig("rstd_done", 2)
    xln_ready = sig("xln_ready", TT)
    xln_turned = sig("xln_turned", 1)
    xlnT_ready = sig("xlnT_ready", 1)
    xhi_ready = sig("xhi_ready", 1)
    xlo_ready = sig("xlo_ready", 1)
    w1hi_ready = sig("w1hi_ready", 0)
    w1lo_ready = sig("w1lo_ready", 0)
    logits_mm = sig("logits_mm", 1)
    logits_ready = sig("logits_ready", 1)
    top_ready = sig("top_ready", TT)
    topi_ready = sig("topi_ready", TT)
    topf_ready = sig("topf_ready", 1)
    gap_ready = sig("gap_ready", 1)
    gtanh_ready = sig("gtanh_ready", 1)
    gw_ready = sig("gw_ready", 2)
    pick_step = sig("pick_step", 4)
    gates_ready = sig("gates_ready", 1)
    gates_turned = sig("gates_turned", 1)
    gT_ready = sig("gT_ready", 1)
    beta_mm = sig("beta_mm", 1)
    acc_ready = sig("acc_ready", 1)
    h_mm = sig("h_mm", JT)
    gelu_ready = sig("gelu_ready", JT)
    o_mm = sig("o_mm", JT)
    bias_ready = sig("bias_ready", NE)
    res_ready = sig("res_ready", NE)
    ssq_ready = sig("ssq_ready", NE * TT)
    evar_ready = sig("evar_ready", NE)
    erstd_ready = sig("erstd_ready", NE)
    escale_ready = sig("escale_ready", NE)
    wexp_ready = sig("wexp_ready", NE * TT)
    acc_added = sig("acc_added", NE)
    stats2_done = sig("stats2_done", 2 * TT)
    rstd2_done = sig("rstd2_done", 2)
    y_ready = sig("y_ready", TT)
    final_ready = sig("final_ready", 1)
    stored = [sig(f"stored{p}", 8) for p in range(2)]

    x3_v = x3_dram.rearrange("(c t p) d -> c p t d", t=TT, p=P)
    out_v = out.rearrange("r s d -> (r s) d").rearrange("(c t p) d -> c p t d", t=TT, p=P)

    def at(view, c):
        return view[c] if isinstance(c, int) else view[bass.ds(c, 1), :, :, :].rearrange("o p t d -> (o p) t d")

    def chunks(eng, prepare, body):
        prepare(0, 0)
        body(0, 0, True, False)
        body(1, 1, True, True)
        with eng.Fori(1, NTC // 2 - 1) as pair:
            body(pair * 2, 0, True, True)
            body(pair * 2 + 1, 1, True, True)
        body(NTC - 2, 0, True, True)
        body(NTC - 1, 1, False, True)

    block = ctx.enter_context(nc.Block())

    @block.sync
    def _(sp):
        sp.dma_start(x3[:, 0], x3_v[0]).then_inc(x3c_loaded[0].sem, 16)
        sp.dma_start(router[:, :], router_w).then_inc(small_loaded.sem, 16)
        sp.dma_start(b2all[:, :, :].rearrange("p e d -> p (e d)"),
                     b2.rearrange("(o e) d -> o (e d)", o=1).to_broadcast([P, NE * DM])).then_inc(b2_loaded.sem, 16)
        sp.dma_start(W1[:, 0, :], w1[0]).then_inc(w1_loaded[0].sem, 16)
        sp.dma_start(W2[:, 0], w2[0].rearrange("(f p) d -> p f d", p=P)).then_inc(w2_loaded[0].sem, 16)
        sp.dma_start(gam[:, :, :].rearrange("p e d -> p (e d)"),
                     gamma.rearrange("(o e) d -> o (e d)", o=1).to_broadcast([P, NE * DM])) \
            .then_inc(small_loaded.sem, 16)
        sp.wait_ge(beta_zero.sem, 1)
        for t in range(TT):
            sp.dma_start(betad[NE * t:NE * t + NE, t, :], beta).then_inc(small_loaded.sem, 16)
        for e in range(1, NE):
            sp.dma_start(W1[:, e, :], w1[e]).then_inc(w1_loaded[e].sem, 16)
            sp.dma_start(W2[:, e], w2[e].rearrange("(f p) d -> p f d", p=P)).then_inc(w2_loaded[e].sem, 16)

        def load_x3(c, p):
            sp.wait_ge(final_ready.sem, final_ready.at(c, -1))
            sp.sem_inc(sp_ticks.sem, 1)
            sp.dma_start(x3[:, p], at(x3_v, c)).then_inc(x3c_loaded[p].sem, 16)

        def store(c, p):
            sp.wait_ge(final_ready.sem, final_ready.at(c, 1))
            sp.sem_inc(sp_ticks.sem, 1)
            sp.dma_start(at(out_v, c), acc[:, p]).then_inc(stored[p].sem, 16)

        def body(c, p, has_next, has_last):
            if has_next:
                load_x3(c + 1, 1 - p)
            if has_last:
                store(c - 1, 1 - p)

        chunks(nc.sync, lambda c, p: None, body)
        store(NTC - 1, 1)
        for p in range(2):
            sp.wait_ge(stored[p].sem, stored[p].at(NTC, 0))

    @block.gpsimd
    def _(pool):
        nc.gpsimd.memset(betad[:, :, :], 0.0).then_inc(beta_zero.sem, 1)
        nc.gpsimd.iota(iota_i[:, :, :], pattern=[[0, TT], [1, NE]], base=0, channel_multiplier=0) \
            .then_inc(const2.sem, 1)

        def rstd(var, ve, r, scale, eps, done, c):
            nc.gpsimd.tensor_scalar(ve, var, scale, eps, ALU.mult, ALU.add).then_inc(done.sem, 1)
            pool.wait_ge(done.sem, done.at(c, 1))
            nc.gpsimd.tensor_tensor(r, ve, mhalf[:, 0:TT], ALU.pow).then_inc(done.sem, 1)

        def prepare(c, p):
            pool.wait_ge(stats_done.sem, stats_done.at(c, 2 * TT))
            pool.sem_inc(pool_ticks.sem, 1)
            rstd(mv[:, :, 1], rs[:, 0, :], rs[:, 1, :], 1.0, EPS_IN, rstd_done, c)

        def rstd_expert(c, e):
            q = e % 2
            pool.wait_ge(ssq_ready.sem, ssq_ready.at(c, TT * (e + 1)))
            pool.sem_inc(pool_ticks.sem, 1)
            nc.gpsimd.tensor_scalar(es[:, q, 0, :], ssq[:, q, :], 1.0 / DM, EPS_OUT, ALU.mult, ALU.add) \
                .then_inc(evar_ready.sem, 1)
            pool.wait_ge(evar_ready.sem, evar_ready.at(c, e + 1))
            pool.wait_ge(escale_ready.sem, escale_ready.at(c, e - 1))
            nc.gpsimd.tensor_tensor(es[:, q, 1, :], es[:, q, 0, :], mhalf[:, 0:TT], ALU.pow) \
                .then_inc(erstd_ready.sem, 1)

        def accumulate(c, e, p):
            pool.wait_ge(wexp_ready.sem, wexp_ready.at(c, TT * (e + 1)))
            if e == 0:
                pool.wait_ge(acc_ready.sem, acc_ready.at(c, 1))
            pool.wait_ge(acc_added.sem, acc_added.at(c, e))
            nc.gpsimd.tensor_tensor(acc[:, p], acc[:, p], wexp[:, e % 2], ALU.add).then_inc(acc_added.sem, 1)

        def body(c, p, has_next, has_last):
            for t in range(0, JT, 2):
                if t % FT == 0 and t >= 8:
                    rstd_expert(c, (t - 8) // FT)
                elif t in (0, 4) and has_last:
                    rstd_expert(c - 1, NE - 2 + t // FT)
                if t % FT == 2 and t >= 10:
                    accumulate(c, (t - 10) // FT, p)
                elif t in (2, 6) and has_last:
                    accumulate(c - 1, NE - 2 + t // FT, 1 - p)
                if t == 10 and has_last:
                    pool.wait_ge(stats2_done.sem, stats2_done.at(c - 1, 2 * TT))
                    pool.sem_inc(pool_ticks.sem, 1)
                    rstd(mv2[:, :, 1], rs2[:, 0, :], rs2[:, 1, :], 1.0, EPS_IN, rstd2_done, c - 1)
                if t == 18 and has_next:
                    prepare(c + 1, 1 - p)

        chunks(nc.gpsimd, prepare, body)
        for e in (NE - 2, NE - 1):
            rstd_expert(NTC - 1, e)
            accumulate(NTC - 1, e, 1)
        pool.wait_ge(stats2_done.sem, stats2_done.at(NTC - 1, 2 * TT))
        rstd(mv2[:, :, 1], rs2[:, 0, :], rs2[:, 1, :], 1.0, EPS_IN, rstd2_done, NTC - 1)

    @block.scalar
    def _(act):
        def take_xlnT(c, p):
            act.wait_ge(xln_turned.sem, xln_turned.at(c, 1))
            act.wait_ge(logits_mm.sem, logits_mm.at(c, 0))
            act.wait_ge(xlo_ready.sem, xlo_ready.at(c, 0))
            nc.scalar.activation(xlnT[:, :], Ta[:, :], ACT.Copy).then_inc(xlnT_ready.sem, 1)
            act.wait_ge(h_mm.sem, h_mm.at(c, -JT))
            nc.scalar.activation(xhi[:, p, :], Ta[:, :], ACT.Copy).then_inc(xhi_ready.sem, 1)

        def gate_tanh(c, p):
            act.wait_ge(gap_ready.sem, gap_ready.at(c, 1))
            nc.scalar.activation(gap[:, :], gap[:, :], ACT.Tanh, scale=0.5).then_inc(gtanh_ready.sem, 1)

        def take_gT(c, p):
            act.wait_ge(gates_turned.sem, gates_turned.at(c, 1))
            act.wait_ge(beta_mm.sem, beta_mm.at(c, 0))
            nc.scalar.activation(gT[:, :], Tb[0:TT * NE, 128:256], ACT.Copy).then_inc(gT_ready.sem, 1)

        def take_beta(c, p):
            act.wait_ge(beta_mm.sem, beta_mm.at(c, 1))
            act.wait_ge(stored[p].sem, stored[p].at(c, -8 * p))
            nc.scalar.activation(acc[:, p].rearrange("p t d -> p (t d)"), Ta[:, :], ACT.Copy) \
                .then_inc(acc_ready.sem, 1)

        def prepare(c, p):
            take_xlnT(c, p)
            gate_tanh(c, p)

        def gelu(c, t):
            act.wait_ge(h_mm.sem, h_mm.at(c, t + 1))
            act.wait_ge(o_mm.sem, o_mm.at(c, t + 1 - HB))
            e, f = divmod(t, FT)
            bias = cols[:, C_B1 + FT * e + f:C_B1 + FT * e + f + 1]
            nc.scalar.activation(hT[:, t % HB, :], Hb[:, t % HB, :], ACT.Gelu, bias=bias) \
                .then_inc(gelu_ready.sem, 1)

        def squares(c, e):
            q = e % 2
            act.wait_ge(res_ready.sem, res_ready.at(c, e + 1))
            act.wait_ge(evar_ready.sem, evar_ready.at(c, e - 1))
            act.wait_ge(ssq_ready.sem, ssq_ready.at(c, TT * (e - 1)))
            for i in range(TT):
                nc.scalar.activation(sq[:, q, i, :], Ob[:, q, i, :], ACT.Square, accum_out=ssq[:, q, i:i + 1]) \
                    .then_inc(ssq_ready.sem, 1)

        def body(c, p, has_next, has_last):
            for t in range(JT):
                gelu(c, t)
                if t % FT == 3 and t >= 7:
                    squares(c, (t - 7) // FT)
                elif t == 3 and has_last:
                    squares(c - 1, NE - 1)
                if t == 0:
                    take_gT(c, p)
                if t == 6:
                    take_beta(c, p)
                if t == 24 and has_next:
                    take_xlnT(c + 1, 1 - p)
                if t == 29 and has_next:
                    gate_tanh(c + 1, 1 - p)

        chunks(nc.scalar, prepare, body)
        squares(NTC - 1, NE - 1)

    @block.vector
    def _(dve):
        dve.wait_ge(const2.sem, 1)
        nc.vector.tensor_copy(iota[:, :, :], iota_i[:, :, :]).then_inc(b2_step.sem, 1)

        def centre(e):
            dve.wait_ge(w2_loaded[e].sem, 16)
            m = w2mean[:, e, :]
            nc.vector.reduce_sum(m, W2[:, e], axis=mybir.AxisListType.X).then_inc(w2_summed.sem, 1)
            dve.wait_ge(w2_summed.sem, 2 * e + 1)
            nc.vector.tensor_scalar(m, m, 1.0 / DM, None, ALU.mult).then_inc(w2_summed.sem, 1)
            dve.wait_ge(w2_summed.sem, 2 * e + 2)
            nc.vector.tensor_tensor(W2[:, e], W2[:, e],
                                    m.rearrange("p (f o) -> p f o", o=1).to_broadcast([P, FT, DM]),
                                    ALU.subtract).then_inc(w2_centred.sem, 1)

        def weights(e):
            centre(e)
            dve.wait_ge(w1_loaded[e].sem, 16)
            nc.vector.tensor_copy(W1hi[:, e, :], W1[:, e, :]).then_inc(w1hi_ready.sem, 1)
            dve.wait_ge(w1hi_ready.sem, e + 1)
            nc.vector.tensor_tensor(W1lo[:, e, :], W1[:, e, :], W1hi[:, e, :].bitcast(F32), ALU.subtract) \
                .then_inc(w1lo_ready.sem, 1)

        def centre_b2():
            dve.wait_ge(b2_loaded.sem, 16)
            nc.vector.reduce_sum(b2mean[:, :], b2all[:, :, :], axis=mybir.AxisListType.X).then_inc(b2_step.sem, 1)
            dve.wait_ge(b2_step.sem, 2)
            nc.vector.tensor_scalar(b2mean[:, :], b2mean[:, :], 1.0 / DM, None, ALU.mult).then_inc(b2_step.sem, 1)
            dve.wait_ge(b2_step.sem, 3)
            nc.vector.tensor_tensor(b2all[:, :, :], b2all[:, :, :],
                                    b2mean[:, :].rearrange("p (e o) -> p e o", o=1).to_broadcast([P, NE, DM]),
                                    ALU.subtract).then_inc(b2_step.sem, 1)
            dve.wait_ge(b2_step.sem, 4)

        def norm(c, p):
            dve.wait_ge(x3c_loaded[p].sem, x3c_loaded[p].at(c, 16 - 8 * p))
            dve.wait_ge(rstd_done.sem, rstd_done.at(c, 0))
            dve.wait_ge(xln_ready.sem, xln_ready.at(c, 0))
            for t in range(TT):
                nc.vector.bn_stats(st[:, t, :], x3[:, p, t, :]).then_inc(stats_done.sem, 1)
            dve.wait_ge(stats_done.sem, stats_done.at(c, TT))
            dve.sem_inc(dve_ticks.sem, 1)
            for t in range(TT):
                nc.vector.bn_aggr(mv[:, t, :], st[:, t, :]).then_inc(stats_done.sem, 1)

        def make_xln(c, p):
            dve.wait_ge(rstd_done.sem, rstd_done.at(c, 2))
            dve.wait_ge(stats_done.sem, stats_done.at(c, 2 * TT))
            dve.wait_ge(res_ready.sem, res_ready.at(c, -NE))
            for t in range(TT):
                nc.vector.tensor_scalar(xln[:, p, t, :], x3[:, p, t, :], mv[:, t, 0:1], rs[:, 1, t:t + 1],
                                        ALU.subtract, ALU.mult).then_inc(xln_ready.sem, 1)

        def low_x(c, p):
            dve.wait_ge(xhi_ready.sem, xhi_ready.at(c, 1))
            dve.wait_ge(h_mm.sem, h_mm.at(c, -JT))
            nc.vector.tensor_tensor(xlo[:, p, :], Ta[:, :], xhi[:, p, :].bitcast(F32), ALU.subtract) \
                .then_inc(xlo_ready.sem, 1)

        def top2(c, p):
            dve.wait_ge(logits_mm.sem, logits_mm.at(c, 1))
            dve.wait_ge(topi_ready.sem, topi_ready.at(c, 0))
            nc.vector.tensor_copy(logits[:, :, :].rearrange("p t e -> p (t e)"), Tb[:, 0:TT * NE]) \
                .then_inc(logits_ready.sem, 1)
            dve.wait_ge(logits_ready.sem, logits_ready.at(c, 1))
            dve.sem_inc(dve_ticks.sem, 1)
            for t in range(TT):
                nc.vector.max(top[:, t, :], logits[:, t, :]).then_inc(top_ready.sem, 1)
            dve.wait_ge(top_ready.sem, top_ready.at(c, TT))
            dve.sem_inc(dve_ticks.sem, 1)
            for t in range(TT):
                nc.vector.max_index(topi[:, t, :], top[:, t, :], logits[:, t, :]).then_inc(topi_ready.sem, 1)
            dve.wait_ge(gw_ready.sem, gw_ready.at(c, 0))
            nc.vector.tensor_tensor(gap[:, :], top[:, :, 0], top[:, :, 1], ALU.subtract).then_inc(gap_ready.sem, 1)
            dve.wait_ge(topi_ready.sem, topi_ready.at(c, TT))
            dve.wait_ge(gates_ready.sem, gates_ready.at(c, 0))
            nc.vector.tensor_copy(topf[:, :, :], topi[:, :, 0:2]).then_inc(topf_ready.sem, 1)
            dve.wait_ge(topf_ready.sem, topf_ready.at(c, 1))
            for k in range(2):
                nc.vector.tensor_tensor(pick[:, k], iota[:, :, :],
                                        topf[:, :, k:k + 1].to_broadcast([P, TT, NE]), ALU.is_equal) \
                    .then_inc(pick_step.sem, 1)

        def make_gates(c, p):
            dve.wait_ge(gtanh_ready.sem, gtanh_ready.at(c, 1))
            nc.vector.tensor_scalar(gw[:, 0, :], gap[:, :], 0.5, 0.5, ALU.mult, ALU.add).then_inc(gw_ready.sem, 1)
            nc.vector.tensor_scalar(gw[:, 1, :], gap[:, :], -0.5, 0.5, ALU.mult, ALU.add).then_inc(gw_ready.sem, 1)
            dve.wait_ge(gw_ready.sem, gw_ready.at(c, 2))
            dve.wait_ge(pick_step.sem, pick_step.at(c, 2))
            for k in range(2):
                nc.vector.tensor_tensor(pick[:, k], pick[:, k],
                                        gw[:, k, :].rearrange("p (t o) -> p t o", o=1).to_broadcast([P, TT, NE]),
                                        ALU.mult).then_inc(pick_step.sem, 1)
            dve.wait_ge(pick_step.sem, pick_step.at(c, 4))
            dve.wait_ge(escale_ready.sem, escale_ready.at(c, -NE))
            dve.wait_ge(gates_turned.sem, gates_turned.at(c, -1))
            nc.vector.tensor_tensor(gates[:, p], pick[:, 0], pick[:, 1], ALU.add).then_inc(gates_ready.sem, 1)

        def add_residual(c, e, p):
            q = e % 2
            dve.wait_ge(o_mm.sem, o_mm.at(c, FT * (e + 1)))
            nc.vector.tensor_tensor(Ob[:, q], Ob[:, q], b2all[:, e:e + 1, :].to_broadcast([P, TT, DM]), ALU.add) \
                .then_inc(bias_ready.sem, 1)
            dve.wait_ge(bias_ready.sem, bias_ready.at(c, e + 1))
            nc.vector.tensor_tensor(Ob[:, q], Ob[:, q], xln[:, p], ALU.add).then_inc(res_ready.sem, 1)

        def scale(c, e, p):
            q = e % 2
            dve.wait_ge(erstd_ready.sem, erstd_ready.at(c, e + 1))
            if e == 0:
                dve.wait_ge(gates_ready.sem, gates_ready.at(c, 1))
            nc.vector.tensor_tensor(es[:, q, 2, :], es[:, q, 1, :], gates[:, p, :, e], ALU.mult) \
                .then_inc(escale_ready.sem, 1)
            dve.wait_ge(escale_ready.sem, escale_ready.at(c, e + 1))
            dve.wait_ge(acc_added.sem, acc_added.at(c, e - 1))
            for t in range(TT):
                nc.vector.scalar_tensor_tensor(wexp[:, q, t, :], Ob[:, q, t, :], es[:, q, 2, t:t + 1],
                                               gam[:, e, :], ALU.mult, ALU.mult).then_inc(wexp_ready.sem, 1)

        def stats_last(c, p):
            dve.wait_ge(acc_added.sem, acc_added.at(c, NE))
            dve.wait_ge(rstd2_done.sem, rstd2_done.at(c, 0))
            dve.wait_ge(y_ready.sem, y_ready.at(c, 0))
            for t in range(TT):
                nc.vector.bn_stats(st2[:, t, :], acc[:, p, t, :]).then_inc(stats2_done.sem, 1)
            dve.wait_ge(stats2_done.sem, stats2_done.at(c, TT))
            dve.sem_inc(dve_ticks.sem, 1)
            for t in range(TT):
                nc.vector.bn_aggr(mv2[:, t, :], st2[:, t, :]).then_inc(stats2_done.sem, 1)

        def finish(c, p):
            dve.wait_ge(rstd2_done.sem, rstd2_done.at(c, 2))
            dve.wait_ge(stats2_done.sem, stats2_done.at(c, 2 * TT))
            for t in range(TT):
                nc.vector.tensor_scalar(acc[:, p, t, :], acc[:, p, t, :], mv2[:, t, 0:1], rs2[:, 1, t:t + 1],
                                        ALU.subtract, ALU.mult).then_inc(y_ready.sem, 1)
            dve.wait_ge(y_ready.sem, y_ready.at(c, TT))
            nc.vector.tensor_tensor(acc[:, p], acc[:, p], x3[:, p], ALU.add).then_inc(final_ready.sem, 1)

        def prepare(c, p):
            norm(c, p)
            make_xln(c, p)
            weights(0)
            low_x(c, p)
            top2(c, p)
            make_gates(c, p)
            centre_b2()

        def body(c, p, has_next, has_last):
            for t in range(JT):
                if isinstance(c, int) and c == 0:
                    if t == 0:
                        weights(1)
                    if t % FT == 0 and t // FT + 2 < NE:
                        weights(t // FT + 2)
                if t % FT == 2 and t >= 6:
                    add_residual(c, (t - 6) // FT, p)
                elif t == 2 and has_last:
                    add_residual(c - 1, NE - 1, 1 - p)
                if t % FT == 1 and t >= 9:
                    scale(c, (t - 9) // FT, p)
                elif t in (1, 5) and has_last:
                    scale(c - 1, NE - 2 + t // FT, 1 - p)
                if has_last:
                    if t == 8:
                        stats_last(c - 1, 1 - p)
                    if t == 12:
                        finish(c - 1, 1 - p)
                if has_next:
                    if t == 16:
                        norm(c + 1, 1 - p)
                    if t == 20:
                        make_xln(c + 1, 1 - p)
                    if t == 24:
                        low_x(c + 1, 1 - p)
                    if t == 26:
                        top2(c + 1, 1 - p)
                    if t == 30:
                        make_gates(c + 1, 1 - p)

        chunks(nc.vector, prepare, body)
        scale(NTC - 1, NE - 2, 1)
        add_residual(NTC - 1, NE - 1, 1)
        scale(NTC - 1, NE - 1, 1)
        stats_last(NTC - 1, 1)
        finish(NTC - 1, 1)

    @block.tensor
    def _(pe):
        def turn_xln(c, p):
            pe.wait_ge(xln_ready.sem, xln_ready.at(c, TT))
            pe.wait_ge(acc_ready.sem, acc_ready.at(c, 0))
            for t in range(TT):
                last = nc.tensor.transpose(Ta[:, P * t:P * t + P], xln[:, p, t, :], ident[:, :])
            last.then_inc(xln_turned.sem, 1)

        def route(c, p):
            pe.wait_ge(xlnT_ready.sem, xlnT_ready.at(c, 1))
            pe.wait_ge(gT_ready.sem, gT_ready.at(c, 0))
            for t in range(TT):
                last = nc.tensor.matmul(Tb[:, NE * t:NE * t + NE], xlnT[:, P * t:P * t + P], router[:, :],
                                        start=True, stop=True)
            last.then_inc(logits_mm.sem, 1)

        def turn_gates(c, p):
            pe.wait_ge(gates_ready.sem, gates_ready.at(c, 1))
            nc.tensor.transpose(Tb[0:TT * NE, 128:256], gates[:, p].rearrange("p t e -> p (t e)"), ident[:, :]) \
                .then_inc(gates_turned.sem, 1)

        def add_beta(c, p):
            pe.wait_ge(gT_ready.sem, gT_ready.at(c, 1))
            nc.tensor.matmul(Ta[:, :], gT[:, :], betad[:, :, :].rearrange("k t d -> k (t d)"),
                             start=True, stop=True).then_inc(beta_mm.sem, 1)

        def prepare(c, p):
            turn_xln(c, p)
            pe.wait_ge(small_loaded.sem, SMALL)
            route(c, p)
            for t in range(LEAD):
                hidden(c, t, p)
            turn_gates(c, p)

        def hidden(c, t, p):
            e, f = divmod(t, FT)
            if isinstance(c, int) and c == 0 and f == 0:
                pe.wait_ge(w1hi_ready.sem, e + 1)
                pe.wait_ge(w1lo_ready.sem, e + 1)
            if t == 0:
                pe.wait_ge(xlo_ready.sem, xlo_ready.at(c, 1))
                pe.wait_ge(xhi_ready.sem, xhi_ready.at(c, 1))
            pe.wait_ge(gelu_ready.sem, gelu_ready.at(c, t + 1 - HB))
            for k, (w, xx) in enumerate(((W1hi, xhi), (W1hi, xlo), (W1lo, xhi))):
                last = nc.tensor.matmul(Hb[:, t % HB, :], w[:, e, P * f:P * f + P], xx[:, p, :],
                                        start=(k == 0), stop=(k == 2))
            last.then_inc(h_mm.sem, 1)

        def outputs(c, t, p):
            e, f = divmod(t, FT)
            q = e % 2
            if f == 0:
                if isinstance(c, int) and c == 0:
                    pe.wait_ge(w2_centred.sem, e + 1)
                pe.wait_ge(wexp_ready.sem, wexp_ready.at(c, TT * (e - 1)))
            pe.wait_ge(gelu_ready.sem, gelu_ready.at(c, t + 1))
            for i in range(TT):
                last = nc.tensor.matmul(Ob[:, q, i, :], hT[:, t % HB, P * i:P * i + P], W2[:, e, f, :],
                                        start=(f == 0 and i == 0), stop=(f == FT - 1), skip_group_check=True)
            last.then_inc(o_mm.sem, 1)

        def body(c, p, has_next, has_last):
            for t in range(JT):
                if t + LEAD < JT:
                    hidden(c, t + LEAD, p)
                elif has_next:
                    hidden(c + 1, t + LEAD - JT, 1 - p)
                outputs(c, t, p)
                if t == 1:
                    add_beta(c, p)
                if has_next:
                    if t == 20:
                        turn_xln(c + 1, 1 - p)
                    if t == 23:
                        route(c + 1, 1 - p)
                    if t == 29:
                        turn_gates(c + 1, 1 - p)

        chunks(nc.tensor, prepare, body)


_INS = ['L0_attn_x', 'L0_attn_ln_w', 'L0_attn_ln_b', 'L0_attn_W_in', 'L0_attn_b_in', 'L0_attn_conv_w',
        'L0_attn_conv_b', 'L0_attn_W_xproj', 'L0_attn_W_dt', 'L0_attn_b_dt', 'L0_attn_A_log', 'L0_attn_D',
        'L0_attn_W_out', 'L0_attn_b_out', 'L0_attn_Wg', 'L0_attn_bg', 'L0_attn_Wv', 'L0_attn_bv',
        'L0_ffn_router_w', 'L0_ffn_w1', 'L0_ffn_b1', 'L0_ffn_w2', 'L0_ffn_b2', 'L0_ffn_gamma',
        'L0_ffn_beta']


def kernel(**inputs):
    import numpy as np
    import concourse.bacc as bacc
    from concourse.bass_utils import run_bass_kernel_spmd

    nc = bacc.Bacc("TRN2", target_bir_lowering=False, num_devices=1)
    arrays, args = {}, []
    for name in _INS:
        a = np.ascontiguousarray(inputs[name])
        arrays[f"in_{name}"] = a
        args.append(nc.dram_tensor(f"in_{name}", a.shape, mybir.dt.from_np(a.dtype), kind="ExternalInput").ap())
    out = nc.dram_tensor("out_0", (ROWS, STEPS, DM), F32, kind="ExternalOutput").ap()
    build(nc, *args, out)
    r = run_bass_kernel_spmd(nc, [arrays], core_ids=[0])
    return r.results[0]["out_0"]
```
